# Optimizing a Trainium2 kernel written in Bass

```python
import numpy as np
import jax
import jax.numpy as jnp

def _softmax(x, axis=-1):
    return jax.nn.softmax(x, axis=axis)

def _gelu(x):
    return jax.nn.gelu(x, approximate=True)

def _silu(x):
    return jax.nn.silu(x)

def _sigmoid(x):
    return jax.nn.sigmoid(x)

def _layernorm(x, axis=-1, eps=1e-05):
    m = jnp.mean(x, axis=axis, keepdims=True)
    v = jnp.var(x, axis=axis, keepdims=True)
    return (x - m) / jnp.sqrt(v + eps)

def _scatter_add(tgt, idx, src, axis=0):
    return tgt.at[idx].add(src)

def _segment_sum(src, seg, n):
    return jax.ops.segment_sum(src, seg, n)
kernel_name = 'mk_recurrent_d2_jaxref_r8_49e61b'

def setup_inputs(seed: int=0):
    np.random.seed(seed)
    _w = jnp.asarray

    def _L0_attn_setup():
        import jax, jax.numpy as jnp
        import numpy as np
        B, T, D, N = (8, 256, 128, 32)
        key = jax.random.key(seed)
        ks = jax.random.split(key, 6)
        sD = 1.0 / np.sqrt(D)
        sN = 1.0 / np.sqrt(N)
        return {'x': jax.random.normal(ks[0], (B, T, D), dtype=jnp.float32), 'Wa': jax.random.normal(ks[1], (D, N), dtype=jnp.float32) * sD, 'ba': jnp.zeros((N,), jnp.float32), 'Wb': jax.random.normal(ks[2], (D, N), dtype=jnp.float32) * sD, 'bb': jnp.zeros((N,), jnp.float32), 'Wc': jax.random.normal(ks[3], (D, N), dtype=jnp.float32) * sD, 'bc': jnp.zeros((N,), jnp.float32), 'Wd': jax.random.normal(ks[4], (D, D), dtype=jnp.float32) * sD, 'bd': jnp.zeros((D,), jnp.float32), 'Wy': jax.random.normal(ks[5], (N, D), dtype=jnp.float32) * sN, 'by': jnp.zeros((D,), jnp.float32)}
    _L0_attn_in = _L0_attn_setup()

    def _L0_ffn_setup():
        import jax, jax.numpy as jnp
        import numpy as np
        DIM = 128
        DEPTH = 2
        HEADS = 8
        DIM_HEAD = 64
        WINDOW = 64
        INNER = HEADS * DIM_HEAD
        HID = int(DIM * 4 * 2 / 3)
        B, N = (2, 1024)
        QK_SCALE = 8.0

        def shift_token(t):
            t1, t2 = jnp.split(t, 2, axis=-1)
            t2 = jnp.pad(t2, ((0, 0), (1, 0), (0, 0)))[:, :-1]
            return jnp.concatenate([t1, t2], axis=-1)

        def l2norm(t):
            return t / jnp.clip(jnp.linalg.norm(t, axis=-1, keepdims=True), 1e-12)

        def rotate_half(x):
            x1, x2 = jnp.split(x, 2, axis=-1)
            return jnp.concatenate([-x2, x1], axis=-1)

        def rotary_xpos(q, k):
            n = q.shape[-2]
            half_idx = jnp.arange(0, DIM_HEAD, 2, dtype=jnp.float32)
            inv_freq = 1.0 / 10000.0 ** (half_idx / DIM_HEAD)
            t = jnp.arange(n, dtype=jnp.float32)
            freqs = t[:, None] * inv_freq[None, :]
            freqs = jnp.concatenate([freqs, freqs], axis=-1)
            base = (half_idx + 0.4 * DIM_HEAD) / (1.4 * DIM_HEAD)
            power = (t - n // 2) / float(WINDOW // 2)
            scale = base[None, :] ** power[:, None]
            scale = jnp.concatenate([scale, scale], axis=-1)
            cos, sin = (jnp.cos(freqs), jnp.sin(freqs))
            q = q * cos * scale + rotate_half(q) * sin * scale
            k = k * cos / scale + rotate_half(k) * sin / scale
            return (q, k)

        def local_attention(q, k, v):
            b, h, n, d = q.shape
            w = n // WINDOW
            bq = q.reshape(b, h, w, WINDOW, d) * QK_SCALE
            bk = k.reshape(b, h, w, WINDOW, d)
            bv = v.reshape(b, h, w, WINDOW, d)

            def look_around(t):
                p = jnp.pad(t, ((0, 0), (0, 0), (1, 0), (0, 0), (0, 0)))
                return jnp.concatenate([p[:, :, :w], p[:, :, 1:]], axis=3)
            bk, bv = (look_around(bk), look_around(bv))
            bt = jnp.arange(n).reshape(w, WINDOW)
            btp = jnp.pad(bt, ((1, 0), (0, 0)), constant_values=-1)
            btk = jnp.concatenate([btp[:w], btp[1:]], axis=1)
            sim = jnp.einsum('bhwid,bhwjd->bhwij', bq, bk)
            i = bt[:, :, None]
            j = btk[:, None, :]
            mask = (i < j) | (i > j + WINDOW) | (j == -1)
            sim = jnp.where(mask, -jnp.finfo(sim.dtype).max, sim)
            attn = jax.nn.softmax(sim, axis=-1)
            out = jnp.einsum('bhwij,bhwjd->bhwid', attn, bv)
            return out.reshape(b, h, n, d)

        def _layer(x, wqkv, qs, ksc, wo, lg, lb, w1, b1, w2, b2):
            b, n, _ = x.shape
            h = shift_token(x)
            qkv = h @ wqkv
            q, k, v = jnp.split(qkv, 3, axis=-1)
            to_heads = lambda t: t.reshape(b, n, HEADS, DIM_HEAD).transpose(0, 2, 1, 3)
            q, k, v = (to_heads(q), to_heads(k), to_heads(v))
            q = l2norm(q) * qs
            k = l2norm(k) * ksc
            q, k = rotary_xpos(q, k)
            o = local_attention(q, k, v)
            o = o.transpose(0, 2, 1, 3).reshape(b, n, INNER)
            x = x + o @ wo
            h = shift_token(x)
            mu = h.mean(-1, keepdims=True)
            var = h.var(-1, keepdims=True)
            h = (h - mu) / jnp.sqrt(var + 1e-05) * lg + lb
            h = h @ w1 + b1
            a, g = jnp.split(h, 2, axis=-1)
            h = a * jax.nn.gelu(g, approximate=False)
            x = x + h @ w2 + b2
            return x
        key = jax.random.key(seed)
        ks = jax.random.split(key, 6)
        return {'x': jax.random.normal(ks[0], (B, N, DIM), jnp.float32), 'wqkv': jax.random.normal(ks[1], (DEPTH, DIM, 3 * INNER), jnp.float32) * 0.02, 'q_scale': jnp.ones((DEPTH, DIM_HEAD), jnp.float32), 'k_scale': jnp.ones((DEPTH, DIM_HEAD), jnp.float32), 'wo': jax.random.normal(ks[2], (DEPTH, INNER, DIM), jnp.float32) * 0.02, 'ln_g': jnp.ones((DEPTH, DIM), jnp.float32), 'ln_b': jnp.zeros((DEPTH, DIM), jnp.float32), 'w1': jax.random.normal(ks[3], (DEPTH, DIM, 2 * HID), jnp.float32) * 0.02, 'b1': jnp.zeros((DEPTH, 2 * HID), jnp.float32), 'w2': jax.random.normal(ks[4], (DEPTH, HID, DIM), jnp.float32) * 0.02, 'b2': jnp.zeros((DEPTH, DIM), jnp.float32)}
    _L0_ffn_in = _L0_ffn_setup()

    def _L1_attn_setup():
        import jax, jax.numpy as jnp
        import numpy as np
        B, S, D_IN, D_OUT, H = (2, 256, 128, 128, 16)
        DK = D_OUT // H
        key = jax.random.key(seed)
        ks = jax.random.split(key, 6)
        s_in = 1.0 / np.sqrt(D_IN)
        s_out = 1.0 / np.sqrt(D_OUT)
        return {'x': jax.random.normal(ks[0], (B, S, D_IN), dtype=jnp.float32), 'Wq': jax.random.uniform(ks[1], (D_OUT, D_IN), jnp.float32, -s_in, s_in), 'Wk': jax.random.uniform(ks[2], (D_OUT, D_IN), jnp.float32, -s_in, s_in), 'Wv': jax.random.uniform(ks[3], (D_OUT, D_IN), jnp.float32, -s_in, s_in), 'Wo': jax.random.uniform(ks[4], (D_OUT, D_OUT), jnp.float32, -s_out, s_out), 'bo': jax.random.uniform(ks[5], (D_OUT,), jnp.float32, -s_out, s_out)}
    _L1_attn_in = _L1_attn_setup()

    def _L1_ffn_setup():
        import jax, jax.numpy as jnp
        import numpy as np
        E, D, F = (16, 128, 256)
        B, N = (2, 256)
        LN_EPS = 1e-05
        key = jax.random.key(seed)
        ks = jax.random.split(key, 8)
        s = 0.02
        return {'x': jax.random.normal(ks[0], (B, N, D), dtype=jnp.float32), 'router_w': jax.random.normal(ks[1], (E, D), dtype=jnp.float32) * s, 'router_b': jnp.zeros((E,), dtype=jnp.float32), 'w1': jax.random.normal(ks[2], (E, F, D), dtype=jnp.float32) * s, 'w2': jax.random.normal(ks[3], (E, D, F), dtype=jnp.float32) * s, 'w3': jax.random.normal(ks[4], (E, F, D), dtype=jnp.float32) * s, 'ln_g': jnp.ones((E, D), dtype=jnp.float32), 'ln_b': jnp.zeros((E, D), dtype=jnp.float32)}
    _L1_ffn_in = _L1_ffn_setup()
    _d = {'L0_attn_x': _L0_attn_in['x'], 'L0_attn_Wa': _L0_attn_in['Wa'], 'L0_attn_ba': _L0_attn_in['ba'], 'L0_attn_Wb': _L0_attn_in['Wb'], 'L0_attn_bb': _L0_attn_in['bb'], 'L0_attn_Wc': _L0_attn_in['Wc'], 'L0_attn_bc': _L0_attn_in['bc'], 'L0_attn_Wd': _L0_attn_in['Wd'], 'L0_attn_bd': _L0_attn_in['bd'], 'L0_attn_Wy': _L0_attn_in['Wy'], 'L0_attn_by': _L0_attn_in['by'], 'L0_ffn_wqkv': _L0_ffn_in['wqkv'], 'L0_ffn_q_scale': _L0_ffn_in['q_scale'], 'L0_ffn_k_scale': _L0_ffn_in['k_scale'], 'L0_ffn_wo': _L0_ffn_in['wo'], 'L0_ffn_ln_g': _L0_ffn_in['ln_g'], 'L0_ffn_ln_b': _L0_ffn_in['ln_b'], 'L0_ffn_w1': _L0_ffn_in['w1'], 'L0_ffn_b1': _L0_ffn_in['b1'], 'L0_ffn_w2': _L0_ffn_in['w2'], 'L0_ffn_b2': _L0_ffn_in['b2'], 'L1_attn_Wq': _L1_attn_in['Wq'], 'L1_attn_Wk': _L1_attn_in['Wk'], 'L1_attn_Wv': _L1_attn_in['Wv'], 'L1_attn_Wo': _L1_attn_in['Wo'], 'L1_attn_bo': _L1_attn_in['bo'], 'L1_ffn_router_w': _L1_ffn_in['router_w'], 'L1_ffn_router_b': _L1_ffn_in['router_b'], 'L1_ffn_w1': _L1_ffn_in['w1'], 'L1_ffn_w2': _L1_ffn_in['w2'], 'L1_ffn_w3': _L1_ffn_in['w3'], 'L1_ffn_ln_g': _L1_ffn_in['ln_g'], 'L1_ffn_ln_b': _L1_ffn_in['ln_b']}
    _x0 = _d['L0_attn_x']
    _d['L0_attn_x'] = jax.random.normal(jax.random.fold_in(jax.random.key(seed), 1), (8, 256, 128), dtype=_x0.dtype)
    del _x0
    return _d

def reference(L0_attn_x, L0_attn_Wa, L0_attn_ba, L0_attn_Wb, L0_attn_bb, L0_attn_Wc, L0_attn_bc, L0_attn_Wd, L0_attn_bd, L0_attn_Wy, L0_attn_by, L0_ffn_wqkv, L0_ffn_q_scale, L0_ffn_k_scale, L0_ffn_wo, L0_ffn_ln_g, L0_ffn_ln_b, L0_ffn_w1, L0_ffn_b1, L0_ffn_w2, L0_ffn_b2, L1_attn_Wq, L1_attn_Wk, L1_attn_Wv, L1_attn_Wo, L1_attn_bo, L1_ffn_router_w, L1_ffn_router_b, L1_ffn_w1, L1_ffn_w2, L1_ffn_w3, L1_ffn_ln_g, L1_ffn_ln_b):

    def _L0_attn_ref(x, Wa, ba, Wb, bb, Wc, bc, Wd, bd, Wy, by):
        import jax, jax.numpy as jnp
        import numpy as np
        B, T, D, N = (8, 256, 128, 32)
        a = jax.nn.sigmoid(jnp.einsum('btd,dn->btn', x, Wa) + ba)
        b = jnp.einsum('btd,dn->btn', x, Wb) + bb
        c = jnp.tanh(jnp.einsum('btd,dn->btn', x, Wc) + bc)
        d = jnp.einsum('btd,de->bte', x, Wd) + bd

        def step(s, abc):
            at, bt, ct = abc
            s = at * s + (1.0 - at) * bt
            return (s, ct * s)
        aT = jnp.swapaxes(a, 0, 1)
        bT = jnp.swapaxes(b, 0, 1)
        cT = jnp.swapaxes(c, 0, 1)
        s0 = jnp.zeros((x.shape[0], Wa.shape[1]), x.dtype)
        _, csT = jax.lax.scan(step, s0, (aT, bT, cT))
        cs = jnp.swapaxes(csT, 0, 1)
        y = jnp.einsum('btn,nd->btd', cs, Wy) + by + d
        return y

    def _L0_ffn_ref(x, wqkv, q_scale, k_scale, wo, ln_g, ln_b, w1, b1, w2, b2):
        import jax, jax.numpy as jnp
        import numpy as np
        DIM = 128
        DEPTH = 2
        HEADS = 8
        DIM_HEAD = 64
        WINDOW = 64
        INNER = HEADS * DIM_HEAD
        HID = int(DIM * 4 * 2 / 3)
        B, N = (2, 1024)
        QK_SCALE = 8.0

        def shift_token(t):
            t1, t2 = jnp.split(t, 2, axis=-1)
            t2 = jnp.pad(t2, ((0, 0), (1, 0), (0, 0)))[:, :-1]
            return jnp.concatenate([t1, t2], axis=-1)

        def l2norm(t):
            return t / jnp.clip(jnp.linalg.norm(t, axis=-1, keepdims=True), 1e-12)

        def rotate_half(x):
            x1, x2 = jnp.split(x, 2, axis=-1)
            return jnp.concatenate([-x2, x1], axis=-1)

        def rotary_xpos(q, k):
            n = q.shape[-2]
            half_idx = jnp.arange(0, DIM_HEAD, 2, dtype=jnp.float32)
            inv_freq = 1.0 / 10000.0 ** (half_idx / DIM_HEAD)
            t = jnp.arange(n, dtype=jnp.float32)
            freqs = t[:, None] * inv_freq[None, :]
            freqs = jnp.concatenate([freqs, freqs], axis=-1)
            base = (half_idx + 0.4 * DIM_HEAD) / (1.4 * DIM_HEAD)
            power = (t - n // 2) / float(WINDOW // 2)
            scale = base[None, :] ** power[:, None]
            scale = jnp.concatenate([scale, scale], axis=-1)
            cos, sin = (jnp.cos(freqs), jnp.sin(freqs))
            q = q * cos * scale + rotate_half(q) * sin * scale
            k = k * cos / scale + rotate_half(k) * sin / scale
            return (q, k)

        def local_attention(q, k, v):
            b, h, n, d = q.shape
            w = n // WINDOW
            bq = q.reshape(b, h, w, WINDOW, d) * QK_SCALE
            bk = k.reshape(b, h, w, WINDOW, d)
            bv = v.reshape(b, h, w, WINDOW, d)

            def look_around(t):
                p = jnp.pad(t, ((0, 0), (0, 0), (1, 0), (0, 0), (0, 0)))
                return jnp.concatenate([p[:, :, :w], p[:, :, 1:]], axis=3)
            bk, bv = (look_around(bk), look_around(bv))
            bt = jnp.arange(n).reshape(w, WINDOW)
            btp = jnp.pad(bt, ((1, 0), (0, 0)), constant_values=-1)
            btk = jnp.concatenate([btp[:w], btp[1:]], axis=1)
            sim = jnp.einsum('bhwid,bhwjd->bhwij', bq, bk)
            i = bt[:, :, None]
            j = btk[:, None, :]
            mask = (i < j) | (i > j + WINDOW) | (j == -1)
            sim = jnp.where(mask, -jnp.finfo(sim.dtype).max, sim)
            attn = jax.nn.softmax(sim, axis=-1)
            out = jnp.einsum('bhwij,bhwjd->bhwid', attn, bv)
            return out.reshape(b, h, n, d)

        def _layer(x, wqkv, qs, ksc, wo, lg, lb, w1, b1, w2, b2):
            b, n, _ = x.shape
            h = shift_token(x)
            qkv = h @ wqkv
            q, k, v = jnp.split(qkv, 3, axis=-1)
            to_heads = lambda t: t.reshape(b, n, HEADS, DIM_HEAD).transpose(0, 2, 1, 3)
            q, k, v = (to_heads(q), to_heads(k), to_heads(v))
            q = l2norm(q) * qs
            k = l2norm(k) * ksc
            q, k = rotary_xpos(q, k)
            o = local_attention(q, k, v)
            o = o.transpose(0, 2, 1, 3).reshape(b, n, INNER)
            x = x + o @ wo
            h = shift_token(x)
            mu = h.mean(-1, keepdims=True)
            var = h.var(-1, keepdims=True)
            h = (h - mu) / jnp.sqrt(var + 1e-05) * lg + lb
            h = h @ w1 + b1
            a, g = jnp.split(h, 2, axis=-1)
            h = a * jax.nn.gelu(g, approximate=False)
            x = x + h @ w2 + b2
            return x
        for l in range(DEPTH):
            x = _layer(x, wqkv[l], q_scale[l], k_scale[l], wo[l], ln_g[l], ln_b[l], w1[l], b1[l], w2[l], b2[l])
        return x

    def _L1_attn_ref(x, Wq, Wk, Wv, Wo, bo):
        import jax, jax.numpy as jnp
        import numpy as np
        B, S, D_IN, D_OUT, H = (2, 256, 128, 128, 16)
        DK = D_OUT // H
        b, s, _ = x.shape
        q = (x @ Wq.T).reshape(b, s, H, DK).transpose(0, 2, 1, 3)
        k = (x @ Wk.T).reshape(b, s, H, DK).transpose(0, 2, 1, 3)
        v = (x @ Wv.T).reshape(b, s, H, DK).transpose(0, 2, 1, 3)
        scores = jnp.einsum('bhqd,bhkd->bhqk', q, k)
        causal = jnp.tril(jnp.ones((s, s), dtype=bool))
        scores = jnp.where(causal, scores, -jnp.inf)
        attn = jax.nn.softmax(scores / np.sqrt(DK), axis=-1)
        ctx = jnp.einsum('bhqk,bhkd->bhqd', attn, v)
        ctx = ctx.transpose(0, 2, 1, 3).reshape(b, s, D_OUT)
        return ctx @ Wo.T + bo

    def _L1_ffn_ref(x, router_w, router_b, w1, w2, w3, ln_g, ln_b):
        import jax, jax.numpy as jnp
        import numpy as np
        E, D, F = (16, 128, 256)
        B, N = (2, 256)
        LN_EPS = 1e-05
        'SparseMixtureOfExperts.forward (eval mode: no router noise, dropout=0).\n\n            Top-2 routing over softmax(router logits), renormalized; each selected\n            expert applies LayerNorm(SwiGLU(x)). Exact math of the torch masked loop,\n            expressed as a scan over experts with zero coefficients for unrouted tokens.\n            '
        Bx, Nx, Dx = x.shape
        xf = x.reshape(-1, Dx)
        logits = xf @ router_w.T + router_b
        probs = jax.nn.softmax(logits, axis=-1)
        top_w, top_e = jax.lax.top_k(probs, 2)
        top_w = top_w / jnp.sum(top_w, axis=-1, keepdims=True)

        def body(acc, params):
            W1, W2, W3, gm, bt, eid = params
            h = jax.nn.silu(xf @ W1.T) * (xf @ W3.T)
            y = h @ W2.T
            mu = jnp.mean(y, axis=-1, keepdims=True)
            var = jnp.var(y, axis=-1, keepdims=True)
            yn = (y - mu) / jnp.sqrt(var + LN_EPS) * gm + bt
            coeff = jnp.sum(jnp.where(top_e == eid, top_w, 0.0), axis=-1)
            return (acc + coeff[:, None] * yn, None)
        eids = jnp.arange(router_w.shape[0], dtype=top_e.dtype)
        out, _ = jax.lax.scan(body, jnp.zeros_like(xf), (w1, w2, w3, ln_g, ln_b, eids))
        return out.reshape(Bx, Nx, Dx)
    x = L0_attn_x
    xn = _layernorm(x, axis=-1)
    s = _L0_attn_ref(xn, L0_attn_Wa, L0_attn_ba, L0_attn_Wb, L0_attn_bb, L0_attn_Wc, L0_attn_bc, L0_attn_Wd, L0_attn_bd, L0_attn_Wy, L0_attn_by)
    g = _silu(_L0_ffn_ref(xn, L0_ffn_wqkv, L0_ffn_q_scale, L0_ffn_k_scale, L0_ffn_wo, L0_ffn_ln_g, L0_ffn_ln_b, L0_ffn_w1, L0_ffn_b1, L0_ffn_w2, L0_ffn_b2))
    x = x + s * g
    xn = _layernorm(x, axis=-1)
    s = _L1_attn_ref(xn, L1_attn_Wq, L1_attn_Wk, L1_attn_Wv, L1_attn_Wo, L1_attn_bo)
    g = _silu(_L1_ffn_ref(xn, L1_ffn_router_w, L1_ffn_router_b, L1_ffn_w1, L1_ffn_w2, L1_ffn_w3, L1_ffn_ln_g, L1_ffn_ln_b))
    x = x + s * g
    return x

_drawn_inputs = setup_inputs


def setup_inputs(seed=0):
    import zlib

    import numpy as np

    out = dict(_drawn_inputs(seed))
    spreads = {'L0_attn_ba': (0.0, 0.8),
     'L0_attn_bb': (0.0, 0.1),
     'L0_attn_bc': (0.0, 0.38),
     'L0_attn_bd': (0.0, 0.1),
     'L0_attn_by': (0.0, 0.1),
     'L0_ffn_q_scale': (1.0, 0.6),
     'L0_ffn_k_scale': (1.0, 0.6),
     'L0_ffn_ln_g': (1.0, 0.6),
     'L0_ffn_ln_b': (0.0, 0.8),
     'L0_ffn_b1': (0.0, 0.8),
     'L0_ffn_b2': (0.0, 0.1),
     'L1_ffn_router_b': (0.0, 0.449),
     'L1_ffn_ln_g': (1.0, 0.6),
     'L1_ffn_ln_b': (0.0, 0.8)}
    factors = {'L0_ffn_wqkv': 2.884,
     'L0_ffn_wo': 2.887,
     'L0_ffn_w1': 5.243,
     'L0_ffn_w2': 5.118,
     'L1_attn_Wq': 8.0,
     'L1_attn_Wk': 8.0,
     'L1_attn_Wv': 2.941,
     'L1_attn_Wo': 3.03,
     'L1_attn_bo': 9.825}
    for name, (base, spread) in spreads.items():
        noise = np.random.default_rng([zlib.crc32(name.encode()), seed]).standard_normal(out[name].shape)
        drawn = base * np.exp(spread * noise) if base else spread * noise
        out[name] = jnp.asarray(drawn.astype(out[name].dtype))
    for name, factor in factors.items():
        out[name] = (out[name] * factor).astype(out[name].dtype)
    return out
```

```python
from contextlib import ExitStack

import concourse.bass as bass
from concourse import mybir

F32 = mybir.dt.float32
BF16 = mybir.dt.bfloat16
U32 = mybir.dt.uint32
I32 = mybir.dt.int32
ALU = mybir.AluOpType
ACT = mybir.ActivationFunctionType
AX = mybir.AxisListType.X

P = 128
D = 128
NB, SEQ = 8, 256
NT = NB * SEQ // P
GT = 4
TURNS = NT // GT
TOK = GT * P
NS = 32
LAYERS = 2
INNER, DH = 512, 64
HID = 341
HC = [(0, 128), (128, 128), (256, 85)]
E, FE = 16, 256
DK1 = 8
CT = 48
CG = 4
EPS = 1e-5
MASKED = -1e30


class Pair:

    def __init__(self, ctx, nc, name):
        self.sems = [ctx.enter_context(nc.semaphore(f"{name}{i}")) for i in range(2)]

    def sem(self, n):
        return self.sems[n % 2]

    def begin(self, eng, by=1):
        for s in self.sems:
            eng.sem_inc(s, by)

    def did(self, half, n):
        return half + (n // 2 + 2)

    def reuse(self, half, n):
        return half + (n // 2 + 1)


def places(*stages):
    at, first = 0, {}
    for name, uses in stages:
        first[name] = at
        at += uses
    assert at % 2 == 0
    return first, at


T_A, T_A_USES = places(*[s for l in range(LAYERS) for s in (
    (("x", l), 1), (("qk", l), 8), (("att", l), 12), (("o", l), 4), (("h", l), 2))], ("x1", 2))
M_A, M_A_USES = places(("ab", 1), ("c", 1), *[s for l in range(LAYERS) for s in (
    (("qkv", l), 12), (("y", l), 1 - l), (("wo", l), 2), (("sh", l), 2), (("w1", l), 6), (("w2", l), 1))],
    ("router", 1))
S_A, S_A_USES = places((0, 12), (1, 12))
O_A, O_A_USES = places((0, 8), (1, 8))
T_P_USES = 2
T_W_USES = 2 * E
M_W_USES = 2
T_B, T_B_USES = places(("att", 24), ("ctx", 2))
M_B, M_B_USES = places(("qk", 8), ("v", 2), ("out", 2))
S_B_USES, O_B_USES = 24, 16
T_C, T_C_USES = places(("g", 4), ("x", 2))
M_C_USES = O_C_USES = CG
T_A0 = T_P_USES // 2
T_W0 = T_A0 + TURNS * T_A_USES // 2
T_B0 = T_W0 + T_W_USES // 2
T_X0 = T_B0 + TURNS * T_B_USES // 2
T_C0 = T_X0 + 1
M_W0 = TURNS * M_A_USES // 2
M_B0 = M_W0 + M_W_USES // 2
M_C0 = M_B0 + TURNS * M_B_USES // 2
S_B0 = TURNS * S_A_USES // 2
O_B0 = TURNS * O_A_USES // 2
O_C0 = O_B0 + TURNS * O_B_USES // 2
PV_C0 = S_B0 + TURNS * S_B_USES // 2
D_A_STEPS, D_B_STEPS, D_C_STEPS, P_A_STEPS, P_C_STEPS = 43, 26, 4, 22, 8


def gated_layers(nc, ins, out):
    ctx = ExitStack()
    with ctx:
        def sb(name, shape, dt=F32):
            return ctx.enter_context(nc.sbuf_tensor(name, shape, dt))

        def sem(name):
            return ctx.enter_context(nc.semaphore(name))

        def pair(name):
            return Pair(ctx, nc, name)

        Tb, Mb, Sb, Ob = ([ctx.enter_context(nc.psum_tensor(f"ps{n}{i}", [P, 512], F32)) for i in range(2)]
                          for n in "TMSO")
        t_full, t_free = pair("t_full"), pair("t_free")
        m_full, m_free = pair("m_full"), pair("m_free")
        s_full, s_free = pair("s_full"), pair("s_free")
        o_free = pair("o_free")
        exp_done = pair("exp_done")
        sq_done, ss_done = pair("sq_done"), pair("ss_done")
        rope_sum, rope_done = pair("rope_sum"), pair("rope_done")

        XG = nc.dram_tensor("xg_scratch", (CT * P, D), F32, kind="Internal").ap()
        YG = nc.dram_tensor("yg_scratch", (CT * P, D), F32, kind="Internal").ap()

        XALL = sb("XALL", [P, NT, D])
        XN1ALL = sb("XN1ALL", [P, NT, D])
        XNT1ALL = sb("XNT1ALL", [P, NT * P])
        S1ALL = sb("S1ALL", [P, NT, D])
        LG = sb("LG", [P, NT, E])
        ident = sb("ident", [P, P])
        identb = sb("identb", [P, P], BF16)
        mask0 = {0: sb("maskl0", [P, 512], BF16), 1: sb("maskc0", [P, 512], BF16)}
        mask1 = {0: sb("maskl1", [P, 512], BF16), 1: sb("maskc1", [P, 512], BF16)}
        shift = sb("shift", [P, P])
        carry = sb("carry", [P, P])
        trib = sb("trib", [P, P], BF16)
        onesb = sb("onesb", [P, P], BF16)
        powm = sb("powm", [P, 16])
        zeros = sb("zeros", [P, 512])
        SE = sb("SE", [P, 2, 512])
        PR = sb("PR", [P, 2, 512])
        PT = sb("PT", [P, 2, 512])
        MX = sb("MX", [P, 2, 4])
        RC = sb("RC", [P, 2, 4])
        ST = sb("ST", [P, GT, 2, 6])
        MV = sb("MV", [P, GT, 2])
        RS = sb("RS", [P, GT])
        WQP = sb("WQP", [P, 4, P])
        WKP = sb("WKP", [P, 4, P])
        WVT = sb("WVT", [P, P])
        WOT = sb("WOT", [P, P])
        RWT = sb("RWT", [P, E])
        borow = sb("borow", [P, D])
        rbrow = sb("rbrow", [P, E])
        GB = sb("GB", [P, E, D])
        BB = sb("BB", [P, E, D])

        ARENA = 31360
        arena = sb("arena", [P, ARENA])
        at = [0]

        def carve(*shape):
            n = 1
            for s in shape:
                n *= s
            v = arena[:, at[0]:at[0] + n]
            at[0] += n
            assert at[0] <= ARENA, at[0]
            if len(shape) == 1:
                return v
            names = "abcd"[:len(shape)]
            return v.rearrange(f"p ({' '.join(names)}) -> p {' '.join(names)}",
                               **{c: s for c, s in zip(names[1:], shape[1:])})

        S0 = carve(GT, D)
        XC = carve(GT, D)
        XNT = carve(TOK)
        HT = carve(2, SEQ)
        VA = carve(GT, 8, DH + 1)
        QT = carve(4, TOK)
        KT = carve(4, TOK)
        SQ = carve(2, 512)
        R1 = carve(2, 512)
        R2 = carve(2, 512)
        RQ = carve(2, 512)
        SS = carve(2, 8)
        RN = carve(2, 8)
        OS = carve(GT, 512)
        OT = carve(2, 512)
        HN = carve(GT, D)
        HNT = carve(TOK)
        GG = carve(2, 512)
        HG = carve(3, 512)
        EG = carve(GT, D)
        EA = carve(SEQ)
        AA = carve(SEQ)
        UU = carve(SEQ)
        SC = carve(SEQ)
        TC = carve(SEQ)
        CS = carve(SEQ)
        WABC = carve(3, NS)
        WD = carve(D)
        WYP = carve(2, D)
        ybrow = carve(2, D)
        bab = carve(4)
        WQKV = carve(LAYERS, 3, INNER)
        WO = carve(LAYERS, 4, D)
        W1 = carve(LAYERS, 2 * HID)
        W2 = carve(LAYERS, 3, D)
        lgc = carve(LAYERS, 2)
        b1c = carve(LAYERS, 2, 3)
        b2row = carve(LAYERS, D)
        ROPE = carve(2, 2, 2, DH)
        QKS = carve(LAYERS, 2, DH)
        RT = carve(LAYERS * 2, 2, 2, DH)
        WRAW = carve(5, P)
        at[0] = 0
        W13 = carve(E, 2 * FE)
        W2T = carve(E, 2 * D)
        after_weights = at[0]
        WST = carve(2, 3, 2 * D)
        QT1 = carve(4, TOK)
        KT1 = carve(4, TOK)
        VA1 = carve(GT, E, DK1 + 1)
        XS = carve(TOK)
        CTX = carve(GT, D)
        CTXT = carve(2, SEQ)
        MAXV = carve(NT, 8)
        ONEH = carve(2, NT, E)
        MIDX = carve(NT, 8)
        MIF = carve(2, NT)
        GW = carve(2, NT)
        CNT = carve(2, NT, E)
        CUM = carve(2, E, NT)
        IOT = carve(E, NT)
        IOTS = carve(E, NT)
        IOTJ = carve(CT, E)
        KEEP = carve(E, NT)
        NTI = carve(4, E)
        PF = carve(2, NT)
        ENDS = carve(CT, E)
        IOTI, IOTI2, IOTI3 = (carve(n).bitcast(I32) for n in (E * NT, E * NT, CT * E))
        EF = carve(CT)
        MB = carve(128)
        POSU = sb("POSU", [P, 2, NT], U32)
        EID = sb("EID", [P, CT], I32)
        WGT = sb("WGT", [P, 2, NT])
        ONEH_B = MB.bitcast(BF16)
        at[0] = after_weights
        XGS = carve(CG, D)
        XGT = carve(TOK)
        HS = carve(2, FE)
        GS = carve(2, FE)
        GTT = carve(2, FE)
        YN = carve(2, D)
        YO = carve(2, D)
        YAB = carve(NT, 2, D)
        G2 = carve(GT, D)
        G3 = carve(GT, D)
        OUTB = carve(2, TOK)

        ld_x, ld_a, ld_l1, ld_raw = sem("ld_x"), sem("ld_a"), sem("ld_l1"), sem("ld_raw")
        ld_w = pair("ld_w")
        zeroed, scattered = sem("zeroed"), sem("scattered")
        gathered = [sem(f"gathered{c}") for c in range(TURNS)]
        ld_g, st_y, st_out = sem("ld_g"), pair("st_y"), pair("st_out")
        pool_consts, dve_consts, tables = sem("pool_consts"), sem("dve_consts"), sem("tables")
        a_over, b_over = sem("a_over"), sem("b_over")
        dve_settled, pool_settled = sem("dve_settled"), sem("pool_settled")
        dstep, pstep = sem("dstep"), sem("pstep")
        stats_done, rstd_done = sem("stats_done"), sem("rstd_done")
        xn_ready, ea_done, cs_done = sem("xn_ready"), sem("ea_done"), sem("cs_done")
        ffn_added, eg_done = sem("ffn_added"), sem("eg_done")
        xn1_ready, xn1_kept = sem("xn1_ready"), sem("xn1_kept")
        onehot, gap_done, gap_exp = sem("onehot"), sem("gap_done"), sem("gap_exp")
        pos_done, xs_ready = sem("pos_done"), sem("xs_ready")
        c_silu, c_yo, c_stats, c_rstd = pair("c_silu"), pair("c_yo"), pair("c_stats"), pair("c_rstd")
        pv_done, iota_raw, iotas = pair("pv_done"), sem("iota_raw"), sem("iotas")
        moe_in, silu_done, out_ready = sem("moe_in"), sem("silu_done"), sem("out_ready")
        ENGINES = 4

        XG3 = XG.rearrange("(j p) d -> j p d", p=P)
        YG3 = YG.rearrange("(j p) d -> j p d", p=P)

        def stage(lanes, kd, dv, q, k, v, o, masks):
            units = []
            for b in range(2):
                for lane in range(lanes):
                    units.append((b, 0, lane, range(4)))
                for lane in range(lanes):
                    for h in range(2):
                        units.append((b, 1, lane, range(2 * h, 2 * h + 2)))
            return dict(lanes=lanes, kd=kd, dv=dv, q=q, k=k, v=v, o=o, masks=masks, units=units)

        ATT0 = stage(2, DH, DH, QT, KT, VA, OS, (mask0[0], mask1[0]))
        ATT1 = stage(4, DK1, DK1, QT1, KT1, VA1, CTX, (mask0[1], mask1[1]))

        def o_use(g, u):
            b, qt, lane, slots = g["units"][u]
            return (2 * b + qt) * g["lanes"] + lane, slots[0] == 0, slots[-1] == 3

        small_loads = []
        for i, w in enumerate(("Wa", "Wb", "Wc")):
            small_loads.append((WABC[:, i, :], ins[f"L0_attn_{w}"]))
        for i, w in enumerate(("ba", "bb", "bc")):
            for b in range(2):
                small_loads.append((bab[NS * b:NS * b + NS, i:i + 1], ins[f"L0_attn_{w}"].unsqueeze(1)))
        small_loads.append((WD, ins["L0_attn_Wd"]))
        for b in range(2):
            small_loads.append((WYP[NS * b:NS * b + NS, b, :], ins["L0_attn_Wy"]))
        small_loads.append((ybrow[:, 0, :], ins["L0_attn_by"].partition_broadcast(P)))
        small_loads.append((ybrow[:, 1, :], ins["L0_attn_bd"].partition_broadcast(P)))
        for k in range(2):
            for x in range(2):
                small_loads.append((ROPE[:, k, x], ins["rope"][k, x].rearrange("(t p) d -> p t d", p=P)))
        for l in range(LAYERS):
            small_loads.append((WQKV[:, l].rearrange("p s n -> p (s n)"), ins["L0_ffn_wqkv"][l]))
            small_loads.append((QKS[:, l, 0, :], ins["L0_ffn_q_scale"][l].partition_broadcast(P)))
            small_loads.append((QKS[:, l, 1, :], ins["L0_ffn_k_scale"][l].partition_broadcast(P)))
            small_loads.append((WO[:, l], ins["L0_ffn_wo"][l].rearrange("(c p) n -> p c n", p=P)))
            small_loads.append((W1[:, l, :], ins["L0_ffn_w1"][l]))
            small_loads.append((W2[:, l, 0:2, :], ins["L0_ffn_w2"][l][0:256].rearrange("(c p) n -> p c n", p=P)))
            small_loads.append((W2[0:85, l, 2, :], ins["L0_ffn_w2"][l][256:HID]))
            small_loads.append((lgc[:, l, 0:1], ins["L0_ffn_ln_g"][l].unsqueeze(1)))
            small_loads.append((lgc[:, l, 1:2], ins["L0_ffn_ln_b"][l].unsqueeze(1)))
            for h in range(2):
                for c, (f, m) in enumerate(HC):
                    small_loads.append((b1c[0:m, l, h, c:c + 1],
                                        ins["L0_ffn_b1"][l][h * HID + f:h * HID + f + m].unsqueeze(1)))
            small_loads.append((b2row[:, l, :], ins["L0_ffn_b2"][l].partition_broadcast(P)))
        LOADED_A = 16 * len(small_loads)
        POOL_CONSTS = 12 + 5 + 4 + 2

        block = ctx.enter_context(nc.Block())

        @block.sync
        def _(sp):
            st_y.begin(sp, 16)
            sp.dma_start(XALL[:], ins["L0_attn_x"].rearrange("b (t p) d -> p (b t) d", p=P)).then_inc(ld_x, 16)
            sp.wait_ge(dve_consts, 1)
            for dst, src in small_loads:
                sp.dma_start(dst, src).then_inc(ld_a, 16)
            for i, w in enumerate(("Wq", "Wk", "Wv", "Wo")):
                sp.dma_start(WRAW[:, i, :], ins[f"L1_attn_{w}"]).then_inc(ld_raw, 16)
            sp.dma_start(WRAW[0:E, 4, :], ins["L1_ffn_router_w"]).then_inc(ld_raw, 16)
            sp.dma_start(borow[:], ins["L1_attn_bo"].partition_broadcast(P)).then_inc(ld_l1, 16)
            sp.dma_start(rbrow[:], ins["L1_ffn_router_b"].partition_broadcast(P)).then_inc(ld_l1, 16)
            sp.dma_start(GB[:].rearrange("p e d -> p (e d)"),
                         ins["L1_ffn_ln_g"].rearrange("e d -> (e d)").partition_broadcast(P)).then_inc(ld_l1, 16)
            sp.dma_start(BB[:].rearrange("p e d -> p (e d)"),
                         ins["L1_ffn_ln_b"].rearrange("e d -> (e d)").partition_broadcast(P)).then_inc(ld_l1, 16)
            sp.wait_ge(pool_consts, POOL_CONSTS)
            for j in range(0, CT, 4):
                sp.dma_start(XG3[j:j + 4].rearrange("j p d -> p j d"),
                             zeros[:].rearrange("p (j d) -> p j d", j=4)).then_inc(zeroed, 16)
            sp.wait_ge(a_over, ENGINES)
            with sp.Fori(0, E // 2) as i:
                for p in range(2):
                    e = i * 2 + p
                    sp.wait_ge(t_full.sem(1), t_full.did(T_W0 + e - 2, 1))
                    sp.dma_start(WST[:, p, 0, :].rearrange("p (k d) -> p k d", k=2),
                                 ins["L1_ffn_w1"][e].rearrange("(k p) d -> p k d", p=P)).then_inc(ld_w.sem(p), 16)
                    sp.dma_start(WST[:, p, 1, :].rearrange("p (k d) -> p k d", k=2),
                                 ins["L1_ffn_w3"][e].rearrange("(k p) d -> p k d", p=P)).then_inc(ld_w.sem(p), 16)
                    sp.dma_start(WST[:, p, 2, :], ins["L1_ffn_w2"][e]).then_inc(ld_w.sem(p), 16)
            sp.wait_ge(scattered, 16 * 2 * NT)
            sp.wait_ge(b_over, ENGINES)
            sp.dma_start(XGS, XG3[0:CG].rearrange("j p d -> p j d")).then_inc(ld_g, 16)

            def turn(i, last):
                if not last:
                    sp.wait_ge(t_full.sem(1), t_full.did(T_X0 + i * (T_C_USES // 2), 1))
                    sp.dma_start(XGS, XG3[bass.ds(i * CG + CG, CG)].rearrange("j p d -> p j d")).then_inc(ld_g, 16)
                for j in range(CG):
                    sp.wait_ge(c_yo.sem(j), c_yo.did(i * (CG // 2), j))
                    sp.dma_start(YG3[i * CG + j], YO[:, j % 2, :]).then_inc(st_y.sem(j), 16)

            with sp.Fori(0, CT // CG - 1) as i:
                turn(i, False)
            turn(CT // CG - 1, True)
            for c in range(TURNS):
                sp.wait_ge(out_ready, c + 1)
                sp.dma_start(out.rearrange("b (t p) d -> p (b t) d", p=P)[:, c * GT:c * GT + GT, :],
                             OUTB[:, c % 2, :].rearrange("p (t d) -> p t d", t=GT)).then_inc(st_out.sem(c), 16)
            for p in range(2):
                sp.wait_ge(st_out.sem(p), 16 * TURNS // 2)

        @block.tensor
        def _(pe):
            def mm(o, lhsT, rhs, start=True, stop=True):
                return nc.tensor.matmul(o, lhsT, rhs, start=start, stop=stop)

            for events in (t_full, m_full, s_full, pv_done):
                events.begin(pe)

            def t_open(ht, n):
                pe.wait_ge(t_free.sem(n), t_free.reuse(ht, n))
                return Tb[n % 2]

            def m_open(hm, n):
                pe.wait_ge(m_free.sem(n), m_free.reuse(hm, n))
                return Mb[n % 2]

            def attention(g, ht, t0, hs, s0, ho, o0, batch_ready):
                units, rows, kd, w = g["units"], P // g["lanes"], g["kd"], g["dv"] + 1
                for k in range(len(units) + 2):
                    if k < len(units):
                        b, qt, lane, slots = units[k]
                        if k % (len(units) // 2) == 0:
                            batch_ready(b)
                        n = s0 + k
                        pe.wait_ge(s_free.sem(n), s_free.reuse(hs, n))
                        bank, keys, r = Sb[n % 2], P * (qt + 1), slice(rows * lane, rows * lane + kd)
                        mm(bank[:], identb[:], g["masks"][qt][:], True, False)
                        for i, s in enumerate(slots):
                            last = mm(bank[:, i * keys:(i + 1) * keys],
                                      g["q"][r, s, (2 * b + qt) * P:(2 * b + qt + 1) * P],
                                      g["k"][r, s, 2 * b * P:2 * b * P + keys], False, i == len(slots) - 1)
                        last.then_inc(s_full.sem(n), 1)
                    if 1 <= k <= len(units):
                        n, m = t0 + k - 1, s0 + k - 1
                        pe.wait_ge(exp_done.sem(m), exp_done.did(hs, m))
                        bank = t_open(ht, n)
                        for c in range(4):
                            last = nc.tensor.transpose(bank[:, c * P:(c + 1) * P], PR[:, m % 2, c * P:(c + 1) * P],
                                                       ident[:])
                        last.then_inc(t_full.sem(n), 1)
                    if k >= 2:
                        u = k - 2
                        b, qt, lane, slots = units[u]
                        n, m = t0 + u, s0 + u
                        o, starts, ends = o_use(g, u)
                        o += o0
                        if starts:
                            pe.wait_ge(o_free.sem(o), o_free.reuse(ho, o))
                        pe.wait_ge(t_free.sem(n), t_free.did(ht, n))
                        c = 0
                        for s in slots:
                            head = g["lanes"] * s + lane
                            for kt in range(qt + 1):
                                last = mm(Ob[o % 2][:, s * w:(s + 1) * w], PT[:, m % 2, c * P:(c + 1) * P],
                                          g["v"][:, 2 * b + kt, head, :], kt == 0, kt == qt)
                                c += 1
                        last.then_inc(pv_done.sem(m), 1)

            pe.wait_ge(ld_raw, 16 * 5)
            pe.wait_ge(pool_consts, POOL_CONSTS)
            for c in range(4):
                last = nc.tensor.transpose(Tb[0][:, c * P:(c + 1) * P], WRAW[:, c, :], ident[:])
            last.then_inc(t_full.sem(0), 1)
            nc.tensor.transpose(Tb[1][:, 0:E], WRAW[0:E, 4, :], ident[0:E, 0:E]).then_inc(t_full.sem(1), 1)
            pe.wait_ge(ld_a, LOADED_A)
            pe.wait_ge(dve_consts, 2)

            with pe.Fori(0, TURNS) as it:
                ht, hm = T_A0 + it * (T_A_USES // 2), it * (M_A_USES // 2)
                hs, ho = it * (S_A_USES // 2), it * (O_A_USES // 2)
                for l in range(LAYERS):
                    if l == 0:
                        pe.wait_ge(xn_ready, it + 1)
                    else:
                        pe.wait_ge(ffn_added, it * LAYERS + 1)
                    n = T_A["x", l]
                    bank = t_open(ht, n)
                    for t in range(GT):
                        last = nc.tensor.transpose(bank[:, t * P:(t + 1) * P], XC[:, t, :], ident[:])
                    last.then_inc(t_full.sem(n), 1)
                    pe.wait_ge(t_free.sem(n), t_free.did(ht, n))
                    if l == 0:
                        n = M_A["ab"]
                        bank = m_open(hm, n)
                        for i in range(2):
                            for b in range(2):
                                last = mm(bank[NS * b:NS * b + NS, i * SEQ:(i + 1) * SEQ], WABC[:, i, :],
                                          XNT[:, b * SEQ:(b + 1) * SEQ])
                        last.then_inc(m_full.sem(n), 1)
                        n = M_A["c"]
                        bank = m_open(hm, n)
                        for b in range(2):
                            last = mm(bank[NS * b:NS * b + NS, 0:SEQ], WABC[:, 2, :], XNT[:, b * SEQ:(b + 1) * SEQ])
                        last.then_inc(m_full.sem(n), 1)
                    for t in range(GT + 1):
                        if t < GT:
                            for i in range(3):
                                n = M_A["qkv", l] + 3 * t + i
                                mm(m_open(hm, n)[:], HT[:, t // 2, (t % 2) * P:(t % 2 + 1) * P], WQKV[:, l, i, :])\
                                    .then_inc(m_full.sem(n), 1)
                        if t >= 1:
                            for i in range(2):
                                n, m = T_A["qk", l] + 2 * (t - 1) + i, 8 * l + 2 * (t - 1) + i
                                pe.wait_ge(rope_done.sem(m), rope_done.did(it * 8, m))
                                bank = t_open(ht, n)
                                for c in range(4):
                                    last = nc.tensor.transpose(bank[:, c * P:(c + 1) * P],
                                                               RQ[:, m % 2, c * P:(c + 1) * P], ident[:])
                                last.then_inc(t_full.sem(n), 1)
                    if l == 0:
                        pe.wait_ge(cs_done, it + 1)
                        n = M_A["y", 0]
                        bank = m_open(hm, n)
                        for t in range(GT):
                            mm(bank[:, t * P:(t + 1) * P], CS[0:2 * NS, (t % 2) * P:(t % 2 + 1) * P],
                               WYP[0:2 * NS, t // 2, :], True, False)
                            last = mm(bank[:, t * P:(t + 1) * P], XNT[:, t * P:(t + 1) * P], WD, False, True)
                        last.then_inc(m_full.sem(n), 1)

                    def ready(b, l=l):
                        n = T_A["qk", l] + 4 * b + 3
                        pe.wait_ge(t_free.sem(n), t_free.did(ht, n))

                    attention(ATT0, ht, T_A["att", l], hs, S_A[l], ho, O_A[l], ready)
                    for t in range(GT):
                        n, o = T_A["o", l] + t, O_A[l] + 2 * t + 1
                        pe.wait_ge(o_free.sem(o), o_free.did(ho, o))
                        pe.wait_ge(o_free.sem(o - 1), o_free.did(ho, o - 1))
                        bank = t_open(ht, n)
                        for c in range(4):
                            last = nc.tensor.transpose(bank[:, c * P:(c + 1) * P], OS[:, t, c * P:(c + 1) * P],
                                                       ident[:])
                        last.then_inc(t_full.sem(n), 1)
                        m = M_A["wo", l] + t // 2
                        if t % 2 == 0:
                            bank = m_open(hm, m)
                        pe.wait_ge(t_free.sem(n), t_free.did(ht, n))
                        for c in range(4):
                            last = mm(Mb[m % 2][:, (t % 2) * P:(t % 2 + 1) * P], OT[:, t % 2, c * P:(c + 1) * P],
                                      WO[:, l, c, :], c == 0, c == 3)
                        if t % 2 == 1:
                            last.then_inc(m_full.sem(m), 1)
                    for b in range(2):
                        n = M_A["wo", l] + b
                        pe.wait_ge(m_free.sem(n), m_free.did(hm, n))
                        n = M_A["sh", l] + b
                        bank = m_open(hm, n)
                        mm(bank[:, 0:64], shift[:], XC[:, 2 * b, 64:D])
                        mm(bank[:, 64:128], shift[:], XC[:, 2 * b + 1, 64:D], True, False)
                        mm(bank[:, 64:128], carry[:], XC[:, 2 * b, 64:D], False, True).then_inc(m_full.sem(n), 1)
                    for b in range(2):
                        n = M_A["sh", l] + b
                        pe.wait_ge(m_free.sem(n), m_free.did(hm, n))
                        n = T_A["h", l] + b
                        bank = t_open(ht, n)
                        for t in range(2):
                            last = nc.tensor.transpose(bank[:, t * P:(t + 1) * P], HN[:, 2 * b + t, :], ident[:])
                        last.then_inc(t_full.sem(n), 1)
                    for b in range(2):
                        n = T_A["h", l] + b
                        pe.wait_ge(t_free.sem(n), t_free.did(ht, n))
                    for c, (f, m) in enumerate(HC):
                        for h in (1, 0):
                            n = M_A["w1", l] + 2 * c + 1 - h
                            mm(m_open(hm, n)[0:m, :], W1[:, l, h * HID + f:h * HID + f + m], HNT)\
                                .then_inc(m_full.sem(n), 1)
                    n = M_A["w1", l] + 5
                    pe.wait_ge(m_free.sem(n), m_free.did(hm, n))
                    n = M_A["w2", l]
                    bank = m_open(hm, n)
                    for t in range(GT):
                        for c, (f, m) in enumerate(HC):
                            last = mm(bank[:, t * P:(t + 1) * P], HG[0:m, c, t * P:(t + 1) * P], W2[0:m, l, c, :],
                                      c == 0, c == 2)
                    last.then_inc(m_full.sem(n), 1)
                pe.wait_ge(xn1_ready, it + 1)
                for b in range(2):
                    n = T_A["x1"] + b
                    bank = t_open(ht, n)
                    for t in range(2):
                        last = nc.tensor.transpose(bank[:, t * P:(t + 1) * P], HN[:, 2 * b + t, :], ident[:])
                    last.then_inc(t_full.sem(n), 1)
                for b in range(2):
                    n = T_A["x1"] + b
                    pe.wait_ge(t_free.sem(n), t_free.did(ht, n))
                n = M_A["router"]
                bank = m_open(hm, n)
                for t in range(GT):
                    last = mm(bank[:, t * E:(t + 1) * E], XNT[:, t * P:(t + 1) * P], RWT[:])
                last.then_inc(m_full.sem(n), 1)
            pe.drain().then_inc(a_over, 1)
            pe.wait_ge(a_over, ENGINES)

            with pe.Fori(0, E // 2) as i:
                ht = T_W0 + i * 2
                for p in range(2):
                    pe.wait_ge(ld_w.sem(p), (i + 1) * 48)
                    bank = t_open(ht, 2 * p)
                    for c in range(4):
                        last = nc.tensor.transpose(bank[:, c * P:(c + 1) * P],
                                                   WST[:, p, c // 2, (c % 2) * P:(c % 2 + 1) * P], ident[:])
                    last.then_inc(t_full.sem(2 * p), 1)
                    bank = t_open(ht, 2 * p + 1)
                    for c in range(2):
                        last = nc.tensor.transpose(bank[:, c * P:(c + 1) * P], WST[:, p, 2, c * P:(c + 1) * P],
                                                   ident[:])
                    last.then_inc(t_full.sem(2 * p + 1), 1)
            pe.wait_ge(onehot, 1)
            mm(m_open(M_W0, 0)[:, 0:NT * E], trib[:], ONEH_B).then_inc(m_full.sem(0), 1)
            mm(m_open(M_W0, 1)[:, 0:NT * E], onesb[:], ONEH_B).then_inc(m_full.sem(1), 1)

            with pe.Fori(0, TURNS) as it:
                ht, hm = T_B0 + it * (T_B_USES // 2), M_B0 + it * (M_B_USES // 2)
                hs, ho = S_B0 + it * (S_B_USES // 2), O_B0 + it * (O_B_USES // 2)
                for g in range(4):
                    for i, w in enumerate((WQP, WKP)):
                        n = M_B["qk"] + 2 * g + i
                        mm(m_open(hm, n)[:], w[:, g, :], XNT1ALL[:, bass.ds(it * TOK, TOK)])\
                            .then_inc(m_full.sem(n), 1)
                pe.wait_ge(xs_ready, it + 1)
                for b in range(2):
                    n = M_B["v"] + b
                    bank = m_open(hm, n)
                    for t in range(2):
                        last = mm(bank[:, t * P:(t + 1) * P], XS[:, (2 * b + t) * P:(2 * b + t + 1) * P], WVT[:])
                    last.then_inc(m_full.sem(n), 1)

                def ready(b):
                    for n in (M_B["qk"] + 6, M_B["qk"] + 7, M_B["v"], M_B["v"] + 1):
                        pe.wait_ge(m_free.sem(n), m_free.did(hm, n))

                attention(ATT1, ht, T_B["att"], hs, 0, ho, 0, ready)
                for b in range(2):
                    n = T_B["ctx"] + b
                    for o in (8 * b + 6, 8 * b + 7):
                        pe.wait_ge(o_free.sem(o), o_free.did(ho, o))
                    bank = t_open(ht, n)
                    for t in range(2):
                        last = nc.tensor.transpose(bank[:, t * P:(t + 1) * P], CTX[:, 2 * b + t, :], ident[:])
                    last.then_inc(t_full.sem(n), 1)
                for b in range(2):
                    n = T_B["ctx"] + b
                    pe.wait_ge(t_free.sem(n), t_free.did(ht, n))
                    n = M_B["out"] + b
                    bank = m_open(hm, n)
                    for t in range(2):
                        last = mm(bank[:, t * P:(t + 1) * P], CTXT[:, b, t * P:(t + 1) * P], WOT[:])
                    last.then_inc(m_full.sem(n), 1)
            pe.drain().then_inc(b_over, 1)
            pe.wait_ge(b_over, ENGINES)

            def tiles_t(ht, n0):
                for b in range(2):
                    bank = t_open(ht, n0 + b)
                    for t in range(2):
                        last = nc.tensor.transpose(bank[:, t * P:(t + 1) * P], XGS[:, 2 * b + t, :], ident[:])
                    last.then_inc(t_full.sem(n0 + b), 1)

            pe.wait_ge(ld_g, 16)
            tiles_t(T_X0, 0)
            for b in range(2):
                pe.wait_ge(t_free.sem(b), t_free.did(T_X0, b))

            def turn(i, last_turn):
                ht, hm, ho = T_C0 + i * (T_C_USES // 2), M_C0 + i * 2, O_C0 + i * 2
                e = [pe.value_load(EID[0:1, bass.ds(i * CG + j, 1)], min_val=0, max_val=E - 1) for j in range(CG)]

                def hidden(j):
                    mm(m_open(hm, j)[:], XGT[:, j * P:(j + 1) * P], W13[:, e[j], :]).then_inc(m_full.sem(j), 1)

                def gate_t(j):
                    pe.wait_ge(m_free.sem(j), m_free.did(hm, j))
                    bank = t_open(ht, j)
                    for c in range(2):
                        last = nc.tensor.transpose(bank[:, c * P:(c + 1) * P], GS[:, j % 2, c * P:(c + 1) * P],
                                                   ident[:])
                    last.then_inc(t_full.sem(j), 1)

                def down(j):
                    pe.wait_ge(t_free.sem(j), t_free.did(ht, j))
                    pe.wait_ge(o_free.sem(j), o_free.reuse(ho, j))
                    for c in range(2):
                        last = mm(Ob[j % 2][:, 0:D], GTT[:, j % 2, c * P:(c + 1) * P],
                                  W2T[:, e[j], c * D:(c + 1) * D], c == 0, c == 1)
                    last.then_inc(pv_done.sem(j), 1)

                hidden(0)
                hidden(1)
                gate_t(0)
                hidden(2)
                gate_t(1)
                down(0)
                hidden(3)
                gate_t(2)
                down(1)
                gate_t(3)
                if not last_turn:
                    pe.wait_ge(ld_g, i * 16 + 32)
                    tiles_t(ht, T_C["x"])
                down(2)
                down(3)
                if not last_turn:
                    for b in range(2):
                        n = T_C["x"] + b
                        pe.wait_ge(t_free.sem(n), t_free.did(ht, n))

            with pe.Fori(0, CT // CG - 1) as i:
                turn(i, False)
            turn(CT // CG - 1, True)

        @block.scalar
        def _(act):
            def act_fn(o, i, f, **kw):
                return nc.scalar.activation(o, i, f, **kw)

            for events in (t_free, exp_done, sq_done, c_silu):
                events.begin(act)

            def attention(g, ht, t0, hs, s0):
                units = g["units"]
                for k in range(len(units) + 1):
                    if k < len(units):
                        n = s0 + k
                        act.wait_ge(s_free.sem(n), s_free.did(hs, n))
                        act_fn(PR[:, n % 2, :], SE[:, n % 2, :], ACT.Exp).then_inc(exp_done.sem(n), 1)
                    if k >= 1:
                        n, m = t0 + k - 1, s0 + k - 1
                        act.wait_ge(t_full.sem(n), t_full.did(ht, n))
                        act.wait_ge(pv_done.sem(m), pv_done.reuse(hs, m))
                        act_fn(PT[:, m % 2, :], Tb[n % 2][:], ACT.Copy).then_inc(t_free.sem(n), 1)

            act.wait_ge(t_full.sem(0), t_full.did(0, 0))
            act.wait_ge(dve_consts, 1)
            for i, w in enumerate((WQP, WKP)):
                act_fn(w[:].rearrange("p g (j d) -> p g j d", j=4)[:, :, :, 0:DK1],
                       Tb[0][:, i * P:(i + 1) * P].rearrange("p (g j d) -> p g j d", g=4, j=4), ACT.Copy)
            act_fn(WVT[:], Tb[0][:, 2 * P:3 * P], ACT.Copy)
            act_fn(WOT[:], Tb[0][:, 3 * P:4 * P], ACT.Copy).then_inc(t_free.sem(0), 1)
            act.wait_ge(t_full.sem(1), t_full.did(0, 1))
            act_fn(RWT[:], Tb[1][:, 0:E], ACT.Copy).then_inc(t_free.sem(1), 1)
            act.wait_ge(tables, 1)
            act.wait_ge(ld_a, LOADED_A)

            with act.Fori(0, TURNS) as it:
                ht, hm = T_A0 + it * (T_A_USES // 2), it * (M_A_USES // 2)
                hs, ho = it * (S_A_USES // 2), it * (O_A_USES // 2)
                for l in range(LAYERS):
                    n = T_A["x", l]
                    act.wait_ge(t_full.sem(n), t_full.did(ht, n))
                    bank = Tb[n % 2][:].rearrange("p (b t) -> p b t", b=2)
                    if l == 0:
                        act.wait_ge(xn1_kept, it + 1)
                        act_fn(XNT, Tb[n % 2][:], ACT.Copy)
                    act_fn(HT[0:64], bank[0:64], ACT.Copy)
                    act_fn(HT[64:P, :, 1:SEQ], bank[64:P, :, 0:SEQ - 1], ACT.Copy).then_inc(t_free.sem(n), 1)
                    if l == 0:
                        n = M_A["ab"]
                        act.wait_ge(m_full.sem(n), m_full.did(hm, n))
                        act_fn(EA[0:2 * NS], Mb[n % 2][0:2 * NS, 0:SEQ], ACT.Exp, scale=-1.0,
                               bias=bab[0:2 * NS, 3:4]).then_inc(ea_done, 1)
                        n = M_A["c"]
                        act.wait_ge(m_full.sem(n), m_full.did(hm, n))
                        act_fn(TC[0:2 * NS], Mb[n % 2][0:2 * NS, 0:SEQ], ACT.Tanh,
                               bias=bab[0:2 * NS, 2:3]).then_inc(m_free.sem(n), 1)
                    for t in range(GT + 1):
                        if t < GT:
                            for i in range(2):
                                n, m = M_A["qkv", l] + 3 * t + i, 8 * l + 2 * t + i
                                act.wait_ge(m_full.sem(n), m_full.did(hm, n))
                                act.wait_ge(ss_done.sem(m), ss_done.reuse(it * 8, m))
                                act_fn(SQ[:, m % 2, :], Mb[n % 2][:], ACT.Square).then_inc(sq_done.sem(m), 1)
                            n = M_A["qkv", l] + 3 * t + 2
                            act.wait_ge(m_full.sem(n), m_full.did(hm, n))
                            act_fn(VA[:, t, :, 0:DH], Mb[n % 2][:].rearrange("p (h d) -> p h d", h=8), ACT.Copy)\
                                .then_inc(m_free.sem(n), 1)
                        if t >= 1:
                            for i, dst in enumerate((QT, KT)):
                                n = T_A["qk", l] + 2 * (t - 1) + i
                                act.wait_ge(t_full.sem(n), t_full.did(ht, n))
                                act_fn(dst[:, :, (t - 1) * P:t * P],
                                       Tb[n % 2][:].rearrange("p (c t) -> p c t", c=4), ACT.Copy)\
                                    .then_inc(t_free.sem(n), 1)
                    attention(ATT0, ht, T_A["att", l], hs, S_A[l])
                    for t in range(GT):
                        n = T_A["o", l] + t
                        act.wait_ge(t_full.sem(n), t_full.did(ht, n))
                        if t == 2:
                            m = M_A["wo", l]
                            act.wait_ge(m_full.sem(m), m_full.did(hm, m))
                        act_fn(OT[:, t % 2, :], Tb[n % 2][:], ACT.Copy).then_inc(t_free.sem(n), 1)
                    for b in range(2):
                        n = T_A["h", l] + b
                        act.wait_ge(t_full.sem(n), t_full.did(ht, n))
                        act_fn(HNT[:, b * SEQ:(b + 1) * SEQ], Tb[n % 2][:, 0:SEQ], ACT.Identity,
                               scale=lgc[:, l, 0:1], bias=lgc[:, l, 1:2]).then_inc(t_free.sem(n), 1)
                    for c, (f, m) in enumerate(HC):
                        n = M_A["w1", l] + 2 * c
                        act.wait_ge(m_full.sem(n), m_full.did(hm, n))
                        if c == 2:
                            act.wait_ge(m_free.sem(n + 1 - 4), m_free.did(hm, n + 1 - 4))
                        act_fn(GG[0:m, c % 2, :], Mb[n % 2][0:m, :], ACT.Gelu, bias=b1c[0:m, l, 1, c:c + 1])\
                            .then_inc(m_free.sem(n), 1)
                act.wait_ge(ffn_added, it * LAYERS + 2)
                act_fn(EG[:].rearrange("p t d -> p (t d)"), XC[:].rearrange("p t d -> p (t d)"), ACT.Exp,
                       scale=-1.0).then_inc(eg_done, 1)
                for b in range(2):
                    n = T_A["x1"] + b
                    act.wait_ge(t_full.sem(n), t_full.did(ht, n))
                    act_fn(XNT[:, b * SEQ:(b + 1) * SEQ], Tb[n % 2][:, 0:SEQ], ACT.Copy).then_inc(t_free.sem(n), 1)
            act.drain().then_inc(a_over, 1)
            act.wait_ge(a_over, ENGINES)

            with act.Fori(0, E // 2) as i:
                for p in range(2):
                    act.wait_ge(t_full.sem(0), t_full.did(T_W0 + i * 2 + p, 0))
                    act_fn(W13[:, i * 2 + p, :], Tb[0][:], ACT.Copy).then_inc(t_free.sem(0), 1)
                    act.wait_ge(t_full.sem(1), t_full.did(T_W0 + i * 2 + p, 1))
                    act_fn(W2T[:, i * 2 + p, :], Tb[1][:, 0:2 * D], ACT.Copy).then_inc(t_free.sem(1), 1)
            act.wait_ge(gap_done, 1)
            act_fn(GW[:, 0, :], GW[:, 1, :], ACT.Exp).then_inc(gap_exp, 1)

            with act.Fori(0, TURNS) as it:
                ht, hm = T_B0 + it * (T_B_USES // 2), M_B0 + it * (M_B_USES // 2)
                hs, ho = S_B0 + it * (S_B_USES // 2), O_B0 + it * (O_B_USES // 2)
                for n in (M_B["v"], M_B["v"] + 1):
                    act.wait_ge(m_full.sem(n), m_full.did(hm - M_B_USES // 2, n))
                act_fn(XS, XNT1ALL[:, bass.ds(it * TOK, TOK)], ACT.Copy).then_inc(xs_ready, 1)
                for g in range(4):
                    for i, dst in enumerate((QT1, KT1)):
                        n = M_B["qk"] + 2 * g + i
                        act.wait_ge(m_full.sem(n), m_full.did(hm, n))
                        act_fn(dst[:, g, :], Mb[n % 2][:], ACT.Copy, scale=DK1 ** -0.5 if i == 0 else 1.0)\
                            .then_inc(m_free.sem(n), 1)
                attention(ATT1, ht, T_B["att"], hs, 0)
                for b in range(2):
                    n = T_B["ctx"] + b
                    act.wait_ge(t_full.sem(n), t_full.did(ht, n))
                    act_fn(CTXT[:, b, :], Tb[n % 2][:, 0:SEQ], ACT.Copy).then_inc(t_free.sem(n), 1)
            act.drain().then_inc(b_over, 1)
            act.wait_ge(b_over, ENGINES)

            def tiles(ht, n0):
                for b in range(2):
                    act.wait_ge(t_full.sem(n0 + b), t_full.did(ht, n0 + b))
                    act_fn(XGT[:, b * SEQ:(b + 1) * SEQ], Tb[(n0 + b) % 2][:, 0:SEQ], ACT.Copy)\
                        .then_inc(t_free.sem(n0 + b), 1)

            tiles(T_X0, 0)

            def turn(i, last_turn):
                ht, hm, ho = T_C0 + i * (T_C_USES // 2), M_C0 + i * 2, O_C0 + i * 2

                def silu(j):
                    act.wait_ge(m_full.sem(j), m_full.did(hm, j))
                    act.wait_ge(m_free.sem(j), m_free.reuse(hm, j))
                    act_fn(HS[:, j % 2, :], Mb[j % 2][:, 0:FE], ACT.Silu).then_inc(c_silu.sem(j), 1)

                def gate_t(j):
                    act.wait_ge(t_full.sem(j), t_full.did(ht, j))
                    act.wait_ge(pv_done.sem(j), pv_done.reuse(PV_C0 + i * 2, j))
                    act_fn(GTT[:, j % 2, :], Tb[j % 2][:, 0:FE], ACT.Copy).then_inc(t_free.sem(j), 1)

                silu(0)
                silu(1)
                gate_t(0)
                silu(2)
                gate_t(1)
                silu(3)
                gate_t(2)
                gate_t(3)
                if not last_turn:
                    tiles(ht, T_C["x"])

            with act.Fori(0, CT // CG - 1) as i:
                turn(i, False)
            turn(CT // CG - 1, True)
            for c in range(TURNS):
                act.wait_ge(moe_in, c + 1)
                act_fn(G3[:].rearrange("p t d -> p (t d)"), G2[:].rearrange("p t d -> p (t d)"), ACT.Silu)\
                    .then_inc(silu_done, 1)

        @block.vector
        def _(dve):
            V = nc.vector
            for events in (m_free, s_free, o_free, ss_done, rope_done, c_stats):
                events.begin(dve)
            steps = [0, 0]

            def settled():
                dve.sem_inc(dve_settled, 1)

            def step(instr, carry_wait=True):
                steps[1] += 1
                instr.then_inc(dstep, 1)
                dve.wait_ge(dstep, steps[0] + steps[1])
                if not carry_wait:
                    settled()

            def attention(g, hs, s0, ho, o0):
                units, w, dv = g["units"], g["dv"] + 1, g["dv"]
                for k in range(len(units) + 3):
                    done = None
                    if k >= 3:
                        o, _, ends = o_use(g, k - 3)
                        done = o0 + o if ends else None
                    if done is not None:
                        m = s0 + k - 3
                        dve.wait_ge(pv_done.sem(m), pv_done.did(hs, m))
                        ob = Ob[done % 2][:, 0:4 * w].rearrange("p (s w) -> p s w", w=w)
                        rc = RC[:, done % 2, :]
                        first = V.reciprocal(rc.unsqueeze(2), ob[:, :, dv:w])
                        if k >= len(units):
                            step(first)
                    if k < len(units):
                        b, qt, lane, slots = units[k]
                        n = s0 + k
                        dve.wait_ge(s_full.sem(n), s_full.did(hs, n))
                        keys, ns = P * (qt + 1), len(slots)
                        sc = Sb[n % 2][:].rearrange("p (s k) -> p s k", s=ns)
                        mx = MX[:, n % 2, 0:ns]
                        step(V.tensor_reduce(mx, sc, AX, ALU.max))
                        dve.wait_ge(exp_done.sem(n), exp_done.reuse(hs, n))
                        V.tensor_tensor(SE[:, n % 2, :].rearrange("p (s k) -> p s k", s=ns), sc,
                                        mx.unsqueeze(2).broadcast_to([P, ns, keys]), ALU.subtract)\
                            .then_inc(s_free.sem(n), 1)
                    if done is not None:
                        b, qt, lane, slots = units[k - 3]
                        dst = g["o"][:, 2 * b + qt, :].rearrange("p (s j d) -> p s j d", s=4, d=dv)[:, :, lane, :]
                        V.tensor_tensor(dst, ob[:, :, 0:dv], rc.unsqueeze(2).broadcast_to([P, 4, dv]), ALU.mult)\
                            .then_inc(o_free.sem(done), 1)

            def norm(dst, src, t):
                return V.tensor_scalar(dst, src, MV[:, t, 0:1], RS[:, t:t + 1], ALU.subtract, ALU.mult)

            V.memset(WYP[:], 0.0)
            V.memset(WQP[:], 0.0)
            V.memset(WKP[:], 0.0).then_inc(dve_consts, 1)
            V.memset(VA[:, :, :, DH:DH + 1], 1.0)
            V.memset(HT[64:P, :, 0:1], 0.0).then_inc(dve_consts, 1)
            dve.wait_ge(ld_a, LOADED_A)
            for l in range(LAYERS):
                for k in range(2):
                    V.tensor_tensor(RT[:, 2 * l + k].rearrange("p x t d -> p (x t) d"),
                                    ROPE[:, k].rearrange("p x t d -> p (x t) d"),
                                    QKS[:, l, k, :].unsqueeze(1).broadcast_to([P, 4, DH]), ALU.mult)
            V.tensor_scalar(bab[0:2 * NS, 3:4], bab[0:2 * NS, 0:1], -1.0, None, ALU.mult)
            V.tensor_tensor(ybrow[:, 0, :], ybrow[:, 0, :], ybrow[:, 1, :], ALU.add).then_inc(tables, 1)
            dve.wait_ge(tables, 1)
            dve.wait_ge(ld_x, 16)
            dve.wait_ge(ld_l1, 16 * 4)
            dve.wait_ge(pool_consts, POOL_CONSTS)

            with dve.Fori(0, TURNS) as it:
                hm = it * (M_A_USES // 2)
                ht = T_A0 + it * (T_A_USES // 2)
                hs, ho = it * (S_A_USES // 2), it * (O_A_USES // 2)
                steps[:] = [it * D_A_STEPS, 0]
                for t in range(GT):
                    last = V.bn_stats(ST[:, t, 0, :], XALL[:, it * GT + t, :])
                step(last, False)
                for t in range(GT):
                    last = V.bn_aggr(MV[:, t, :], ST[:, t, 0, :])
                last.then_inc(stats_done, 1)
                dve.wait_ge(rstd_done, it * 6 + 1)
                for t in range(GT):
                    last = norm(XC[:, t, :], XALL[:, it * GT + t, :], t)
                last.then_inc(xn_ready, 1)
                for l in range(LAYERS):
                    if l == 0:
                        dve.wait_ge(ea_done, it + 1)
                        r = slice(0, 2 * NS)
                        step(V.tensor_scalar(AA[r], EA[r], 1.0, None, ALU.add))
                        step(V.reciprocal(AA[r], AA[r]))
                        step(V.tensor_scalar(UU[r], AA[r], -1.0, 1.0, ALU.mult, ALU.add))
                        n = M_A["ab"]
                        V.scalar_tensor_tensor(UU[r], Mb[n % 2][r, SEQ:2 * SEQ], bab[r, 1:2], UU[r], ALU.add, ALU.mult)\
                            .then_inc(m_free.sem(n), 1)
                        dve.wait_ge(m_free.sem(n), m_free.did(hm, n))
                        step(V.tensor_tensor_scan(SC[r], AA[r], UU[r], 0.0, ALU.mult, ALU.add))
                        n = M_A["c"]
                        dve.wait_ge(m_free.sem(n), m_free.did(hm, n))
                        V.tensor_tensor(CS[r], TC[r], SC[r], ALU.mult).then_inc(cs_done, 1)
                    for n in range(9):
                        if n < 8:
                            t, i, m = n // 2, n % 2, 8 * l + n
                            u = M_A["qkv", l] + 3 * t + i
                            dve.wait_ge(sq_done.sem(m), sq_done.did(it * 8, m))
                            V.tensor_reduce(SS[:, m % 2, :], SQ[:, m % 2, :].rearrange("p (h d) -> p h d", h=8),
                                            AX, ALU.add).then_inc(ss_done.sem(m), 1)
                            src = Mb[u % 2][:].rearrange("p (h d) -> p h d", h=8)
                            dve.wait_ge(rope_done.sem(m), rope_done.reuse(it * 8, m))
                            for x, dst in enumerate((R1, R2)):
                                last = V.tensor_tensor(dst[:, m % 2, :].rearrange("p (h d) -> p h d", h=8), src,
                                                       RT[:, 2 * l + i, x, t % 2, :].unsqueeze(1)
                                                       .broadcast_to([P, 8, DH]), ALU.mult)
                            last.then_inc(m_free.sem(u), 1)
                        if n >= 1:
                            m = 8 * l + n - 1
                            dve.wait_ge(rope_sum.sem(m), rope_sum.did(it * 8, m))
                            w = T_A["qk", l] + n - 1
                            if n - 1 >= 2:
                                dve.wait_ge(t_full.sem(w), t_full.did(ht, w - 2))
                            V.tensor_tensor(RQ[:, m % 2, :].rearrange("p (h d) -> p h d", h=8),
                                            R1[:, m % 2, :].rearrange("p (h d) -> p h d", h=8),
                                            RN[:, m % 2, :].unsqueeze(2).broadcast_to([P, 8, DH]), ALU.mult)\
                                .then_inc(rope_done.sem(m), 1)
                    if l == 0:
                        n = M_A["y", 0]
                        dve.wait_ge(m_full.sem(n), m_full.did(hm, n))
                        V.tensor_tensor(S0, Mb[n % 2][:].rearrange("p (t d) -> p t d", t=GT),
                                        ybrow[:, 0, :].unsqueeze(1).broadcast_to([P, GT, D]), ALU.add)\
                            .then_inc(m_free.sem(n), 1)
                    attention(ATT0, hs, S_A[l], ho, O_A[l])
                    for b in range(2):
                        n = M_A["wo", l] + b
                        dve.wait_ge(m_full.sem(n), m_full.did(hm, n))
                        V.tensor_tensor(XC[:, 2 * b:2 * b + 2, :], XC[:, 2 * b:2 * b + 2, :],
                                        Mb[n % 2][:, 0:SEQ].rearrange("p (t d) -> p t d", t=2), ALU.add)\
                            .then_inc(m_free.sem(n), 1)
                    for b in range(2):
                        n = M_A["wo", l] + b
                        dve.wait_ge(m_free.sem(n), m_free.did(hm, n))
                        n = M_A["sh", l] + b
                        dve.wait_ge(m_full.sem(n), m_full.did(hm, n))
                        settled()
                        for t in range(2):
                            V.bn_stats(ST[:, 2 * b + t, 0, :], XC[:, 2 * b + t, 0:64])
                            last = V.bn_stats(ST[:, 2 * b + t, 1, :], Mb[n % 2][:, t * 64:(t + 1) * 64])
                        step(last, False)
                        for t in range(2):
                            last = V.bn_aggr(MV[:, 2 * b + t, :], ST[:, 2 * b + t].rearrange("p s c -> p (s c)"))
                        last.then_inc(stats_done, 1)
                    for b in range(2):
                        n = M_A["sh", l] + b
                        dve.wait_ge(rstd_done, it * 6 + 2 + 2 * l + b)
                        for t in range(2):
                            norm(HN[:, 2 * b + t, 0:64], XC[:, 2 * b + t, 0:64], 2 * b + t)
                            last = norm(HN[:, 2 * b + t, 64:D], Mb[n % 2][:, t * 64:(t + 1) * 64], 2 * b + t)
                        last.then_inc(m_free.sem(n), 1)
                    for c, (f, m) in enumerate(HC):
                        n = M_A["w1", l] + 2 * c + 1
                        dve.wait_ge(m_free.sem(n - 1), m_free.did(hm, n - 1))
                        dve.wait_ge(m_full.sem(n), m_full.did(hm, n))
                        V.scalar_tensor_tensor(HG[0:m, c, :], Mb[n % 2][0:m, :], b1c[0:m, l, 0, c:c + 1],
                                               GG[0:m, c % 2, :], ALU.add, ALU.mult).then_inc(m_free.sem(n), 1)
                    n = M_A["w2", l]
                    dve.wait_ge(m_full.sem(n), m_full.did(hm, n))
                    V.tensor_tensor(XC, XC, Mb[n % 2][:].rearrange("p (t d) -> p t d", t=GT), ALU.add)\
                        .then_inc(m_free.sem(n), 1)
                    dve.wait_ge(m_free.sem(n), m_free.did(hm, n))
                    V.tensor_tensor(XC, XC, b2row[:, l, :].unsqueeze(1).broadcast_to([P, GT, D]), ALU.add)\
                        .then_inc(ffn_added, 1)
                dve.wait_ge(eg_done, it + 1)
                step(V.tensor_scalar(EG, EG, 1.0, None, ALU.add))
                step(V.reciprocal(EG, EG))
                step(V.tensor_tensor(EG, EG, XC, ALU.mult))
                step(V.tensor_tensor(EG, EG, S0, ALU.mult))
                xt = XALL[:, bass.ds(it * GT, GT), :]
                step(V.tensor_tensor(xt, xt, EG, ALU.add), False)
                for t in range(GT):
                    last = V.bn_stats(ST[:, t, 0, :], XALL[:, it * GT + t, :])
                step(last, False)
                for t in range(GT):
                    last = V.bn_aggr(MV[:, t, :], ST[:, t, 0, :])
                last.then_inc(stats_done, 1)
                dve.wait_ge(rstd_done, it * 6 + 6)
                for t in range(GT):
                    last = norm(HN[:, t, :], XALL[:, it * GT + t, :], t)
                last.then_inc(xn1_ready, 1)
                n = M_A["router"]
                dve.wait_ge(m_full.sem(n), m_full.did(hm, n))
                V.tensor_tensor(LG[:, bass.ds(it * GT, GT), :], Mb[n % 2][:, 0:GT * E].rearrange("p (t e) -> p t e", t=GT),
                                rbrow[:].unsqueeze(1).broadcast_to([P, GT, E]), ALU.add).then_inc(m_free.sem(n), 1)
                dve.wait_ge(m_free.sem(n), m_free.did(hm, n))
                assert steps[1] == D_A_STEPS, steps[1]
            dve.drain().then_inc(a_over, 1)
            dve.wait_ge(a_over, ENGINES)

            steps[:] = [TURNS * D_A_STEPS, 0]
            dve.wait_ge(iotas, 3)
            V.memset(VA1[:, :, :, DK1:DK1 + 1], 1.0)
            V.memset(KEEP, 1.0)
            for t in range(NT):
                last = V.max(MAXV[:, t, :], LG[:, t, :])
            step(last)
            for t in range(NT):
                last = V.max_index(MIDX[:, t, :].bitcast(U32), MAXV[:, t, :], LG[:, t, :])
            step(last)
            V.memset(KEEP[:, :, 0:1], 0.0)
            V.tensor_tensor(GW[:, 1, :], MAXV[:, :, 1], MAXV[:, :, 0], ALU.subtract).then_inc(gap_done, 1)
            step(V.tensor_copy(MIF.rearrange("p k t -> p t k"), MIDX[:, :, 0:2].bitcast(U32)))
            for k in range(2):
                last = V.tensor_tensor(ONEH[:, k], IOT.rearrange("p e t -> p t e"),
                                       MIF[:, k, :].unsqueeze(2).broadcast_to([P, NT, E]), ALU.is_equal)
            step(last)
            V.tensor_tensor(ONEH_B.rearrange("p (t e) -> p t e", t=NT), ONEH[:, 0], ONEH[:, 1], ALU.add)\
                .then_inc(onehot, 1)
            dve.wait_ge(gap_exp, 1)
            step(V.tensor_scalar(GW[:, 1, :], GW[:, 0, :], 1.0, None, ALU.add))
            step(V.reciprocal(WGT[:, 0, :], GW[:, 1, :]))
            V.tensor_tensor(WGT[:, 1, :], WGT[:, 0, :], GW[:, 0, :], ALU.mult)
            dve.wait_ge(m_full.sem(0), m_full.did(M_W0, 0))
            V.tensor_copy(CNT[:, 0].rearrange("p t e -> p (t e)"), Mb[0][:, 0:NT * E]).then_inc(m_free.sem(0), 1)
            dve.wait_ge(m_full.sem(1), m_full.did(M_W0, 1))
            V.tensor_copy(CNT[:, 1].rearrange("p t e -> p (t e)"), Mb[1][:, 0:NT * E]).then_inc(m_free.sem(1), 1)
            dve.wait_ge(m_free.sem(0), m_free.did(M_W0, 0))
            dve.wait_ge(m_free.sem(1), m_free.did(M_W0, 1))
            step(V.tensor_copy(CUM[:, 0], CNT[:, 1].rearrange("p t e -> p e t")))
            step(V.tensor_tensor_scan(CUM[:, 1].rearrange("p e t -> p (e t)"), KEEP.rearrange("p e t -> p (e t)"),
                                      CUM[:, 0].rearrange("p e t -> p (e t)"), 0.0, ALU.mult, ALU.add))
            step(V.tensor_tensor(CNT[:, 1], CUM[:, 1, :, NT - 1].unsqueeze(2).broadcast_to([P, E, NT]),
                                 IOTS[:], ALU.is_gt))
            step(V.tensor_reduce(NTI[:, 0, :], CNT[:, 1], AX, ALU.add))
            step(V.memset(NTI[:, 3, :], 1.0))
            step(V.tensor_tensor_scan(NTI[:, 1, :], NTI[:, 3, :], NTI[:, 0, :], 0.0, ALU.mult, ALU.add))
            step(V.tensor_tensor(NTI[:, 2, :], NTI[:, 1, :], NTI[:, 0, :], ALU.subtract))
            step(V.tensor_tensor(ENDS, NTI[:, 1, :].unsqueeze(1).broadcast_to([P, CT, E]), IOTJ, ALU.is_le))
            step(V.tensor_reduce(EF, ENDS, AX, ALU.add))
            step(V.tensor_scalar(EF, EF, float(E - 1), None, ALU.min))
            step(V.tensor_copy(EID[:], EF))
            step(V.tensor_tensor(CUM[:, 1], CUM[:, 1], CUM[:, 0], ALU.subtract))
            step(V.tensor_tensor(CNT[:, 0], CNT[:, 0], CUM[:, 1].rearrange("p e t -> p t e"), ALU.add))
            step(V.scalar_tensor_tensor(CNT[:, 0], NTI[:, 2, :].unsqueeze(1).broadcast_to([P, NT, E]), float(P),
                                        CNT[:, 0], ALU.mult, ALU.add))
            for k in range(2):
                step(V.tensor_tensor(ONEH[:, k], ONEH[:, k], CNT[:, 0], ALU.mult))
                step(V.tensor_reduce(PF[:, k, :], ONEH[:, k], AX, ALU.add))
            V.tensor_copy(POSU[:], PF).then_inc(pos_done, 1)
            routing_steps = steps[1]

            b0 = TURNS * D_A_STEPS + routing_steps
            with dve.Fori(0, TURNS) as it:
                hm = M_B0 + it * (M_B_USES // 2)
                hs, ho = S_B0 + it * (S_B_USES // 2), O_B0 + it * (O_B_USES // 2)
                steps[:] = [b0 + it * D_B_STEPS, 0]
                for b in range(2):
                    n = M_B["v"] + b
                    dve.wait_ge(m_full.sem(n), m_full.did(hm, n))
                    V.tensor_copy(VA1[:, 2 * b:2 * b + 2, :, 0:DK1],
                                  Mb[n % 2][:, 0:SEQ].rearrange("p (t h d) -> p t h d", t=2, h=E)).then_inc(m_free.sem(n), 1)
                attention(ATT1, hs, 0, ho, 0)
                for b in range(2):
                    n = M_B["out"] + b
                    dve.wait_ge(m_full.sem(n), m_full.did(hm, n))
                    V.tensor_tensor(S1ALL[:, bass.ds(it * GT + 2 * b, 2), :],
                                    Mb[n % 2][:, 0:SEQ].rearrange("p (t d) -> p t d", t=2),
                                    borow[:].unsqueeze(1).broadcast_to([P, 2, D]), ALU.add).then_inc(m_free.sem(n), 1)
                assert steps[1] == D_B_STEPS, steps[1]
            dve.drain().then_inc(b_over, 1)
            dve.wait_ge(b_over, ENGINES)

            c0 = b0 + TURNS * D_B_STEPS

            def turn(i):
                ht, hm, ho = T_C0 + i * (T_C_USES // 2), M_C0 + i * 2, O_C0 + i * 2
                hp = PV_C0 + i * 2
                steps[:] = [c0 + i * D_C_STEPS, 0]
                for k in range(CG + 3):
                    if k < CG:
                        dve.wait_ge(c_silu.sem(k), c_silu.did(i * 2, k))
                        if k >= 2:
                            dve.wait_ge(t_full.sem(k), t_full.did(ht, k - 2))
                        V.tensor_tensor(GS[:, k % 2, :], HS[:, k % 2, :], Mb[k % 2][:, FE:2 * FE], ALU.mult)\
                            .then_inc(m_free.sem(k), 1)
                    if 2 <= k < CG + 2:
                        j = k - 2
                        dve.wait_ge(pv_done.sem(j), pv_done.did(hp, j))
                        settled()
                        step(V.bn_stats(ST[:, j, 0, :], Ob[j % 2][:, 0:D]), False)
                        V.bn_aggr(MV[:, j, :], ST[:, j, 0, :]).then_inc(c_stats.sem(j), 1)
                    if k >= 3:
                        j = k - 3
                        dve.wait_ge(c_rstd.sem(j), c_rstd.did(i * 2, j))
                        dve.wait_ge(c_yo.sem(j), c_yo.reuse(i * 2, j))
                        norm(YN[:, j % 2, :], Ob[j % 2][:, 0:D], j).then_inc(o_free.sem(j), 1)
                assert steps[1] == D_C_STEPS, steps[1]

            with dve.Fori(0, CT // CG - 1) as i:
                turn(i)
            turn(CT // CG - 1)
            steps[:] = [c0 + CT // CG * D_C_STEPS, 0]
            for c in range(TURNS):
                dve.wait_ge(gathered[c], 16 * 2 * GT)
                ts = slice(c * GT, c * GT + GT)
                if c:
                    dve.wait_ge(silu_done, c)
                if c >= 2:
                    dve.wait_ge(st_out.sem(c), 16)
                ob = OUTB[:, c % 2, :].rearrange("p (t d) -> p t d", t=GT)
                V.tensor_tensor(G2, YAB[:, ts, 0, :], WGT[:, 0, ts].unsqueeze(2).broadcast_to([P, GT, D]), ALU.mult)
                step(V.tensor_tensor(ob, YAB[:, ts, 1, :], WGT[:, 1, ts].unsqueeze(2).broadcast_to([P, GT, D]),
                                     ALU.mult))
                V.tensor_tensor(G2, G2, ob, ALU.add).then_inc(moe_in, 1)
                dve.wait_ge(silu_done, c + 1)
                step(V.tensor_tensor(ob, G3, S1ALL[:, ts, :], ALU.mult))
                V.tensor_tensor(ob, ob, XALL[:, ts, :], ALU.add).then_inc(out_ready, 1)

        @block.gpsimd
        def _(pool):
            G = nc.gpsimd
            for events in (rope_sum, c_yo, c_rstd):
                events.begin(pool)
            pool.sem_inc(xn1_kept, 1)
            steps = [0, 0]

            def settled():
                pool.sem_inc(pool_settled, 1)

            def step(instr):
                steps[1] += 1
                instr.then_inc(pstep, 1)
                pool.wait_ge(pstep, steps[0] + steps[1])

            for v, c in ((ident, 0.0), (identb, 0.0), (shift, 0.0), (carry, 0.0), (trib, 1.0), (onesb, 1.0),
                         (powm, -0.5), (zeros, 0.0), (mask0[0], 0.0), (mask1[0], 0.0), (mask0[1], 0.0),
                         (mask1[1], 0.0)):
                G.memset(v[:], c).then_inc(pool_consts, 1)
            pool.wait_ge(pool_consts, 12)
            one = dict(compare_op=ALU.not_equal, fill=1.0, channel_multiplier=1)
            for v, base in ((ident, 0), (identb, 0), (shift, 1), (carry, -(P - 1))):
                G.affine_select(out=v[:], in_=v[:], base=base, pattern=[[-1, P]], **one).then_inc(pool_consts, 1)
            G.affine_select(out=trib[:], in_=trib[:], compare_op=ALU.is_gt, fill=0.0, base=0, pattern=[[1, P]],
                            channel_multiplier=-1).then_inc(pool_consts, 1)
            for qt in range(2):
                keys = P * (qt + 1)
                for m in ((mask0, mask1)[qt][0], (mask0, mask1)[qt][1]):
                    G.affine_select(out=m[:], in_=m[:], compare_op=ALU.is_ge, fill=MASKED, base=qt * P,
                                    pattern=[[0, 512 // keys], [-1, keys]], channel_multiplier=1)\
                        .then_inc(pool_consts, 1)
            pool.wait_ge(pool_consts, 12 + 5 + 4)
            for qt in range(2):
                keys = P * (qt + 1)
                m = (mask0, mask1)[qt][0]
                G.affine_select(out=m[:], in_=m[:], compare_op=ALU.is_ge, fill=MASKED, base=64 - qt * P,
                                pattern=[[0, 512 // keys], [1, keys]], channel_multiplier=-1)\
                    .then_inc(pool_consts, 1)
            pool.wait_ge(pool_consts, POOL_CONSTS)

            def rstd(o, var):
                n = var.shape[1]
                step(G.tensor_scalar(o, var, EPS, None, ALU.add))
                return G.tensor_tensor(o, o, powm[:, 0:n], ALU.pow)

            with pool.Fori(0, TURNS) as it:
                steps[:] = [it * P_A_STEPS, 0]
                ht = T_A0 + it * (T_A_USES // 2)
                hm = it * (M_A_USES // 2)
                pool.wait_ge(stats_done, it * 6 + 1)
                settled()
                rstd(RS[:], MV[:, :, 1]).then_inc(rstd_done, 1)
                for l in range(LAYERS):
                    for n in range(8):
                        m, u = 8 * l + n, M_A["qkv", l] + 3 * (n // 2) + n % 2
                        pool.wait_ge(ss_done.sem(m), ss_done.did(it * 8, m))
                        pool.wait_ge(rope_done.sem(m), rope_done.reuse(it * 8, m))
                        settled()
                        step(G.tensor_scalar(RN[:, m % 2, :], SS[:, m % 2, :], 1e-24, None, ALU.max))
                        G.tensor_tensor(RN[:, m % 2, :], RN[:, m % 2, :], powm[:, 0:8], ALU.pow)
                        pool.wait_ge(m_free.sem(u), m_free.did(hm, u))
                        r1, r2 = (r[:, m % 2, :].rearrange("p (h s d) -> p h s d", h=8, s=2) for r in (R1, R2))
                        G.tensor_tensor(r1, r1, r2[:, :, ::-1, :], ALU.add).then_inc(rope_sum.sem(m), 1)
                    for b in range(2):
                        pool.wait_ge(stats_done, it * 6 + 2 + 2 * l + b)
                        settled()
                        rstd(RS[:, 2 * b:2 * b + 2], MV[:, 2 * b:2 * b + 2, 1]).then_inc(rstd_done, 1)
                pool.wait_ge(stats_done, it * 6 + 6)
                settled()
                rstd(RS[:], MV[:, :, 1]).then_inc(rstd_done, 1)
                pool.wait_ge(xn1_ready, it + 1)
                G.tensor_copy(XN1ALL[:, bass.ds(it * GT, GT), :], HN)
                for b in range(2):
                    n = T_A["x1"] + b
                    pool.wait_ge(t_free.sem(n), t_free.did(ht, n))
                G.tensor_copy(XNT1ALL[:, bass.ds(it * TOK, TOK)], XNT).then_inc(xn1_kept, 1)
                assert steps[1] == P_A_STEPS, steps[1]
            pool.drain().then_inc(a_over, 1)
            pool.wait_ge(a_over, ENGINES)
            step_c0 = TURNS * P_A_STEPS

            G.iota(IOTI.rearrange("p (e t) -> p e t", e=E), [[1, E], [0, NT]], base=0, channel_multiplier=0)\
                .then_inc(iota_raw, 1)
            G.iota(IOTI2.rearrange("p (e t) -> p e t", e=E), [[0, E], [P, NT]], base=0, channel_multiplier=0)\
                .then_inc(iota_raw, 1)
            G.iota(IOTI3.rearrange("p (j e) -> p j e", e=E), [[1, CT], [0, E]], base=0, channel_multiplier=0)\
                .then_inc(iota_raw, 1)
            pool.wait_ge(iota_raw, 3)
            G.tensor_copy(IOT.rearrange("p e t -> p (e t)"), IOTI).then_inc(iotas, 1)
            G.tensor_copy(IOTS.rearrange("p e t -> p (e t)"), IOTI2).then_inc(iotas, 1)
            G.tensor_copy(IOTJ.rearrange("p j e -> p (j e)"), IOTI3).then_inc(iotas, 1)
            pool.wait_ge(zeroed, 16 * CT // 4)
            pool.wait_ge(pos_done, 1)
            for t in range(NT):
                for k in range(2):
                    G.indirect_dma_start(XG, bass.IndirectOffsetOnAxis(POSU[:, k, t:t + 1], 0), XN1ALL[:, t, :], None)\
                        .then_inc(scattered, 16)
            pool.drain().then_inc(b_over, 1)
            pool.wait_ge(b_over, ENGINES)

            def turn(i):
                steps[:] = [step_c0 + i * P_C_STEPS, 0]
                for k in range(CG + 1):
                    if k < CG:
                        pool.wait_ge(c_stats.sem(k), c_stats.did(i * 2, k))
                        settled()
                        rstd(RS[:, k:k + 1], MV[:, k, 1:2]).then_inc(c_rstd.sem(k), 1)
                    if k >= 1:
                        j = k - 1
                        e = pool.value_load(EID[0:1, bass.ds(i * CG + j, 1)], min_val=0, max_val=E - 1)
                        pool.wait_ge(o_free.sem(j), o_free.did(O_C0 + i * 2, j))
                        pool.wait_ge(st_y.sem(j), st_y.reuse(i * 2, j) * 16)
                        step(G.tensor_tensor(YO[:, j % 2, :], YN[:, j % 2, :], GB[:, e, :], ALU.mult))
                        G.tensor_tensor(YO[:, j % 2, :], YO[:, j % 2, :], BB[:, e, :], ALU.add)\
                            .then_inc(c_yo.sem(j), 1)
                assert steps[1] == P_C_STEPS, steps[1]

            with pool.Fori(0, CT // CG - 1) as i:
                turn(i)
            turn(CT // CG - 1)
            for p in range(2):
                pool.wait_ge(st_y.sem(p), 16 * (CT // 2 + 1))
            for t in range(NT):
                for k in range(2):
                    G.indirect_dma_start(YAB[:, t, k, :], None, YG, bass.IndirectOffsetOnAxis(POSU[:, k, t:t + 1], 0))\
                        .then_inc(gathered[t // GT], 16)


def rope_tables():
    import numpy as np
    n, window = SEQ, 64
    half = np.arange(0, DH, 2, dtype=np.float32)
    inv = (np.float32(1.0) / np.float32(10000.0) ** (half / np.float32(DH))).astype(np.float32)
    t = np.arange(n, dtype=np.float32)
    freqs = (t[:, None] * inv[None, :]).astype(np.float32).astype(np.float64)
    base = ((half + np.float32(0.4 * DH)) / np.float32(1.4 * DH)).astype(np.float64)
    power = (t - n // 2).astype(np.float64) / float(window // 2)
    scale = base[None, :] ** power[:, None]
    cos, sin = np.cos(freqs), np.sin(freqs)
    tab = np.zeros((2, 2, n, DH), np.float64)
    for i, s in enumerate((8.0 * scale, 1.0 / scale)):
        tab[i, 0] = np.concatenate([cos * s, cos * s], -1)
        tab[i, 1] = np.concatenate([sin * s, -sin * s], -1)
    return tab.astype(np.float32)


NAMES = [f"L0_attn_{n}" for n in ("x", "Wa", "ba", "Wb", "bb", "Wc", "bc", "Wd", "bd", "Wy", "by")] + \
        [f"L0_ffn_{n}" for n in ("wqkv", "q_scale", "k_scale", "wo", "ln_g", "ln_b", "w1", "b1", "w2", "b2")] + \
        [f"L1_attn_{n}" for n in ("Wq", "Wk", "Wv", "Wo", "bo")] + \
        [f"L1_ffn_{n}" for n in ("router_w", "router_b", "w1", "w2", "w3", "ln_g", "ln_b")]


def kernel(**inputs):
    import numpy as np
    import concourse.bacc as bacc
    from concourse.bass_utils import run_bass_kernel_spmd

    nc = bacc.Bacc("TRN2", target_bir_lowering=False, num_devices=1)
    arrays = {f"in_{n}": np.ascontiguousarray(inputs[n]) for n in NAMES}
    arrays["in_rope"] = rope_tables()
    ins = {n[3:]: nc.dram_tensor(n, a.shape, mybir.dt.from_np(a.dtype), kind="ExternalInput").ap()
           for n, a in arrays.items()}
    out = nc.dram_tensor("out", (NB, SEQ, D), F32, kind="ExternalOutput").ap()
    gated_layers(nc, ins, out)
    return run_bass_kernel_spmd(nc, [arrays], core_ids=[0]).results[0]["out"]
```

```python
from contextlib import ExitStack

import concourse.bass as bass
from concourse import mybir

F32 = mybir.dt.float32
BF16 = mybir.dt.bfloat16
U32 = mybir.dt.uint32
I32 = mybir.dt.int32
ALU = mybir.AluOpType
ACT = mybir.ActivationFunctionType
AX = mybir.AxisListType.X

P = 128
D = 128
NB, SEQ = 8, 256
NT = NB * SEQ // P
GT = 4
TURNS = NT // GT
TOK = GT * P
NS = 32
LAYERS = 2
INNER, DH = 512, 64
HID = 341
HC = [(0, 128), (128, 128), (256, 85)]
E, FE = 16, 256
DK1 = 8
CT = 48
CG = 4
EPS = 1e-5
MASKED = -1e30


class Pair:

    def __init__(self, ctx, nc, name):
        self.sems = [ctx.enter_context(nc.semaphore(f"{name}{i}")) for i in range(2)]

    def sem(self, n):
        return self.sems[n % 2]

    def begin(self, eng, by=1):
        for s in self.sems:
            eng.sem_inc(s, by)

    def did(self, half, n):
        return half + (n // 2 + 2)

    def reuse(self, half, n):
        return half + (n // 2 + 1)


def latest(*events):
    return sorted({n % 2: n for n in sorted(events)}.values())


def places(*stages):
    at, first = 0, {}
    for name, uses in stages:
        first[name] = at
        at += uses
    assert at % 2 == 0
    return first, at



UNITS = 6


def qkv_steps(l, b):
    steps = []
    for j in range(7):
        step = []
        if j < 4:
            step.append(("qk", l, 4 * b + j))
            if j % 2:
                step.append(("v", l, 2 * b + j // 2))
        if 0 <= j - 2 < 4:
            step.append(("scale", l, 4 * b + j - 2))
        if j >= 3:
            step.append(("qkT", l, 4 * b + j - 3))
        steps.append(step)
    return steps


def attention_steps(l, b):
    steps = []
    for k in range(UNITS + 4):
        step = []
        for kind, j in (("T", k - 2), ("V", k - 3), ("O", k - 4), ("S", k)):
            if 0 <= j < UNITS:
                step.append((kind, l, b, j))
        steps.append(step)
    return steps


def ffn_steps(l, b):
    steps = [[("oT", l, 2 * b)], [("oT", l, 2 * b + 1)], [("wo", l, b)], [("res", l, b)], [("sh", l, b)],
             [("nh", l, b)], [("hT", l, b)]]
    return steps + [[("w1", l, b, c)] for c in range(3)] + [[("w2", l, b)]]


def merged(*streams):
    spots = [((i + 0.5) / len(s), j, step) for j, s in enumerate(streams) for i, step in enumerate(s)]
    return [item for _, _, step in sorted(spots, key=lambda s: s[:2]) for item in step]


def turn_order():
    order = [("st0", 0), ("st0", 1), ("nm0", 0), ("x", 0, 0), ("nm0", 1), ("x", 0, 1)]
    order += merged(qkv_steps(0, 0), [[("ab",)], [("c",)], [("scan",)]])
    order += merged(attention_steps(0, 0), qkv_steps(0, 1))
    order += merged(attention_steps(0, 1), ffn_steps(0, 0), [[("y",)]])
    order += [("x", 1, 0)]
    order += merged(qkv_steps(1, 0), ffn_steps(0, 1))
    order += [("x", 1, 1)]
    order += merged(attention_steps(1, 0), qkv_steps(1, 1))
    order += merged(attention_steps(1, 1), ffn_steps(1, 0))
    order += merged(ffn_steps(1, 1), [[("gate", 0)], [("nm1", 0)], [("x1T", 0)]])
    order += [("gate", 1), ("nm1", 1), ("x1T", 1), ("router",)]
    return order


def numbered(kinds):
    items = [i for i in ORDER if i[0] in kinds]
    return {i: n for n, i in enumerate(items)}, len(items)


ORDER = turn_order()
T_A, T_A_USES = numbered(("x", "qkT", "T", "oT", "hT", "x1T"))
M_A, M_A_USES = numbered(("ab", "c", "y", "qk", "v", "wo", "sh", "w1", "w2", "router"))
S_A, S_A_USES = numbered(("S",))
O_A_USES = 16
QK, QK_EVENTS = numbered(("qk",))
STATS, STATS_EVENTS = numbered(("st0", "sh", "gate"))
GELUS, GELU_EVENTS = numbered(("w1",))
FFNS, FFN_EVENTS = numbered(("w2",))
assert (T_A_USES | M_A_USES | S_A_USES) % 2 == 0
T_P_USES = 2
T_W_USES = 2 * E
M_W_USES = 2
T_B, T_B_USES = places(("att", 24), ("ctx", 2))
M_B, M_B_USES = places(("q", 1), ("k", 1), ("v", 2), ("out", 2))
S_B_USES, O_B_USES = 24, 16
T_C, T_C_USES = places(("g", 4), ("x", 2))
M_C_USES = O_C_USES = CG
T_A0 = T_P_USES // 2
T_W0 = T_A0 + TURNS * T_A_USES // 2
T_B0 = T_W0 + T_W_USES // 2
T_X0 = T_B0 + TURNS * T_B_USES // 2
T_C0 = T_X0 + 1
M_W0 = TURNS * M_A_USES // 2
M_B0 = M_W0 + M_W_USES // 2
M_C0 = M_B0 + TURNS * M_B_USES // 2
S_B0 = TURNS * S_A_USES // 2
O_B0 = TURNS * O_A_USES // 2
O_C0 = O_B0 + TURNS * O_B_USES // 2
PV_C0 = S_B0 + TURNS * S_B_USES // 2
D_A_STEPS, D_B_STEPS, D_C_STEPS, P_A_STEPS, P_C_STEPS = 56, 40, 4, 24, 8


def gated_layers(nc, ins, out):
    ctx = ExitStack()
    with ctx:
        def sb(name, shape, dt=F32):
            return ctx.enter_context(nc.sbuf_tensor(name, shape, dt))

        def sem(name):
            return ctx.enter_context(nc.semaphore(name))

        def pair(name):
            return Pair(ctx, nc, name)

        Tb, Mb, Sb, Ob = ([ctx.enter_context(nc.psum_tensor(f"ps{n}{i}", [P, 512], F32)) for i in range(2)]
                          for n in "TMSO")
        t_full, t_free = pair("t_full"), pair("t_free")
        m_full, m_free = pair("m_full"), pair("m_free")
        s_full, s_free = pair("s_full"), pair("s_free")
        o_free = pair("o_free")
        exp_done = pair("exp_done")
        sq_done, ss_done = pair("sq_done"), pair("ss_done")
        rope_sum, rope_done = pair("rope_sum"), pair("rope_done")

        XG = nc.dram_tensor("xg_scratch", (CT * P, D), F32, kind="Internal").ap()
        YG = nc.dram_tensor("yg_scratch", (CT * P, D), F32, kind="Internal").ap()

        XALL = sb("XALL", [P, NT, D])
        XN1ALL = sb("XN1ALL", [P, NT, D])
        XNT1ALL = sb("XNT1ALL", [P, NT * P])
        S1ALL = sb("S1ALL", [P, NT, D])
        LG = sb("LG", [P, NT, E])
        ident = sb("ident", [P, P])
        identb = sb("identb", [P, P], BF16)
        mask0 = {0: sb("maskl0", [P, 512], BF16), 1: sb("maskc0", [P, 512], BF16)}
        mask1 = {0: sb("maskl1", [P, 512], BF16), 1: sb("maskc1", [P, 512], BF16)}
        shift = sb("shift", [P, P])
        carry = sb("carry", [P, P])
        trib = sb("trib", [P, P], BF16)
        onesb = sb("onesb", [P, P], BF16)
        powm = sb("powm", [P, 16])
        zeros = sb("zeros", [P, 512])
        SE = sb("SE", [P, 2, 512])
        PR = sb("PR", [P, 2, 512])
        PT = sb("PT", [P, 2, 512])
        MX = sb("MX", [P, 2, 4])
        RC = sb("RC", [P, 2, 4])
        ST = sb("ST", [P, GT, 2, 6])
        MV = sb("MV", [P, GT, 2])
        RS = sb("RS", [P, GT])
        WQT = sb("WQT", [P, P])
        WKT = sb("WKT", [P, P])
        headm = sb("headm", [P, E])
        WVT = sb("WVT", [P, P])
        WOT = sb("WOT", [P, P])
        RWT = sb("RWT", [P, E])
        borow = sb("borow", [P, D])
        rbrow = sb("rbrow", [P, E])
        GB = sb("GB", [P, E, D])
        BB = sb("BB", [P, E, D])

        ARENA = 32784
        arena = sb("arena", [P, ARENA])
        at = [0]

        def carve(*shape):
            n = 1
            for s in shape:
                n *= s
            v = arena[:, at[0]:at[0] + n]
            at[0] += n
            assert at[0] <= ARENA, at[0]
            if len(shape) == 1:
                return v
            names = "abcd"[:len(shape)]
            return v.rearrange(f"p ({' '.join(names)}) -> p {' '.join(names)}",
                               **{c: s for c, s in zip(names[1:], shape[1:])})

        S0 = carve(GT, D)
        XC = carve(GT, D)
        XNT = carve(TOK)
        HT = carve(2, SEQ)
        VA = carve(GT, 8, DH + 1)
        QT = carve(2, 4, TOK)
        KT = carve(4, TOK)
        SQ = carve(2, 512)
        R1 = carve(4, 512)
        R2 = carve(2, 512)
        SS = carve(4, 8)
        RN = carve(4, 8)
        OS = carve(GT, 512)
        OT = carve(2, 512)
        HN = carve(GT, D)
        HNT = carve(TOK)
        GG = carve(2, SEQ)
        HG = carve(3, 512)
        EG = carve(GT, D)
        EA = carve(SEQ)
        AA = carve(SEQ)
        UU = carve(SEQ)
        SC = carve(SEQ)
        TC = carve(SEQ)
        CS = carve(SEQ)
        WABC = carve(3, NS)
        WD = carve(D)
        WYP = carve(2, D)
        ybrow = carve(2, D)
        bab = carve(4)
        WQKV = carve(LAYERS, 3, INNER)
        WO = carve(LAYERS, 4, D)
        W1 = carve(LAYERS, 2 * HID)
        W2 = carve(LAYERS, 3, D)
        lgc = carve(LAYERS, 2)
        b1c = carve(LAYERS, 2, 3)
        b2row = carve(LAYERS, D)
        ROPE = carve(2, 2, 2, DH)
        QKS = carve(LAYERS, 2, DH)
        RT = carve(LAYERS * 2, 2, 2, DH)
        WRAW = carve(5, P)
        at[0] = 0
        W13 = carve(E, 2 * FE)
        W2T = carve(E, 2 * D)
        after_weights = at[0]
        WST = carve(2, 3, 2 * D)
        XQ = carve(TOK)
        QT1 = carve(E, TOK)
        KT1 = carve(TOK)
        VA1 = carve(GT, E, DK1 + 1)
        XS = carve(TOK)
        CTX = carve(GT, D)
        CTXT = carve(2, SEQ)
        MAXV = carve(NT, 8)
        ONEH = carve(2, NT, E)
        MIDX = carve(NT, 8)
        MIF = carve(2, NT)
        GW = carve(2, NT)
        CNT = carve(2, NT, E)
        CUM = carve(2, E, NT)
        IOT = carve(E, NT)
        IOTS = carve(E, NT)
        IOTJ = carve(CT, E)
        KEEP = carve(E, NT)
        NTI = carve(4, E)
        PF = carve(2, NT)
        ENDS = carve(CT, E)
        IOTI, IOTI2, IOTI3 = (carve(n).bitcast(I32) for n in (E * NT, E * NT, CT * E))
        EF = carve(CT)
        MB = carve(128)
        POSU = sb("POSU", [P, 2, NT], U32)
        EID = sb("EID", [P, CT], I32)
        WGT = sb("WGT", [P, 2, NT])
        ONEH_B = MB.bitcast(BF16)
        at[0] = after_weights
        XGS = carve(CG, D)
        XGT = carve(TOK)
        HS = carve(2, FE)
        GS = carve(2, FE)
        GTT = carve(2, FE)
        YN = carve(2, D)
        YO = carve(2, D)
        YAB = carve(NT, 2, D)
        G2 = carve(GT, D)
        G3 = carve(GT, D)
        OUTB = carve(2, TOK)

        ld_x, ld_a, ld_l1, ld_raw = sem("ld_x"), sem("ld_a"), sem("ld_l1"), sem("ld_raw")
        ld_w = pair("ld_w")
        zeroed, scattered = sem("zeroed"), sem("scattered")
        gathered = [sem(f"gathered{c}") for c in range(TURNS)]
        ld_g, st_y, st_out = sem("ld_g"), pair("st_y"), pair("st_out")
        pool_consts, dve_consts, tables = sem("pool_consts"), sem("dve_consts"), sem("tables")
        a_over, b_over = sem("a_over"), sem("b_over")
        dve_settled, pool_settled = sem("dve_settled"), sem("pool_settled")
        dstep, pstep = sem("dstep"), sem("pstep")
        stats_done, rstd_done = sem("stats_done"), sem("rstd_done")
        xn_ready, ea_done, cs_done = sem("xn_ready"), sem("ea_done"), sem("cs_done")
        ffn_added, gate_done = sem("ffn_added"), sem("gate_done")
        xn1_ready, xn1_kept, gelu_done = sem("xn1_ready"), sem("xn1_kept"), sem("gelu_done")
        onehot, gap_done, gap_exp = sem("onehot"), sem("gap_done"), sem("gap_exp")
        pos_done, xs_ready = sem("pos_done"), sem("xs_ready")
        c_silu, c_yo, c_stats, c_rstd = pair("c_silu"), pair("c_yo"), pair("c_stats"), pair("c_rstd")
        pv_done, iota_raw, iotas = pair("pv_done"), sem("iota_raw"), sem("iotas")
        moe_in, silu_done, out_ready = sem("moe_in"), sem("silu_done"), sem("out_ready")
        q_masked = sem("q_masked")

        def masked(it, b, n):
            return it * (2 * E) + (b * E + n + 1)

        ENGINES = 4

        XG3 = XG.rearrange("(j p) d -> j p d", p=P)
        YG3 = YG.rearrange("(j p) d -> j p d", p=P)

        def stage(lanes, dv, q, k, v, o, masks):
            units = []
            for b in range(2):
                for lane in range(lanes):
                    units.append((b, 0, lane, range(4)))
                for lane in range(lanes):
                    for h in range(2):
                        units.append((b, 1, lane, range(2 * h, 2 * h + 2)))
            return dict(lanes=lanes, dv=dv, q=q, k=k, v=v, o=o, masks=masks, units=units)

        ATT0 = stage(2, DH, lambda lane, s: QT[:, lane, s, :], lambda s: KT[:, s, :], VA, OS, (mask0[0], mask1[0]))
        ATT1 = stage(4, DK1, lambda lane, s: QT1[:, 4 * s + lane, :], lambda s: KT1, VA1, CTX, (mask0[1], mask1[1]))

        def unit_of(b, k):
            return UNITS * b + k

        def o_use(g, u):
            b, qt, lane, slots = g["units"][u]
            return (2 * b + qt) * g["lanes"] + lane, slots[0] == 0, slots[-1] == 3

        small_loads = []
        for i, w in enumerate(("Wa", "Wb", "Wc")):
            small_loads.append((WABC[:, i, :], ins[f"L0_attn_{w}"]))
        for i, w in enumerate(("ba", "bb", "bc")):
            for b in range(2):
                small_loads.append((bab[NS * b:NS * b + NS, i:i + 1], ins[f"L0_attn_{w}"].unsqueeze(1)))
        small_loads.append((WD, ins["L0_attn_Wd"]))
        for b in range(2):
            small_loads.append((WYP[NS * b:NS * b + NS, b, :], ins["L0_attn_Wy"]))
        small_loads.append((ybrow[:, 0, :], ins["L0_attn_by"].partition_broadcast(P)))
        small_loads.append((ybrow[:, 1, :], ins["L0_attn_bd"].partition_broadcast(P)))
        for k in range(2):
            for x in range(2):
                small_loads.append((ROPE[:, k, x], ins["rope"][k, x].rearrange("(t p) d -> p t d", p=P)))
        for l in range(LAYERS):
            small_loads.append((WQKV[:, l].rearrange("p s n -> p (s n)"), ins["L0_ffn_wqkv"][l]))
            small_loads.append((QKS[:, l, 0, :], ins["L0_ffn_q_scale"][l].partition_broadcast(P)))
            small_loads.append((QKS[:, l, 1, :], ins["L0_ffn_k_scale"][l].partition_broadcast(P)))
            small_loads.append((WO[:, l], ins["L0_ffn_wo"][l].rearrange("(c p) n -> p c n", p=P)))
            small_loads.append((W1[:, l, :], ins["L0_ffn_w1"][l]))
            small_loads.append((W2[:, l, 0:2, :], ins["L0_ffn_w2"][l][0:256].rearrange("(c p) n -> p c n", p=P)))
            small_loads.append((W2[0:85, l, 2, :], ins["L0_ffn_w2"][l][256:HID]))
            small_loads.append((lgc[:, l, 0:1], ins["L0_ffn_ln_g"][l].unsqueeze(1)))
            small_loads.append((lgc[:, l, 1:2], ins["L0_ffn_ln_b"][l].unsqueeze(1)))
            for h in range(2):
                for c, (f, m) in enumerate(HC):
                    small_loads.append((b1c[0:m, l, h, c:c + 1],
                                        ins["L0_ffn_b1"][l][h * HID + f:h * HID + f + m].unsqueeze(1)))
            small_loads.append((b2row[:, l, :], ins["L0_ffn_b2"][l].partition_broadcast(P)))
        LOADED_A = 16 * len(small_loads)
        POOL_CONSTS = 13 + 6 + 4 + 3

        block = ctx.enter_context(nc.Block())

        @block.sync
        def _(sp):
            st_y.begin(sp, 16)
            sp.dma_start(XALL[:], ins["L0_attn_x"].rearrange("b (t p) d -> p (b t) d", p=P)).then_inc(ld_x, 16)
            sp.wait_ge(dve_consts, 1)
            for dst, src in small_loads:
                sp.dma_start(dst, src).then_inc(ld_a, 16)
            for i, w in enumerate(("Wq", "Wk", "Wv", "Wo")):
                sp.dma_start(WRAW[:, i, :], ins[f"L1_attn_{w}"]).then_inc(ld_raw, 16)
            sp.dma_start(WRAW[0:E, 4, :], ins["L1_ffn_router_w"]).then_inc(ld_raw, 16)
            sp.dma_start(borow[:], ins["L1_attn_bo"].partition_broadcast(P)).then_inc(ld_l1, 16)
            sp.dma_start(rbrow[:], ins["L1_ffn_router_b"].partition_broadcast(P)).then_inc(ld_l1, 16)
            sp.dma_start(GB[:].rearrange("p e d -> p (e d)"),
                         ins["L1_ffn_ln_g"].rearrange("e d -> (e d)").partition_broadcast(P)).then_inc(ld_l1, 16)
            sp.dma_start(BB[:].rearrange("p e d -> p (e d)"),
                         ins["L1_ffn_ln_b"].rearrange("e d -> (e d)").partition_broadcast(P)).then_inc(ld_l1, 16)
            sp.wait_ge(pool_consts, POOL_CONSTS)
            for j in range(0, CT, 4):
                sp.dma_start(XG3[j:j + 4].rearrange("j p d -> p j d"),
                             zeros[:].rearrange("p (j d) -> p j d", j=4)).then_inc(zeroed, 16)
            sp.wait_ge(a_over, ENGINES)
            with sp.Fori(0, E // 2) as i:
                for p in range(2):
                    e = i * 2 + p
                    sp.wait_ge(t_full.sem(1), t_full.did(T_W0 + e - 2, 1))
                    sp.dma_start(WST[:, p, 0, :].rearrange("p (k d) -> p k d", k=2),
                                 ins["L1_ffn_w1"][e].rearrange("(k p) d -> p k d", p=P)).then_inc(ld_w.sem(p), 16)
                    sp.dma_start(WST[:, p, 1, :].rearrange("p (k d) -> p k d", k=2),
                                 ins["L1_ffn_w3"][e].rearrange("(k p) d -> p k d", p=P)).then_inc(ld_w.sem(p), 16)
                    sp.dma_start(WST[:, p, 2, :], ins["L1_ffn_w2"][e]).then_inc(ld_w.sem(p), 16)
            sp.wait_ge(scattered, 16 * 2 * NT)
            sp.wait_ge(b_over, ENGINES)
            sp.dma_start(XGS, XG3[0:CG].rearrange("j p d -> p j d")).then_inc(ld_g, 16)

            def turn(i, last):
                if not last:
                    sp.wait_ge(t_full.sem(1), t_full.did(T_X0 + i * (T_C_USES // 2), 1))
                    sp.dma_start(XGS, XG3[bass.ds(i * CG + CG, CG)].rearrange("j p d -> p j d")).then_inc(ld_g, 16)
                for j in range(CG):
                    sp.wait_ge(c_yo.sem(j), c_yo.did(i * (CG // 2), j))
                    sp.dma_start(YG3[i * CG + j], YO[:, j % 2, :]).then_inc(st_y.sem(j), 16)

            with sp.Fori(0, CT // CG - 1) as i:
                turn(i, False)
            turn(CT // CG - 1, True)
            for c in range(TURNS):
                sp.wait_ge(out_ready, c + 1)
                sp.dma_start(out.rearrange("b (t p) d -> p (b t) d", p=P)[:, c * GT:c * GT + GT, :],
                             OUTB[:, c % 2, :].rearrange("p (t d) -> p t d", t=GT)).then_inc(st_out.sem(c), 16)
            for p in range(2):
                sp.wait_ge(st_out.sem(p), 16 * TURNS // 2)

        @block.tensor
        def _(pe):
            def mm(o, lhsT, rhs, start=True, stop=True):
                return nc.tensor.matmul(o, lhsT, rhs, start=start, stop=stop)

            for events in (t_full, m_full, s_full, pv_done):
                events.begin(pe)

            def t_open(ht, n):
                pe.wait_ge(t_free.sem(n), t_free.reuse(ht, n))
                return Tb[n % 2]

            def m_open(hm, n, *read):
                for e in latest(n - 2, *read):
                    pe.wait_ge(m_free.sem(e), m_free.did(hm, e))
                return Mb[n % 2]

            def scores(g, u, hs, n):
                b, qt, lane, slots = g["units"][u]
                pe.wait_ge(s_free.sem(n), s_free.reuse(hs, n))
                bank, keys = Sb[n % 2], P * (qt + 1)
                mm(bank[:], identb[:], g["masks"][qt][:], True, False)
                for i, s in enumerate(slots):
                    last = mm(bank[:, i * keys:(i + 1) * keys],
                              g["q"](lane, s)[:, (2 * b + qt) * P:(2 * b + qt + 1) * P],
                              g["k"](s)[:, 2 * b * P:2 * b * P + keys], False, i == len(slots) - 1)
                last.then_inc(s_full.sem(n), 1)

            def turn_probs(ht, n, hs, m):
                pe.wait_ge(exp_done.sem(m), exp_done.did(hs, m))
                bank = t_open(ht, n)
                for c in range(4):
                    last = nc.tensor.transpose(bank[:, c * P:(c + 1) * P], PR[:, m % 2, c * P:(c + 1) * P], ident[:])
                last.then_inc(t_full.sem(n), 1)

            def values(g, u, ht, n, hs, m, ho, o0):
                b, qt, lane, slots = g["units"][u]
                o, starts, ends = o_use(g, u)
                o += o0
                if starts:
                    pe.wait_ge(o_free.sem(o), o_free.reuse(ho, o))
                pe.wait_ge(t_free.sem(n), t_free.did(ht, n))
                c, w = 0, g["dv"] + 1
                for s in slots:
                    head = g["lanes"] * s + lane
                    for kt in range(qt + 1):
                        last = mm(Ob[o % 2][:, s * w:(s + 1) * w], PT[:, m % 2, c * P:(c + 1) * P],
                                  g["v"][:, 2 * b + kt, head, :], kt == 0, kt == qt)
                        c += 1
                last.then_inc(pv_done.sem(m), 1)

            pe.wait_ge(ld_raw, 16 * 5)
            pe.wait_ge(pool_consts, POOL_CONSTS)
            for c in range(4):
                last = nc.tensor.transpose(Tb[0][:, c * P:(c + 1) * P], WRAW[:, c, :], ident[:])
            last.then_inc(t_full.sem(0), 1)
            nc.tensor.transpose(Tb[1][:, 0:E], WRAW[0:E, 4, :], ident[0:E, 0:E]).then_inc(t_full.sem(1), 1)
            pe.wait_ge(ld_a, LOADED_A)
            pe.wait_ge(dve_consts, 2)

            with pe.Fori(0, TURNS) as it:
                ht, hm = T_A0 + it * (T_A_USES // 2), it * (M_A_USES // 2)
                hs, ho, hq = it * (S_A_USES // 2), it * (O_A_USES // 2), it * (QK_EVENTS // 2)

                def copied(*items):
                    for n in latest(*(T_A[i] for i in items)):
                        pe.wait_ge(t_free.sem(n), t_free.did(ht, n))

                for item in ORDER:
                    kind, *of = item
                    if kind == "x":
                        l, b = of
                        if l == 0:
                            pe.wait_ge(xn_ready, it * 2 + (b + 1))
                        else:
                            pe.wait_ge(ffn_added, it * FFN_EVENTS + (FFNS["w2", 0, b] + 1))
                        bank = t_open(ht, T_A[item])
                        for t in range(2):
                            last = nc.tensor.transpose(bank[:, t * P:(t + 1) * P], XC[:, 2 * b + t, :], ident[:])
                        last.then_inc(t_full.sem(T_A[item]), 1)
                    if kind == "ab":
                        copied(("x", 0, 0), ("x", 0, 1))
                        bank = m_open(hm, M_A[item])
                        for i in range(2):
                            for b in range(2):
                                last = mm(bank[NS * b:NS * b + NS, i * SEQ:(i + 1) * SEQ], WABC[:, i, :],
                                          XNT[:, b * SEQ:(b + 1) * SEQ])
                        last.then_inc(m_full.sem(M_A[item]), 1)
                    if kind == "c":
                        bank = m_open(hm, M_A[item])
                        for b in range(2):
                            last = mm(bank[NS * b:NS * b + NS, 0:SEQ], WABC[:, 2, :], XNT[:, b * SEQ:(b + 1) * SEQ])
                        last.then_inc(m_full.sem(M_A[item]), 1)
                    if kind == "y":
                        pe.wait_ge(cs_done, it + 1)
                        bank = m_open(hm, M_A[item])
                        for t in range(GT):
                            mm(bank[:, t * P:(t + 1) * P], CS[0:2 * NS, (t % 2) * P:(t % 2 + 1) * P],
                               WYP[0:2 * NS, t // 2, :], True, False)
                            last = mm(bank[:, t * P:(t + 1) * P], XNT[:, t * P:(t + 1) * P], WD, False, True)
                        last.then_inc(m_full.sem(M_A[item]), 1)
                    if kind in ("qk", "v"):
                        l, n = of
                        t, i = (n // 2, n % 2) if kind == "qk" else (n, 2)
                        if kind == "qk" and n % 4 == 0:
                            copied(("x", l, t // 2))
                        mm(m_open(hm, M_A[item])[:], HT[:, t // 2, (t % 2) * P:(t % 2 + 1) * P], WQKV[:, l, i, :])\
                            .then_inc(m_full.sem(M_A[item]), 1)
                    if kind == "qkT":
                        l, n = of
                        m, u = QK["qk", l, n], T_A[item]
                        pe.wait_ge(rope_done.sem(m), rope_done.did(hq, m))
                        bank = t_open(ht, u)
                        for c in range(4):
                            last = nc.tensor.transpose(bank[:, c * P:(c + 1) * P], R1[:, m % 4, c * P:(c + 1) * P],
                                                       ident[:])
                        last.then_inc(t_full.sem(u), 1)
                    if kind == "S":
                        l, b, k = of
                        if k == 0:
                            copied(("qkT", l, 4 * b + 2), ("qkT", l, 4 * b + 3))
                        scores(ATT0, unit_of(b, k), hs, S_A[item])
                    if kind == "T":
                        turn_probs(ht, T_A[item], hs, S_A["S", *of])
                    if kind == "V":
                        l, b, k = of
                        values(ATT0, unit_of(b, k), ht, T_A["T", l, b, k], hs, S_A["S", l, b, k], ho, 8 * l)
                    if kind == "oT":
                        l, t = of
                        for o in (8 * l + 2 * t, 8 * l + 2 * t + 1):
                            pe.wait_ge(o_free.sem(o), o_free.did(ho, o))
                        bank = t_open(ht, T_A[item])
                        for c in range(4):
                            last = nc.tensor.transpose(bank[:, c * P:(c + 1) * P], OS[:, t, c * P:(c + 1) * P],
                                                       ident[:])
                        last.then_inc(t_full.sem(T_A[item]), 1)
                    if kind == "wo":
                        l, b = of
                        copied(("oT", l, 2 * b), ("oT", l, 2 * b + 1))
                        bank = m_open(hm, M_A[item])
                        for t in range(2):
                            for c in range(4):
                                last = mm(bank[:, t * P:(t + 1) * P], OT[:, t, c * P:(c + 1) * P], WO[:, l, c, :],
                                          c == 0, c == 3)
                        last.then_inc(m_full.sem(M_A[item]), 1)
                    if kind == "sh":
                        l, b = of
                        bank = m_open(hm, M_A[item], M_A["wo", l, b])
                        mm(bank[:, 0:64], shift[:], XC[:, 2 * b, 64:D])
                        mm(bank[:, 64:128], shift[:], XC[:, 2 * b + 1, 64:D], True, False)
                        mm(bank[:, 64:128], carry[:], XC[:, 2 * b, 64:D], False, True).then_inc(m_full.sem(M_A[item]), 1)
                    if kind == "hT":
                        l, b = of
                        n = M_A["sh", l, b]
                        pe.wait_ge(m_free.sem(n), m_free.did(hm, n))
                        bank = t_open(ht, T_A[item])
                        for t in range(2):
                            last = nc.tensor.transpose(bank[:, t * P:(t + 1) * P], HN[:, 2 * b + t, :], ident[:])
                        last.then_inc(t_full.sem(T_A[item]), 1)
                    if kind == "w1":
                        l, b, c = of
                        f, m = HC[c]
                        if c == 0:
                            copied(("hT", l, b))
                        bank = m_open(hm, M_A[item])
                        for h in (1, 0):
                            last = mm(bank[0:m, (1 - h) * SEQ:(2 - h) * SEQ], W1[:, l, h * HID + f:h * HID + f + m],
                                      HNT[:, b * SEQ:(b + 1) * SEQ])
                        last.then_inc(m_full.sem(M_A[item]), 1)
                    if kind == "w2":
                        l, b = of
                        bank = m_open(hm, M_A[item], M_A["w1", l, b, 2])
                        for t in range(2):
                            for c, (f, m) in enumerate(HC):
                                last = mm(bank[:, t * P:(t + 1) * P], HG[0:m, c, (2 * b + t) * P:(2 * b + t + 1) * P],
                                          W2[0:m, l, c, :], c == 0, c == 2)
                        last.then_inc(m_full.sem(M_A[item]), 1)
                    if kind == "x1T":
                        b, = of
                        pe.wait_ge(xn1_ready, it * 2 + (b + 1))
                        bank = t_open(ht, T_A[item])
                        for t in range(2):
                            last = nc.tensor.transpose(bank[:, t * P:(t + 1) * P], HN[:, 2 * b + t, :], ident[:])
                        last.then_inc(t_full.sem(T_A[item]), 1)
                    if kind == "router":
                        copied(("x1T", 0), ("x1T", 1))
                        bank = m_open(hm, M_A[item])
                        for t in range(GT):
                            last = mm(bank[:, t * E:(t + 1) * E], XNT[:, t * P:(t + 1) * P], RWT[:])
                        last.then_inc(m_full.sem(M_A[item]), 1)
            pe.drain().then_inc(a_over, 1)
            pe.wait_ge(a_over, ENGINES)

            with pe.Fori(0, E // 2) as i:
                ht = T_W0 + i * 2
                for p in range(2):
                    pe.wait_ge(ld_w.sem(p), (i + 1) * 48)
                    bank = t_open(ht, 2 * p)
                    for c in range(4):
                        last = nc.tensor.transpose(bank[:, c * P:(c + 1) * P],
                                                   WST[:, p, c // 2, (c % 2) * P:(c % 2 + 1) * P], ident[:])
                    last.then_inc(t_full.sem(2 * p), 1)
                    bank = t_open(ht, 2 * p + 1)
                    for c in range(2):
                        last = nc.tensor.transpose(bank[:, c * P:(c + 1) * P], WST[:, p, 2, c * P:(c + 1) * P],
                                                   ident[:])
                    last.then_inc(t_full.sem(2 * p + 1), 1)
            pe.wait_ge(onehot, 1)
            mm(m_open(M_W0, 0)[:, 0:NT * E], trib[:], ONEH_B).then_inc(m_full.sem(0), 1)
            mm(m_open(M_W0, 1)[:, 0:NT * E], onesb[:], ONEH_B).then_inc(m_full.sem(1), 1)

            with pe.Fori(0, TURNS) as it:
                ht, hm = T_B0 + it * (T_B_USES // 2), M_B0 + it * (M_B_USES // 2)
                hs, ho = S_B0 + it * (S_B_USES // 2), O_B0 + it * (O_B_USES // 2)
                for n, w in ((M_B["q"], WQT), (M_B["k"], WKT)):
                    mm(m_open(hm, n)[:], w[:], XNT1ALL[:, bass.ds(it * TOK, TOK)]).then_inc(m_full.sem(n), 1)
                pe.wait_ge(xs_ready, it + 1)
                for b in range(2):
                    n = M_B["v"] + b
                    bank = m_open(hm, n)
                    for t in range(2):
                        last = mm(bank[:, t * P:(t + 1) * P], XS[:, (2 * b + t) * P:(2 * b + t + 1) * P], WVT[:])
                    last.then_inc(m_full.sem(n), 1)

                def ready(k, b):
                    if k == 0 and b == 0:
                        for n in (M_B["v"], M_B["v"] + 1):
                            pe.wait_ge(m_free.sem(n), m_free.did(hm, n))
                    if k < 4:
                        pe.wait_ge(q_masked, masked(it, b, 4 * k + 4))

                for k in range(24 + 3):
                    if k < 24:
                        ready(k % 12, k // 12)
                        scores(ATT1, k, hs, k)
                    if 2 <= k < 24 + 2:
                        turn_probs(ht, T_B["att"] + k - 2, hs, k - 2)
                    if k >= 3:
                        values(ATT1, k - 3, ht, T_B["att"] + k - 3, hs, k - 3, ho, 0)
                for b in range(2):
                    n = T_B["ctx"] + b
                    for o in (8 * b + 6, 8 * b + 7):
                        pe.wait_ge(o_free.sem(o), o_free.did(ho, o))
                    bank = t_open(ht, n)
                    for t in range(2):
                        last = nc.tensor.transpose(bank[:, t * P:(t + 1) * P], CTX[:, 2 * b + t, :], ident[:])
                    last.then_inc(t_full.sem(n), 1)
                for b in range(2):
                    n = T_B["ctx"] + b
                    pe.wait_ge(t_free.sem(n), t_free.did(ht, n))
                    n = M_B["out"] + b
                    bank = m_open(hm, n)
                    for t in range(2):
                        last = mm(bank[:, t * P:(t + 1) * P], CTXT[:, b, t * P:(t + 1) * P], WOT[:])
                    last.then_inc(m_full.sem(n), 1)
            pe.drain().then_inc(b_over, 1)
            pe.wait_ge(b_over, ENGINES)

            def tiles_t(ht, n0):
                for b in range(2):
                    bank = t_open(ht, n0 + b)
                    for t in range(2):
                        last = nc.tensor.transpose(bank[:, t * P:(t + 1) * P], XGS[:, 2 * b + t, :], ident[:])
                    last.then_inc(t_full.sem(n0 + b), 1)

            pe.wait_ge(ld_g, 16)
            tiles_t(T_X0, 0)
            for b in range(2):
                pe.wait_ge(t_free.sem(b), t_free.did(T_X0, b))

            def turn(i, last_turn):
                ht, hm, ho = T_C0 + i * (T_C_USES // 2), M_C0 + i * 2, O_C0 + i * 2
                e = [pe.value_load(EID[0:1, bass.ds(i * CG + j, 1)], min_val=0, max_val=E - 1) for j in range(CG)]

                def hidden(j):
                    mm(m_open(hm, j)[:], XGT[:, j * P:(j + 1) * P], W13[:, e[j], :]).then_inc(m_full.sem(j), 1)

                def gate_t(j):
                    pe.wait_ge(m_free.sem(j), m_free.did(hm, j))
                    bank = t_open(ht, j)
                    for c in range(2):
                        last = nc.tensor.transpose(bank[:, c * P:(c + 1) * P], GS[:, j % 2, c * P:(c + 1) * P],
                                                   ident[:])
                    last.then_inc(t_full.sem(j), 1)

                def down(j):
                    pe.wait_ge(t_free.sem(j), t_free.did(ht, j))
                    pe.wait_ge(o_free.sem(j), o_free.reuse(ho, j))
                    for c in range(2):
                        last = mm(Ob[j % 2][:, 0:D], GTT[:, j % 2, c * P:(c + 1) * P],
                                  W2T[:, e[j], c * D:(c + 1) * D], c == 0, c == 1)
                    last.then_inc(pv_done.sem(j), 1)

                hidden(0)
                hidden(1)
                gate_t(0)
                hidden(2)
                gate_t(1)
                down(0)
                hidden(3)
                gate_t(2)
                down(1)
                gate_t(3)
                if not last_turn:
                    pe.wait_ge(ld_g, i * 16 + 32)
                    tiles_t(ht, T_C["x"])
                down(2)
                down(3)
                if not last_turn:
                    for b in range(2):
                        n = T_C["x"] + b
                        pe.wait_ge(t_free.sem(n), t_free.did(ht, n))

            with pe.Fori(0, CT // CG - 1) as i:
                turn(i, False)
            turn(CT // CG - 1, True)

        @block.scalar
        def _(act):
            def act_fn(o, i, f, **kw):
                return nc.scalar.activation(o, i, f, **kw)

            for events in (t_free, exp_done, sq_done, c_silu):
                events.begin(act)

            def exponentials(hs, n):
                act.wait_ge(s_free.sem(n), s_free.did(hs, n))
                act_fn(PR[:, n % 2, :], SE[:, n % 2, :], ACT.Exp).then_inc(exp_done.sem(n), 1)

            def keep_probs(ht, n, hs, m):
                act.wait_ge(t_full.sem(n), t_full.did(ht, n))
                act.wait_ge(pv_done.sem(m), pv_done.reuse(hs, m))
                act_fn(PT[:, m % 2, :], Tb[n % 2][:], ACT.Copy).then_inc(t_free.sem(n), 1)

            act.wait_ge(t_full.sem(0), t_full.did(0, 0))
            for i, w in enumerate((WQT, WKT)):
                act_fn(w[:], Tb[0][:, i * P:(i + 1) * P], ACT.Copy)
            act_fn(WVT[:], Tb[0][:, 2 * P:3 * P], ACT.Copy)
            act_fn(WOT[:], Tb[0][:, 3 * P:4 * P], ACT.Copy).then_inc(t_free.sem(0), 1)
            act.wait_ge(t_full.sem(1), t_full.did(0, 1))
            act_fn(RWT[:], Tb[1][:, 0:E], ACT.Copy).then_inc(t_free.sem(1), 1)
            act.wait_ge(tables, 1)
            act.wait_ge(ld_a, LOADED_A)
            act.wait_ge(dve_consts, 2)

            with act.Fori(0, TURNS) as it:
                ht, hm = T_A0 + it * (T_A_USES // 2), it * (M_A_USES // 2)
                hs, hq = it * (S_A_USES // 2), it * (QK_EVENTS // 2)

                def from_t(item):
                    n = T_A[item]
                    act.wait_ge(t_full.sem(n), t_full.did(ht, n))
                    return Tb[n % 2], t_free.sem(n)

                def from_m(item):
                    n = M_A[item]
                    act.wait_ge(m_full.sem(n), m_full.did(hm, n))
                    return Mb[n % 2], m_free.sem(n)

                for item in ORDER:
                    kind, *of = item
                    if kind == "x":
                        l, b = of
                        bank, free = from_t(item)
                        if l == 0:
                            act.wait_ge(xn1_kept, it * 2 + (b + 1))
                            act_fn(XNT[:, b * SEQ:(b + 1) * SEQ], bank[:, 0:SEQ], ACT.Copy)
                        act_fn(HT[0:64, b], bank[0:64, 0:SEQ], ACT.Copy)
                        act_fn(HT[64:P, b, 1:SEQ], bank[64:P, 0:SEQ - 1], ACT.Copy).then_inc(free, 1)
                    if kind == "ab":
                        bank, free = from_m(item)
                        act_fn(EA[0:2 * NS], bank[0:2 * NS, 0:SEQ], ACT.Exp, scale=-1.0,
                               bias=bab[0:2 * NS, 3:4]).then_inc(ea_done, 1)
                    if kind == "c":
                        bank, free = from_m(item)
                        act_fn(TC[0:2 * NS], bank[0:2 * NS, 0:SEQ], ACT.Tanh, bias=bab[0:2 * NS, 2:3])\
                            .then_inc(free, 1)
                    if kind == "qk":
                        m = QK[item]
                        bank, free = from_m(item)
                        act.wait_ge(ss_done.sem(m), ss_done.reuse(hq, m))
                        act_fn(SQ[:, m % 2, :], bank[:], ACT.Square).then_inc(sq_done.sem(m), 1)
                    if kind == "v":
                        l, t = of
                        bank, free = from_m(item)
                        act_fn(VA[:, t, :, 0:DH], bank[:].rearrange("p (h d) -> p h d", h=8), ACT.Copy)\
                            .then_inc(free, 1)
                    if kind == "qkT":
                        l, n = of
                        bank, free = from_t(item)
                        ts = slice(n // 2 * P, (n // 2 + 1) * P)
                        if n % 2 == 0:
                            for lane in range(2):
                                r = slice(DH * lane, DH * lane + DH)
                                last = act_fn(QT[r, lane, :, ts], bank[r, :].rearrange("p (c t) -> p c t", c=4),
                                              ACT.Copy)
                        else:
                            last = act_fn(KT[:, :, ts], bank[:].rearrange("p (c t) -> p c t", c=4), ACT.Copy)
                        last.then_inc(free, 1)
                    if kind == "T":
                        keep_probs(ht, T_A[item], hs, S_A["S", *of])
                    if kind == "S":
                        exponentials(hs, S_A[item])
                    if kind == "oT":
                        l, t = of
                        bank, free = from_t(item)
                        if t >= 2:
                            m = M_A["wo", l, 0]
                            act.wait_ge(m_full.sem(m), m_full.did(hm, m))
                        act_fn(OT[:, t % 2, :], bank[:], ACT.Copy).then_inc(free, 1)
                    if kind == "hT":
                        l, b = of
                        bank, free = from_t(item)
                        act_fn(HNT[:, b * SEQ:(b + 1) * SEQ], bank[:, 0:SEQ], ACT.Identity,
                               scale=lgc[:, l, 0:1], bias=lgc[:, l, 1:2]).then_inc(free, 1)
                    if kind == "w1":
                        l, b, c = of
                        g, m = GELUS[item], HC[c][1]
                        bank, free = from_m(item)
                        if g >= 2:
                            n = next(M_A[i] for i in GELUS if GELUS[i] == g - 2)
                            act.wait_ge(m_free.sem(n), m_free.did(hm, n))
                        act_fn(GG[0:m, g % 2, :], bank[0:m, 0:SEQ], ACT.Gelu, bias=b1c[0:m, l, 1, c:c + 1])\
                            .then_inc(gelu_done, 1)
                    if kind == "gate":
                        b, = of
                        act.wait_ge(ffn_added, it * FFN_EVENTS + (FFNS["w2", 1, b] + 1))
                        act_fn(EG[:, 2 * b:2 * b + 2, :].rearrange("p t d -> p (t d)"),
                               XC[:, 2 * b:2 * b + 2, :].rearrange("p t d -> p (t d)"), ACT.Silu)\
                            .then_inc(gate_done, 1)
                    if kind == "x1T":
                        b, = of
                        bank, free = from_t(item)
                        act_fn(XNT[:, b * SEQ:(b + 1) * SEQ], bank[:, 0:SEQ], ACT.Copy).then_inc(free, 1)
            act.drain().then_inc(a_over, 1)
            act.wait_ge(a_over, ENGINES)

            with act.Fori(0, E // 2) as i:
                for p in range(2):
                    act.wait_ge(t_full.sem(0), t_full.did(T_W0 + i * 2 + p, 0))
                    act_fn(W13[:, i * 2 + p, :], Tb[0][:], ACT.Copy).then_inc(t_free.sem(0), 1)
                    act.wait_ge(t_full.sem(1), t_full.did(T_W0 + i * 2 + p, 1))
                    act_fn(W2T[:, i * 2 + p, :], Tb[1][:, 0:2 * D], ACT.Copy).then_inc(t_free.sem(1), 1)
            act.wait_ge(gap_done, 1)
            act_fn(GW[:, 0, :], GW[:, 1, :], ACT.Exp).then_inc(gap_exp, 1)

            with act.Fori(0, TURNS) as it:
                ht, hm = T_B0 + it * (T_B_USES // 2), M_B0 + it * (M_B_USES // 2)
                hs, ho = S_B0 + it * (S_B_USES // 2), O_B0 + it * (O_B_USES // 2)
                for n in (M_B["v"], M_B["v"] + 1):
                    act.wait_ge(m_full.sem(n), m_full.did(hm - M_B_USES // 2, n))
                act_fn(XS, XNT1ALL[:, bass.ds(it * TOK, TOK)], ACT.Copy).then_inc(xs_ready, 1)
                n = M_B["q"]
                act.wait_ge(m_full.sem(n), m_full.did(hm, n))
                act.wait_ge(q_masked, masked(it, 0, 0))
                act_fn(XQ, Mb[n % 2][:], ACT.Copy, scale=DK1 ** -0.5).then_inc(m_free.sem(n), 1)
                n = M_B["k"]
                act.wait_ge(m_full.sem(n), m_full.did(hm, n))
                act_fn(KT1, Mb[n % 2][:], ACT.Copy).then_inc(m_free.sem(n), 1)
                for k in range(24 + 2):
                    if k >= 2:
                        keep_probs(ht, T_B["att"] + k - 2, hs, k - 2)
                    if k < 24:
                        exponentials(hs, k)
                for b in range(2):
                    n = T_B["ctx"] + b
                    act.wait_ge(t_full.sem(n), t_full.did(ht, n))
                    act_fn(CTXT[:, b, :], Tb[n % 2][:, 0:SEQ], ACT.Copy).then_inc(t_free.sem(n), 1)
            act.drain().then_inc(b_over, 1)
            act.wait_ge(b_over, ENGINES)

            def tiles(ht, n0):
                for b in range(2):
                    act.wait_ge(t_full.sem(n0 + b), t_full.did(ht, n0 + b))
                    act_fn(XGT[:, b * SEQ:(b + 1) * SEQ], Tb[(n0 + b) % 2][:, 0:SEQ], ACT.Copy)\
                        .then_inc(t_free.sem(n0 + b), 1)

            tiles(T_X0, 0)

            def turn(i, last_turn):
                ht, hm, ho = T_C0 + i * (T_C_USES // 2), M_C0 + i * 2, O_C0 + i * 2

                def silu(j):
                    act.wait_ge(m_full.sem(j), m_full.did(hm, j))
                    act.wait_ge(m_free.sem(j), m_free.reuse(hm, j))
                    act_fn(HS[:, j % 2, :], Mb[j % 2][:, 0:FE], ACT.Silu).then_inc(c_silu.sem(j), 1)

                def gate_t(j):
                    act.wait_ge(t_full.sem(j), t_full.did(ht, j))
                    act.wait_ge(pv_done.sem(j), pv_done.reuse(PV_C0 + i * 2, j))
                    act_fn(GTT[:, j % 2, :], Tb[j % 2][:, 0:FE], ACT.Copy).then_inc(t_free.sem(j), 1)

                silu(0)
                silu(1)
                gate_t(0)
                silu(2)
                gate_t(1)
                silu(3)
                gate_t(2)
                gate_t(3)
                if not last_turn:
                    tiles(ht, T_C["x"])

            with act.Fori(0, CT // CG - 1) as i:
                turn(i, False)
            turn(CT // CG - 1, True)
            for c in range(TURNS):
                act.wait_ge(moe_in, c + 1)
                act_fn(G3[:].rearrange("p t d -> p (t d)"), G2[:].rearrange("p t d -> p (t d)"), ACT.Silu)\
                    .then_inc(silu_done, 1)

        @block.vector
        def _(dve):
            V = nc.vector
            for events in (m_free, s_free, o_free, ss_done, rope_done, c_stats):
                events.begin(dve)
            steps = [0, 0]

            def settled():
                dve.sem_inc(dve_settled, 1)

            def step(instr, carry_wait=True):
                steps[1] += 1
                instr.then_inc(dstep, 1)
                dve.wait_ge(dstep, steps[0] + steps[1])
                if not carry_wait:
                    settled()

            def less_maximum(g, u, hs, n):
                b, qt, lane, slots = g["units"][u]
                dve.wait_ge(s_full.sem(n), s_full.did(hs, n))
                keys, ns = P * (qt + 1), len(slots)
                sc = Sb[n % 2][:].rearrange("p (s k) -> p s k", s=ns)
                mx = MX[:, n % 2, 0:ns]
                step(V.tensor_reduce(mx, sc, AX, ALU.max))
                dve.wait_ge(exp_done.sem(n), exp_done.reuse(hs, n))
                V.tensor_tensor(SE[:, n % 2, :].rearrange("p (s k) -> p s k", s=ns), sc,
                                mx.unsqueeze(2).broadcast_to([P, ns, keys]), ALU.subtract)\
                    .then_inc(s_free.sem(n), 1)

            def normalise(g, u, hs, m, o0):
                b, qt, lane, slots = g["units"][u]
                o, _, ends = o_use(g, u)
                if not ends:
                    return
                o, dv, w = o0 + o, g["dv"], g["dv"] + 1
                dve.wait_ge(pv_done.sem(m), pv_done.did(hs, m))
                ob = Ob[o % 2][:, 0:4 * w].rearrange("p (s w) -> p s w", w=w)
                rc = RC[:, o % 2, :].unsqueeze(2)
                step(V.reciprocal(rc, ob[:, :, dv:w]))
                dst = g["o"][:, 2 * b + qt, :].rearrange("p (s j d) -> p s j d", s=4, d=dv)[:, :, lane, :]
                V.tensor_tensor(dst, ob[:, :, 0:dv], rc.broadcast_to([P, 4, dv]), ALU.mult).then_inc(o_free.sem(o), 1)

            def norm(dst, src, t):
                return V.tensor_scalar(dst, src, MV[:, t, 0:1], RS[:, t:t + 1], ALU.subtract, ALU.mult)

            V.memset(WYP[:], 0.0).then_inc(dve_consts, 1)
            V.memset(QT[DH:P, 0], 0.0)
            V.memset(QT[0:DH, 1], 0.0)
            V.memset(VA[:, :, :, DH:DH + 1], 1.0)
            V.memset(HT[64:P, :, 0:1], 0.0).then_inc(dve_consts, 1)
            dve.wait_ge(ld_a, LOADED_A)
            for l in range(LAYERS):
                for k in range(2):
                    V.tensor_tensor(RT[:, 2 * l + k].rearrange("p x t d -> p (x t) d"),
                                    ROPE[:, k].rearrange("p x t d -> p (x t) d"),
                                    QKS[:, l, k, :].unsqueeze(1).broadcast_to([P, 4, DH]), ALU.mult)
            V.tensor_scalar(bab[0:2 * NS, 3:4], bab[0:2 * NS, 0:1], -1.0, None, ALU.mult)
            V.tensor_tensor(ybrow[:, 0, :], ybrow[:, 0, :], ybrow[:, 1, :], ALU.add).then_inc(tables, 1)
            dve.wait_ge(tables, 1)
            dve.wait_ge(ld_x, 16)
            dve.wait_ge(ld_l1, 16 * 4)
            dve.wait_ge(pool_consts, POOL_CONSTS)

            with dve.Fori(0, TURNS) as it:
                hm = it * (M_A_USES // 2)
                ht = T_A0 + it * (T_A_USES // 2)
                hs, ho = it * (S_A_USES // 2), it * (O_A_USES // 2)
                steps[:] = [it * D_A_STEPS, 0]
                hq = it * (QK_EVENTS // 2)

                def m_bank(item):
                    n = M_A[item]
                    dve.wait_ge(m_full.sem(n), m_full.did(hm, n))
                    return Mb[n % 2], m_free.sem(n)

                def scale_ready(item):
                    dve.wait_ge(rstd_done, it * STATS_EVENTS + (STATS[item] + 1))

                def whole_stats(b):
                    for t in (2 * b, 2 * b + 1):
                        last = V.bn_stats(ST[:, t, 0, :], XALL[:, it * GT + t, :])
                    step(last, False)
                    for t in (2 * b, 2 * b + 1):
                        last = V.bn_aggr(MV[:, t, :], ST[:, t, 0, :])
                    last.then_inc(stats_done, 1)

                for item in ORDER:
                    kind, *of = item
                    if kind == "st0":
                        whole_stats(of[0])
                    if kind == "nm0":
                        b, = of
                        scale_ready(("st0", b))
                        for t in (2 * b, 2 * b + 1):
                            last = norm(XC[:, t, :], XALL[:, it * GT + t, :], t)
                        last.then_inc(xn_ready, 1)
                    if kind == "ab":
                        dve.wait_ge(ea_done, it + 1)
                        r, n = slice(0, 2 * NS), M_A[item]
                        step(V.tensor_scalar(AA[r], EA[r], 1.0, None, ALU.add))
                        step(V.reciprocal(AA[r], AA[r]))
                        step(V.tensor_scalar(UU[r], AA[r], -1.0, 1.0, ALU.mult, ALU.add))
                        V.scalar_tensor_tensor(UU[r], Mb[n % 2][r, SEQ:2 * SEQ], bab[r, 1:2], UU[r], ALU.add, ALU.mult)\
                            .then_inc(m_free.sem(n), 1)
                    if kind == "scan":
                        r = slice(0, 2 * NS)
                        for n in latest(M_A["ab",], M_A["c",]):
                            dve.wait_ge(m_free.sem(n), m_free.did(hm, n))
                        step(V.tensor_tensor_scan(SC[r], AA[r], UU[r], 0.0, ALU.mult, ALU.add))
                        V.tensor_tensor(CS[r], TC[r], SC[r], ALU.mult).then_inc(cs_done, 1)
                    if kind == "y":
                        bank, free = m_bank(item)
                        V.tensor_tensor(S0, bank[:].rearrange("p (t d) -> p t d", t=GT),
                                        ybrow[:, 0, :].unsqueeze(1).broadcast_to([P, GT, D]), ALU.add).then_inc(free, 1)
                    if kind == "qk":
                        l, n = of
                        t, i, m, u = n // 2, n % 2, QK[item], M_A[item]
                        dve.wait_ge(sq_done.sem(m), sq_done.did(hq, m))
                        V.tensor_reduce(SS[:, m % 4, :], SQ[:, m % 2, :].rearrange("p (h d) -> p h d", h=8),
                                        AX, ALU.add).then_inc(ss_done.sem(m), 1)
                        src = Mb[u % 2][:].rearrange("p (h d) -> p h d", h=8)
                        dve.wait_ge(rope_sum.sem(m), rope_sum.reuse(hq, m))
                        if m >= 4:
                            w = next(T_A["qkT", *i[1:]] for i in QK if QK[i] == m - 4)
                            dve.wait_ge(t_full.sem(w), t_full.did(ht, w))
                        for x, dst in enumerate((R1[:, m % 4, :], R2[:, m % 2, :])):
                            last = V.tensor_tensor(dst.rearrange("p (h d) -> p h d", h=8), src,
                                                   RT[:, 2 * l + n % 2, x, t % 2, :].unsqueeze(1)
                                                   .broadcast_to([P, 8, DH]), ALU.mult)
                        last.then_inc(m_free.sem(u), 1)
                    if kind == "scale":
                        m = QK["qk", *of]
                        dve.wait_ge(rope_sum.sem(m), rope_sum.did(hq, m))
                        r1 = R1[:, m % 4, :].rearrange("p (h d) -> p h d", h=8)
                        V.tensor_tensor(r1, r1, RN[:, m % 4, :].unsqueeze(2).broadcast_to([P, 8, DH]), ALU.mult)\
                            .then_inc(rope_done.sem(m), 1)
                    if kind == "S":
                        l, b, k = of
                        less_maximum(ATT0, unit_of(b, k), hs, S_A[item])
                    if kind == "O":
                        l, b, k = of
                        normalise(ATT0, unit_of(b, k), hs, S_A["S", l, b, k], 8 * l)
                    if kind == "res":
                        l, b = of
                        bank, free = m_bank(("wo", l, b))
                        V.tensor_tensor(XC[:, 2 * b:2 * b + 2, :], XC[:, 2 * b:2 * b + 2, :],
                                        bank[:, 0:SEQ].rearrange("p (t d) -> p t d", t=2), ALU.add).then_inc(free, 1)
                    if kind == "sh":
                        l, b = of
                        n = M_A["wo", l, b]
                        dve.wait_ge(m_free.sem(n), m_free.did(hm, n))
                        bank, free = m_bank(item)
                        settled()
                        for t in range(2):
                            V.bn_stats(ST[:, 2 * b + t, 0, :], XC[:, 2 * b + t, 0:64])
                            last = V.bn_stats(ST[:, 2 * b + t, 1, :], bank[:, t * 64:(t + 1) * 64])
                        step(last, False)
                        for t in range(2):
                            last = V.bn_aggr(MV[:, 2 * b + t, :], ST[:, 2 * b + t].rearrange("p s c -> p (s c)"))
                        last.then_inc(stats_done, 1)
                    if kind == "nh":
                        l, b = of
                        n = M_A["sh", l, b]
                        scale_ready(("sh", l, b))
                        for t in range(2):
                            norm(HN[:, 2 * b + t, 0:64], XC[:, 2 * b + t, 0:64], 2 * b + t)
                            last = norm(HN[:, 2 * b + t, 64:D], Mb[n % 2][:, t * 64:(t + 1) * 64], 2 * b + t)
                        last.then_inc(m_free.sem(n), 1)
                    if kind == "w1":
                        l, b, c = of
                        g, n, m = GELUS[item], M_A[item], HC[c][1]
                        dve.wait_ge(gelu_done, it * GELU_EVENTS + (g + 1))
                        V.scalar_tensor_tensor(HG[0:m, c, b * SEQ:(b + 1) * SEQ], Mb[n % 2][0:m, SEQ:2 * SEQ],
                                               b1c[0:m, l, 0, c:c + 1], GG[0:m, g % 2, :], ALU.add, ALU.mult)\
                            .then_inc(m_free.sem(n), 1)
                    if kind == "w2":
                        l, b = of
                        bank, free = m_bank(item)
                        xc, n = XC[:, 2 * b:2 * b + 2, :], M_A[item]
                        V.tensor_tensor(xc, xc, bank[:, 0:SEQ].rearrange("p (t d) -> p t d", t=2), ALU.add)\
                            .then_inc(free, 1)
                        dve.wait_ge(m_free.sem(n), m_free.did(hm, n))
                        V.tensor_tensor(xc, xc, b2row[:, l, :].unsqueeze(1).broadcast_to([P, 2, D]), ALU.add)\
                            .then_inc(ffn_added, 1)
                    if kind == "gate":
                        b, = of
                        dve.wait_ge(gate_done, it * 2 + (b + 1))
                        eg = EG[:, 2 * b:2 * b + 2, :]
                        step(V.tensor_tensor(eg, eg, S0[:, 2 * b:2 * b + 2, :], ALU.mult))
                        xt = XALL[:, bass.ds(it * GT + 2 * b, 2), :]
                        step(V.tensor_tensor(xt, xt, eg, ALU.add), False)
                        whole_stats(b)
                    if kind == "nm1":
                        b, = of
                        scale_ready(("gate", b))
                        for t in (2 * b, 2 * b + 1):
                            last = norm(HN[:, t, :], XALL[:, it * GT + t, :], t)
                        last.then_inc(xn1_ready, 1)
                    if kind == "router":
                        bank, free = m_bank(item)
                        V.tensor_tensor(LG[:, bass.ds(it * GT, GT), :],
                                        bank[:, 0:GT * E].rearrange("p (t e) -> p t e", t=GT),
                                        rbrow[:].unsqueeze(1).broadcast_to([P, GT, E]), ALU.add).then_inc(free, 1)
                        n = M_A[item]
                        dve.wait_ge(m_free.sem(n), m_free.did(hm, n))
                assert steps[1] == D_A_STEPS, steps[1]
            dve.drain().then_inc(a_over, 1)
            dve.wait_ge(a_over, ENGINES)

            steps[:] = [TURNS * D_A_STEPS, 0]
            dve.wait_ge(iotas, 3)
            V.memset(VA1[:, :, :, DK1:DK1 + 1], 1.0)
            V.memset(KEEP, 1.0)
            for t in range(NT):
                last = V.max(MAXV[:, t, :], LG[:, t, :])
            step(last)
            for t in range(NT):
                last = V.max_index(MIDX[:, t, :].bitcast(U32), MAXV[:, t, :], LG[:, t, :])
            step(last)
            V.memset(KEEP[:, :, 0:1], 0.0)
            V.tensor_tensor(GW[:, 1, :], MAXV[:, :, 1], MAXV[:, :, 0], ALU.subtract).then_inc(gap_done, 1)
            step(V.tensor_copy(MIF.rearrange("p k t -> p t k"), MIDX[:, :, 0:2].bitcast(U32)))
            for k in range(2):
                last = V.tensor_tensor(ONEH[:, k], IOT.rearrange("p e t -> p t e"),
                                       MIF[:, k, :].unsqueeze(2).broadcast_to([P, NT, E]), ALU.is_equal)
            step(last)
            V.tensor_tensor(ONEH_B.rearrange("p (t e) -> p t e", t=NT), ONEH[:, 0], ONEH[:, 1], ALU.add)\
                .then_inc(onehot, 1)
            dve.wait_ge(gap_exp, 1)
            step(V.tensor_scalar(GW[:, 1, :], GW[:, 0, :], 1.0, None, ALU.add))
            step(V.reciprocal(WGT[:, 0, :], GW[:, 1, :]))
            V.tensor_tensor(WGT[:, 1, :], WGT[:, 0, :], GW[:, 0, :], ALU.mult)
            dve.wait_ge(m_full.sem(0), m_full.did(M_W0, 0))
            V.tensor_copy(CNT[:, 0].rearrange("p t e -> p (t e)"), Mb[0][:, 0:NT * E]).then_inc(m_free.sem(0), 1)
            dve.wait_ge(m_full.sem(1), m_full.did(M_W0, 1))
            V.tensor_copy(CNT[:, 1].rearrange("p t e -> p (t e)"), Mb[1][:, 0:NT * E]).then_inc(m_free.sem(1), 1)
            dve.wait_ge(m_free.sem(0), m_free.did(M_W0, 0))
            dve.wait_ge(m_free.sem(1), m_free.did(M_W0, 1))
            step(V.tensor_copy(CUM[:, 0], CNT[:, 1].rearrange("p t e -> p e t")))
            step(V.tensor_tensor_scan(CUM[:, 1].rearrange("p e t -> p (e t)"), KEEP.rearrange("p e t -> p (e t)"),
                                      CUM[:, 0].rearrange("p e t -> p (e t)"), 0.0, ALU.mult, ALU.add))
            step(V.tensor_tensor(CNT[:, 1], CUM[:, 1, :, NT - 1].unsqueeze(2).broadcast_to([P, E, NT]),
                                 IOTS[:], ALU.is_gt))
            step(V.tensor_reduce(NTI[:, 0, :], CNT[:, 1], AX, ALU.add))
            step(V.memset(NTI[:, 3, :], 1.0))
            step(V.tensor_tensor_scan(NTI[:, 1, :], NTI[:, 3, :], NTI[:, 0, :], 0.0, ALU.mult, ALU.add))
            step(V.tensor_tensor(NTI[:, 2, :], NTI[:, 1, :], NTI[:, 0, :], ALU.subtract))
            step(V.tensor_tensor(ENDS, NTI[:, 1, :].unsqueeze(1).broadcast_to([P, CT, E]), IOTJ, ALU.is_le))
            step(V.tensor_reduce(EF, ENDS, AX, ALU.add))
            step(V.tensor_scalar(EF, EF, float(E - 1), None, ALU.min))
            step(V.tensor_copy(EID[:], EF))
            step(V.tensor_tensor(CUM[:, 1], CUM[:, 1], CUM[:, 0], ALU.subtract))
            step(V.tensor_tensor(CNT[:, 0], CNT[:, 0], CUM[:, 1].rearrange("p e t -> p t e"), ALU.add))
            step(V.scalar_tensor_tensor(CNT[:, 0], NTI[:, 2, :].unsqueeze(1).broadcast_to([P, NT, E]), float(P),
                                        CNT[:, 0], ALU.mult, ALU.add))
            for k in range(2):
                step(V.tensor_tensor(ONEH[:, k], ONEH[:, k], CNT[:, 0], ALU.mult))
                step(V.tensor_reduce(PF[:, k, :], ONEH[:, k], AX, ALU.add))
            V.tensor_copy(POSU[:], PF).then_inc(pos_done, 1)
            routing_steps = steps[1]

            b0 = TURNS * D_A_STEPS + routing_steps
            with dve.Fori(0, TURNS) as it:
                hm = M_B0 + it * (M_B_USES // 2)
                hs, ho = S_B0 + it * (S_B_USES // 2), O_B0 + it * (O_B_USES // 2)
                steps[:] = [b0 + it * D_B_STEPS, 0]
                for b in range(2):
                    n = M_B["v"] + b
                    dve.wait_ge(m_full.sem(n), m_full.did(hm, n))
                    V.tensor_copy(VA1[:, 2 * b:2 * b + 2, :, 0:DK1],
                                  Mb[n % 2][:, 0:SEQ].rearrange("p (t h d) -> p t h d", t=2, h=E)).then_inc(m_free.sem(n), 1)
                for k in range(24 + 4):
                    if k >= 4:
                        normalise(ATT1, k - 4, hs, k - 4, 0)
                    if k < 24:
                        less_maximum(ATT1, k, hs, k)
                for b in range(2):
                    n = M_B["out"] + b
                    dve.wait_ge(m_full.sem(n), m_full.did(hm, n))
                    V.tensor_tensor(S1ALL[:, bass.ds(it * GT + 2 * b, 2), :],
                                    Mb[n % 2][:, 0:SEQ].rearrange("p (t d) -> p t d", t=2),
                                    borow[:].unsqueeze(1).broadcast_to([P, 2, D]), ALU.add).then_inc(m_free.sem(n), 1)
                assert steps[1] == D_B_STEPS, steps[1]
            dve.drain().then_inc(b_over, 1)
            dve.wait_ge(b_over, ENGINES)

            c0 = b0 + TURNS * D_B_STEPS

            def turn(i):
                ht, hm, ho = T_C0 + i * (T_C_USES // 2), M_C0 + i * 2, O_C0 + i * 2
                hp = PV_C0 + i * 2
                steps[:] = [c0 + i * D_C_STEPS, 0]
                for k in range(CG + 3):
                    if k < CG:
                        dve.wait_ge(c_silu.sem(k), c_silu.did(i * 2, k))
                        if k >= 2:
                            dve.wait_ge(t_full.sem(k), t_full.did(ht, k - 2))
                        V.tensor_tensor(GS[:, k % 2, :], HS[:, k % 2, :], Mb[k % 2][:, FE:2 * FE], ALU.mult)\
                            .then_inc(m_free.sem(k), 1)
                    if 2 <= k < CG + 2:
                        j = k - 2
                        dve.wait_ge(pv_done.sem(j), pv_done.did(hp, j))
                        settled()
                        step(V.bn_stats(ST[:, j, 0, :], Ob[j % 2][:, 0:D]), False)
                        V.bn_aggr(MV[:, j, :], ST[:, j, 0, :]).then_inc(c_stats.sem(j), 1)
                    if k >= 3:
                        j = k - 3
                        dve.wait_ge(c_rstd.sem(j), c_rstd.did(i * 2, j))
                        dve.wait_ge(c_yo.sem(j), c_yo.reuse(i * 2, j))
                        norm(YN[:, j % 2, :], Ob[j % 2][:, 0:D], j).then_inc(o_free.sem(j), 1)
                assert steps[1] == D_C_STEPS, steps[1]

            with dve.Fori(0, CT // CG - 1) as i:
                turn(i)
            turn(CT // CG - 1)
            steps[:] = [c0 + CT // CG * D_C_STEPS, 0]
            for c in range(TURNS):
                dve.wait_ge(gathered[c], 16 * 2 * GT)
                ts = slice(c * GT, c * GT + GT)
                if c:
                    dve.wait_ge(silu_done, c)
                if c >= 2:
                    dve.wait_ge(st_out.sem(c), 16)
                ob = OUTB[:, c % 2, :].rearrange("p (t d) -> p t d", t=GT)
                V.tensor_tensor(G2, YAB[:, ts, 0, :], WGT[:, 0, ts].unsqueeze(2).broadcast_to([P, GT, D]), ALU.mult)
                step(V.tensor_tensor(ob, YAB[:, ts, 1, :], WGT[:, 1, ts].unsqueeze(2).broadcast_to([P, GT, D]),
                                     ALU.mult))
                V.tensor_tensor(G2, G2, ob, ALU.add).then_inc(moe_in, 1)
                dve.wait_ge(silu_done, c + 1)
                step(V.tensor_tensor(ob, G3, S1ALL[:, ts, :], ALU.mult))
                V.tensor_tensor(ob, ob, XALL[:, ts, :], ALU.add).then_inc(out_ready, 1)

        @block.gpsimd
        def _(pool):
            G = nc.gpsimd
            for events in (rope_sum, c_yo, c_rstd):
                events.begin(pool)
            pool.sem_inc(xn1_kept, 2)
            steps = [0, 0]

            def settled():
                pool.sem_inc(pool_settled, 1)

            def step(instr):
                steps[1] += 1
                instr.then_inc(pstep, 1)
                pool.wait_ge(pstep, steps[0] + steps[1])

            for v, c in ((ident, 0.0), (identb, 0.0), (shift, 0.0), (carry, 0.0), (trib, 1.0), (onesb, 1.0),
                         (powm, -0.5), (zeros, 0.0), (headm, 1.0), (mask0[0], 0.0), (mask1[0], 0.0), (mask0[1], 0.0),
                         (mask1[1], 0.0)):
                G.memset(v[:], c).then_inc(pool_consts, 1)
            pool.wait_ge(pool_consts, 13)
            one = dict(compare_op=ALU.not_equal, fill=1.0, channel_multiplier=1)
            for v, base in ((ident, 0), (identb, 0), (shift, 1), (carry, -(P - 1))):
                G.affine_select(out=v[:], in_=v[:], base=base, pattern=[[-1, P]], **one).then_inc(pool_consts, 1)
            G.affine_select(out=trib[:], in_=trib[:], compare_op=ALU.is_gt, fill=0.0, base=0, pattern=[[1, P]],
                            channel_multiplier=-1).then_inc(pool_consts, 1)
            G.affine_select(out=headm[:], in_=headm[:], compare_op=ALU.is_ge, fill=0.0, base=0,
                            pattern=[[-DK1, E]], channel_multiplier=1).then_inc(pool_consts, 1)
            for qt in range(2):
                keys = P * (qt + 1)
                for m in ((mask0, mask1)[qt][0], (mask0, mask1)[qt][1]):
                    G.affine_select(out=m[:], in_=m[:], compare_op=ALU.is_ge, fill=MASKED, base=qt * P,
                                    pattern=[[0, 512 // keys], [-1, keys]], channel_multiplier=1)\
                        .then_inc(pool_consts, 1)
            pool.wait_ge(pool_consts, 13 + 6 + 4)
            G.affine_select(out=headm[:], in_=headm[:], compare_op=ALU.is_ge, fill=0.0, base=DK1 - 1,
                            pattern=[[DK1, E]], channel_multiplier=-1).then_inc(pool_consts, 1)
            for qt in range(2):
                keys = P * (qt + 1)
                m = (mask0, mask1)[qt][0]
                G.affine_select(out=m[:], in_=m[:], compare_op=ALU.is_ge, fill=MASKED, base=64 - qt * P,
                                pattern=[[0, 512 // keys], [1, keys]], channel_multiplier=-1)\
                    .then_inc(pool_consts, 1)
            pool.wait_ge(pool_consts, POOL_CONSTS)

            def rstd(o, var):
                n = var.shape[1]
                step(G.tensor_scalar(o, var, EPS, None, ALU.add))
                return G.tensor_tensor(o, o, powm[:, 0:n], ALU.pow)

            with pool.Fori(0, TURNS) as it:
                steps[:] = [it * P_A_STEPS, 0]
                ht = T_A0 + it * (T_A_USES // 2)
                hm = it * (M_A_USES // 2)
                hq = it * (QK_EVENTS // 2)
                for item in ORDER:
                    kind, *of = item
                    if kind in ("st0", "sh", "gate"):
                        b = of[-1]
                        pool.wait_ge(stats_done, it * STATS_EVENTS + (STATS[item] + 1))
                        settled()
                        rstd(RS[:, 2 * b:2 * b + 2], MV[:, 2 * b:2 * b + 2, 1]).then_inc(rstd_done, 1)
                    if kind == "qk":
                        m, u = QK[item], M_A[item]
                        pool.wait_ge(ss_done.sem(m), ss_done.did(hq, m))
                        settled()
                        step(G.tensor_scalar(RN[:, m % 4, :], SS[:, m % 4, :], 1e-24, None, ALU.max))
                        G.tensor_tensor(RN[:, m % 4, :], RN[:, m % 4, :], powm[:, 0:8], ALU.pow)
                        pool.wait_ge(m_free.sem(u), m_free.did(hm, u))
                        r1, r2 = (r.rearrange("p (h s d) -> p h s d", h=8, s=2) for r in (R1[:, m % 4, :], R2[:, m % 2, :]))
                        G.tensor_tensor(r1, r1, r2[:, :, ::-1, :], ALU.add).then_inc(rope_sum.sem(m), 1)
                    if kind == "x1T":
                        b, = of
                        pool.wait_ge(xn1_ready, it * 2 + (b + 1))
                        G.tensor_copy(XN1ALL[:, bass.ds(it * GT + 2 * b, 2), :], HN[:, 2 * b:2 * b + 2, :])
                        n = T_A[item]
                        pool.wait_ge(t_free.sem(n), t_free.did(ht, n))
                        G.tensor_copy(XNT1ALL[:, bass.ds(it * TOK + b * SEQ, SEQ)], XNT[:, b * SEQ:(b + 1) * SEQ])\
                            .then_inc(xn1_kept, 1)
                assert steps[1] == P_A_STEPS, steps[1]
            pool.drain().then_inc(a_over, 1)
            pool.wait_ge(a_over, ENGINES)
            step_c0 = TURNS * P_A_STEPS

            G.iota(IOTI.rearrange("p (e t) -> p e t", e=E), [[1, E], [0, NT]], base=0, channel_multiplier=0)\
                .then_inc(iota_raw, 1)
            G.iota(IOTI2.rearrange("p (e t) -> p e t", e=E), [[0, E], [P, NT]], base=0, channel_multiplier=0)\
                .then_inc(iota_raw, 1)
            G.iota(IOTI3.rearrange("p (j e) -> p j e", e=E), [[1, CT], [0, E]], base=0, channel_multiplier=0)\
                .then_inc(iota_raw, 1)
            pool.wait_ge(iota_raw, 3)
            G.tensor_copy(IOT.rearrange("p e t -> p (e t)"), IOTI).then_inc(iotas, 1)
            G.tensor_copy(IOTS.rearrange("p e t -> p (e t)"), IOTI2).then_inc(iotas, 1)
            G.tensor_copy(IOTJ.rearrange("p j e -> p (j e)"), IOTI3).then_inc(iotas, 1)
            pool.sem_inc(q_masked, 1)

            def mask_heads(it):
                hm, hs = M_B0 + it * (M_B_USES // 2), S_B0 + it * (S_B_USES // 2)
                for b in range(2):
                    if b == 0:
                        n = M_B["q"]
                        pool.wait_ge(m_free.sem(n), m_free.did(hm, n))
                    n = 12 * b + 11
                    pool.wait_ge(s_full.sem(n), s_full.did(hs - S_B_USES // 2, n))
                    settled()
                    for lane in range(4):
                        for s in range(4):
                            h = 4 * s + lane
                            G.tensor_scalar(QT1[:, h, b * SEQ:(b + 1) * SEQ], XQ[:, b * SEQ:(b + 1) * SEQ],
                                            headm[:, h:h + 1], None, ALU.mult).then_inc(q_masked, 1)

            mask_heads(0)
            pool.wait_ge(zeroed, 16 * CT // 4)
            pool.wait_ge(pos_done, 1)
            for t in range(NT):
                for k in range(2):
                    G.indirect_dma_start(XG, bass.IndirectOffsetOnAxis(POSU[:, k, t:t + 1], 0), XN1ALL[:, t, :], None)\
                        .then_inc(scattered, 16)
            with pool.Fori(1, TURNS) as it:
                mask_heads(it)
            pool.drain().then_inc(b_over, 1)
            pool.wait_ge(b_over, ENGINES)

            def turn(i):
                steps[:] = [step_c0 + i * P_C_STEPS, 0]
                for k in range(CG + 1):
                    if k < CG:
                        pool.wait_ge(c_stats.sem(k), c_stats.did(i * 2, k))
                        settled()
                        rstd(RS[:, k:k + 1], MV[:, k, 1:2]).then_inc(c_rstd.sem(k), 1)
                    if k >= 1:
                        j = k - 1
                        e = pool.value_load(EID[0:1, bass.ds(i * CG + j, 1)], min_val=0, max_val=E - 1)
                        pool.wait_ge(o_free.sem(j), o_free.did(O_C0 + i * 2, j))
                        pool.wait_ge(st_y.sem(j), st_y.reuse(i * 2, j) * 16)
                        step(G.tensor_tensor(YO[:, j % 2, :], YN[:, j % 2, :], GB[:, e, :], ALU.mult))
                        G.tensor_tensor(YO[:, j % 2, :], YO[:, j % 2, :], BB[:, e, :], ALU.add)\
                            .then_inc(c_yo.sem(j), 1)
                assert steps[1] == P_C_STEPS, steps[1]

            with pool.Fori(0, CT // CG - 1) as i:
                turn(i)
            turn(CT // CG - 1)
            for p in range(2):
                pool.wait_ge(st_y.sem(p), 16 * (CT // 2 + 1))
            for t in range(NT):
                for k in range(2):
                    G.indirect_dma_start(YAB[:, t, k, :], None, YG, bass.IndirectOffsetOnAxis(POSU[:, k, t:t + 1], 0))\
                        .then_inc(gathered[t // GT], 16)


def rope_tables():
    import numpy as np
    n, window = SEQ, 64
    half = np.arange(0, DH, 2, dtype=np.float32)
    inv = (np.float32(1.0) / np.float32(10000.0) ** (half / np.float32(DH))).astype(np.float32)
    t = np.arange(n, dtype=np.float32)
    freqs = (t[:, None] * inv[None, :]).astype(np.float32).astype(np.float64)
    base = ((half + np.float32(0.4 * DH)) / np.float32(1.4 * DH)).astype(np.float64)
    power = (t - n // 2).astype(np.float64) / float(window // 2)
    scale = base[None, :] ** power[:, None]
    cos, sin = np.cos(freqs), np.sin(freqs)
    tab = np.zeros((2, 2, n, DH), np.float64)
    for i, s in enumerate((8.0 * scale, 1.0 / scale)):
        tab[i, 0] = np.concatenate([cos * s, cos * s], -1)
        tab[i, 1] = np.concatenate([sin * s, -sin * s], -1)
    return tab.astype(np.float32)


NAMES = [f"L0_attn_{n}" for n in ("x", "Wa", "ba", "Wb", "bb", "Wc", "bc", "Wd", "bd", "Wy", "by")] + \
        [f"L0_ffn_{n}" for n in ("wqkv", "q_scale", "k_scale", "wo", "ln_g", "ln_b", "w1", "b1", "w2", "b2")] + \
        [f"L1_attn_{n}" for n in ("Wq", "Wk", "Wv", "Wo", "bo")] + \
        [f"L1_ffn_{n}" for n in ("router_w", "router_b", "w1", "w2", "w3", "ln_g", "ln_b")]


def kernel(**inputs):
    import numpy as np
    import concourse.bacc as bacc
    from concourse.bass_utils import run_bass_kernel_spmd

    nc = bacc.Bacc("TRN2", target_bir_lowering=False, num_devices=1)
    arrays = {f"in_{n}": np.ascontiguousarray(inputs[n]) for n in NAMES}
    arrays["in_rope"] = rope_tables()
    ins = {n[3:]: nc.dram_tensor(n, a.shape, mybir.dt.from_np(a.dtype), kind="ExternalInput").ap()
           for n, a in arrays.items()}
    out = nc.dram_tensor("out", (NB, SEQ, D), F32, kind="ExternalOutput").ap()
    gated_layers(nc, ins, out)
    return run_bass_kernel_spmd(nc, [arrays], core_ids=[0]).results[0]["out"]
```

```python
from contextlib import ExitStack

import concourse.bass as bass
from concourse import mybir

F32 = mybir.dt.float32
BF16 = mybir.dt.bfloat16
U32 = mybir.dt.uint32
I32 = mybir.dt.int32
ALU = mybir.AluOpType
ACT = mybir.ActivationFunctionType
AX = mybir.AxisListType.X

P = 128
D = 128
NB, SEQ = 8, 256
NT = NB * SEQ // P
GT = 4
TURNS = NT // GT
OUT_TILES = 8
TOK = GT * P
NS = 32
LAYERS = 2
INNER, DH = 512, 64
HID = 341
HC = [(0, 128), (128, 128), (256, 85)]
E, FE = 16, 256
DK1 = 8
CT = 48
CG = 8
C_TURNS = CT // CG
EPS = 1e-5
MASKED = -1e30


class Pair:

    def __init__(self, ctx, nc, name):
        self.sems = [ctx.enter_context(nc.semaphore(f"{name}{i}")) for i in range(2)]

    def sem(self, n):
        return self.sems[n % 2]

    def begin(self, eng, by=1):
        for s in self.sems:
            eng.sem_inc(s, by)

    def did(self, half, n):
        return half + (n // 2 + 2)

    def reuse(self, half, n):
        return half + (n // 2 + 1)


def latest(*events):
    return sorted({n % 2: n for n in sorted(events)}.values())


UNITS = 6
STARTS = (0, 1, 2, 2, 4, 4)
ENGINE_NAMES = ("PE", "ACT", "DVE", "Pool")
PARTS = {
    "st0": (("DVE", 0.7), ("Pool", 0.6)), "nm0": (("DVE", 0.5),),
    "x": (("PE", 0.3), ("ACT", 1.0)),
    "ab": (("PE", 1.8), ("ACT", 0.4), ("DVE", 3.0)), "c": (("PE", 0.9), ("ACT", 0.4)), "scan": (("DVE", 1.0),),
    "y": (("PE", 1.8), ("DVE", 0.6)),
    "qk": (("PE", 0.9), ("ACT", 0.5), ("DVE", 1.8), ("Pool", 3.1)), "v": (("PE", 0.9), ("ACT", 0.6)),
    "scale": (("DVE", 0.6),), "qkT": (("PE", 0.5), ("ACT", 0.8)),
    "S": (("PE", 1.1), ("DVE", 1.3), ("ACT", 0.5)), "T": (("PE", 0.5), ("ACT", 0.6)),
    "V": (("PE", 0.5),), "O": (("DVE", 0.5),),
    "oT": (("PE", 0.5), ("ACT", 0.6)), "wo": (("PE", 1.8), ("DVE", 0.4)),
    "sh": (("PE", 0.4), ("DVE", 1.2), ("Pool", 0.6)), "nh": (("DVE", 0.8),),
    "hT": (("PE", 0.3), ("ACT", 0.4)), "w1": (("PE", 0.9), ("ACT", 0.5), ("DVE", 0.4)),
    "w2": (("PE", 1.4), ("DVE", 0.8)),
    "gate": (("ACT", 0.5), ("DVE", 2.0), ("Pool", 0.6)), "nm1": (("DVE", 0.5),),
    "x1T": (("PE", 0.3), ("ACT", 0.4), ("Pool", 2.0)), "router": (("PE", 0.4), ("DVE", 0.2)),
}
HANDOVER = 0.25
TABLES = {"w1": "gelu", "S": "exp", "ab": "exp", "c": "exp", "gate": "silu"}
TABLE_LOAD = 1.3
BANKS = {"T": ("x", "qkT", "T", "oT", "hT", "x1T"), "S": ("S",),
         "M": ("ab", "c", "y", "qk", "v", "wo", "sh", "w1", "w2", "router")}
FREED_BY = {"x": "ACT", "qk": "DVE", "S": "DVE", "x1T": "ACT"}
SLACK, NEVER = 0.05, 1e9


HEAD_ITEMS = {("st0", 0), ("nm0", 0), ("x", 0, 0), ("v", 0, 0), ("v", 0, 1)} | \
             {(kind, 0, n) for kind in ("qk", "scale", "qkT") for n in range(4)}


def section_items(head, rest):
    after = {}

    def last(*item):
        return item, PARTS[item[0]][-1][0]

    def add(item, *parts):
        after[item] = list(parts)

    for b in range(2):
        add(("st0", b), *([last("nm1", 0)] if b == 0 else []))
        add(("nm0", b), last("st0", b), *([last("nm0", 1)] if b == 0 else []))
        for l in range(2):
            if l == 0:
                add(("x", l, b), last("nm0", b), *([(("y",), "PE")] if b == 0 else []))
            else:
                add(("x", l, b), last("w2", 0, b))
            for n in range(4 * b, 4 * b + 4):
                add(("qk", l, n), last("x", l, b), *([(("qk", l, n - 1), "PE")] if n % 4 else []))
                add(("scale", l, n), last("qk", l, n))
                add(("qkT", l, n), last("scale", l, n))
                if n % 2:
                    add(("v", l, n // 2), (("qk", l, n), "PE"))
            qkv = [last("qkT", l, n) for n in range(4 * b, 4 * b + 4)] + [last("v", l, 2 * b + t) for t in range(2)]
            for k in range(UNITS):
                add(("S", l, b, k), *([(("S", l, b, k - 1), "PE")] if k else qkv))
                add(("T", l, b, k), last("S", l, b, k))
                add(("V", l, b, k), last("T", l, b, k))
                if k == UNITS - 1 or STARTS[k + 1] == k + 1:
                    add(("O", l, b, k), last("V", l, b, k))
            for t in range(2):
                add(("oT", l, 2 * b + t), *[last("O", l, b, k) for k in ((0, 1), (3, 5))[t]])
            add(("wo", l, b), last("oT", l, 2 * b), last("oT", l, 2 * b + 1))
            add(("sh", l, b), last("wo", l, b))
            add(("nh", l, b), last("sh", l, b))
            add(("hT", l, b), last("nh", l, b))
            for c in range(3):
                add(("w1", l, b, c), last("hT", l, b), *([(("w1", l, b, c - 1), "PE")] if c else []))
            add(("w2", l, b), *[last("w1", l, b, c) for c in range(3)])
        add(("gate", b), last("w2", 1, b), last("y"), *([(("gate", 0), "ACT"), (("gate", 0), "DVE")] if b else []))
        add(("nm1", b), last("gate", b), *([last("nm1", 0)] if b else []))
        add(("x1T", b), last("nm1", b), *([last("x1T", 0)] if b else []))
    add(("ab",), last("x", 0, 1))
    add(("c",), (("ab",), "PE"))
    add(("scan",), last("ab"), last("c"))
    add(("y",), last("scan"))
    add(("router",), (("x1T", 0), "ACT"), (("x1T", 1), "ACT"))

    def holds(item, part):
        if part[0] in HEAD_ITEMS:
            return head and item in HEAD_ITEMS
        return rest

    return {item: [p for p in parts if holds(item, p)] for item, parts in after.items()
            if (head if item in HEAD_ITEMS else rest)}


def section_order(head, rest):
    after = section_items(head, rest)
    length = {(i, e): t for i in after for e, t in PARTS[i[0]]}
    before, followers, behind = {}, {p: [] for p in length}, {}
    for i, parts in after.items():
        for e, _ in PARTS[i[0]]:
            before[i, e] = parts
            for p in parts:
                followers[p].append((i, e))
            parts = [(i, e)]

    def work_behind(p):
        if p not in behind:
            behind[p] = length[p] + HANDOVER + max([work_behind(q) for q in followers[p]], default=0)
        return behind[p]

    done, order, free_at = {}, {e: [] for e in ENGINE_NAMES}, dict.fromkeys(ENGINE_NAMES, 0.0)

    def on(engine, *kinds):
        return [i for i in order[engine] if i[0] in kinds]

    def handed(item, engine):
        return done.get((item, engine), NEVER) + HANDOVER

    def start(p):
        item, e = p
        kind, of = item[0], item[1:]
        t = [free_at[e]] + [done[q] + (HANDOVER if q[1] != e else 0.08) for q in before[p]]
        for kinds in BANKS.values():
            if e == "PE" and kind in kinds and len(on("PE", *kinds)) >= 2:
                u = on("PE", *kinds)[-2]
                t.append(handed(("nh", *u[1:]), "DVE") if u[0] == "sh"
                         else handed(u, FREED_BY.get(u[0], PARTS[u[0]][-1][0])))
        for leader, kinds in (("PE", ("S", "T", "V")), ("PE", ("qk", "scale")), ("DVE", ("st0", "sh", "gate"))):
            if kind not in kinds or (e == leader and kind in (kinds[0], "sh", "gate")):
                continue
            stats = leader == "DVE"
            if stats and e != "Pool":
                continue
            seq = on(leader, *(kinds if stats else kinds[0:1]))
            n = len(on(e, *(kinds if stats else (kind,))))
            if n >= len(seq) or seq[n][1:] != of or (stats and seq[n] != item):
                return NEVER
            two = seq[n - 2][1:] if n >= 2 else None
            if two:
                t += {("S", "DVE"): [handed(("S", *two), "ACT")], ("S", "ACT"): [handed(("T", *two), "ACT")],
                      ("T", "ACT"): [handed(("V", *two), "PE")], ("qk", "ACT"): [handed(("qk", *two), "DVE")],
                      ("qk", "DVE"): [handed(("qk", *two), "Pool")]}.get((kind, e), [])
            if n >= 4 and (kind, e) == ("qk", "DVE"):
                t.append(handed(("qkT", *seq[n - 4][1:]), "PE"))
        if kind == "V" and STARTS[of[2]] == of[2]:
            opened = [i for i in on("PE", "V") if STARTS[i[3]] == i[3]]
            if len(opened) >= 2:
                l, b, k = opened[-2][1:]
                t.append(handed(("O", l, b, k if k < 2 else k + 1), "DVE"))
        if (kind, e) == ("w1", "ACT") and len(on("ACT", "w1")) >= 2:
            t.append(handed(on("ACT", "w1")[-2], "DVE"))
        tables = [TABLES[i[0]] for i in order["ACT"] if i[0] in TABLES]
        if e == "ACT" and kind in TABLES and tables[-1:] != [TABLES[kind]]:
            return max(t) + TABLE_LOAD
        return max(t)

    left = list(length)
    while left:
        can = [(start(p), p) for p in left if all(q in done for q in before[p])]
        t0, first = min(can, key=lambda c: c[0])
        t, p = min((c for c in can if c[1][1] == first[1] and c[0] <= t0 + SLACK),
                   key=lambda c: -work_behind(c[1]))
        left.remove(p)
        free_at[p[1]] = done[p] = t + length[p]
        order[p[1]].append(p[0])
    return order


class Section:

    def __init__(self, head, rest, before=None):
        self.order = order = section_order(head, rest)
        self.before, self.counts = before or {}, {}

        def number(name, items):
            n0 = self.before.get(name, 0)
            self.counts[name] = len(items)
            return {i: n0 + n for n, i in enumerate(items)}

        def of(engine, *kinds):
            return [i for i in order[engine] if i[0] in kinds]

        self.T, self.M, self.S = (number(pair, of("PE", *BANKS[pair])) for pair in "TMS")
        self.O = number("O", [i for i in of("PE", "V") if STARTS[i[3]] == i[3]])
        self.QK = number("QK", of("PE", "qk"))
        self.STATS = number("STATS", of("DVE", "st0", "sh", "gate"))
        self.GELUS = number("GELUS", of("ACT", "w1"))
        self.FFNS = number("FFNS", of("DVE", "w2"))

    def o_of(self, l, b, k):
        return self.O["V", l, b, STARTS[k]]

    def earlier(self, name):
        n = self.before.get(name, 0)
        return [n - 2, n - 1]


HEAD = Section(True, False)
BODY = Section(True, True, HEAD.counts)
TAIL = Section(False, True, HEAD.counts)
T_A_USES, M_A_USES, S_A_USES, O_A_USES, QK_EVENTS, STATS_EVENTS, GELU_EVENTS, FFN_EVENTS = (
    BODY.counts[name] for name in ("T", "M", "S", "O", "QK", "STATS", "GELUS", "FFNS"))
assert (T_A_USES | M_A_USES | S_A_USES | O_A_USES | QK_EVENTS) % 2 == 0
T_P_USES = 2
B_UNITS = 24
TURN_LAG, VALUE_LAG, O_LAG = 2, 3, 4
WEIGHT_STEPS = (3, 10, 15, 21)


def b_extras(k, first, last):
    extras = [("weights", j) for j, at in enumerate(WEIGHT_STEPS) if at == k]
    extras += [("prep", 1)] * (k == 2) + [("prep", 2)] * (k == 16 and not last)
    extras += [("ctx", -1)] * (k == 5 and not first) + [("out", -1)] * (k == 6 and not first)
    extras += [("ctx", 0)] * (k == 17) + [("out", 0)] * (k == 18) + [("rank", 0)] * (k == 8 and first)
    if k == B_UNITS + O_LAG - 1:
        extras += [("ctx", 1), ("out", 1)]
    return extras


class AttentionTurn:

    def __init__(self, first, last, before):
        self.first, self.last, self.before = first, last, before
        self.steps = range(B_UNITS + (O_LAG if last else 0))
        uses = {"T": [], "M": []}
        for k in self.steps:
            if self.unit(k, TURN_LAG) is not None:
                uses["T"].append(("T", k - TURN_LAG))
            for kind, b in b_extras(k, first, last):
                pair, parts = {"prep": ("M", ("qk", "v")), "weights": ("T", ("w13", "w2")), "ctx": ("T", ("ctx",)),
                               "out": ("M", ("out",)), "rank": ("M", ("ranks", "counts"))}[kind]
                uses[pair] += [(part, b) for part in parts]
        self.T, self.M = ({u: before[pair] + n for n, u in enumerate(uses[pair])} for pair in "TM")

    def unit(self, k, lag):
        u = k - lag
        return u if u < B_UNITS and (u >= 0 or not self.first) else None

    def earlier(self, pair):
        return [self.before[pair] - 2, self.before[pair] - 1]


B_FIRST = AttentionTurn(True, False, {"T": 0, "M": 2})
B_MID, B_LAST = (AttentionTurn(False, last, {"T": len(B_FIRST.T), "M": 2 + len(B_FIRST.M)}) for last in (False, True))
T_B_USES, M_B_USES = len(B_MID.T), len(B_MID.M)
S_B_USES, O_B_USES = B_UNITS, 16
LAST_TURNED = B_MID.before["T"] + T_B_USES - B_MID.T["T", B_UNITS - VALUE_LAG]
T_B_ALL, M_B_ALL = (b + len(first) + 2 * len(mid) + len(last) for b, first, mid, last in
                    ((0, B_FIRST.T, B_MID.T, B_LAST.T), (2, B_FIRST.M, B_MID.M, B_LAST.M)))
assert (T_B_USES | M_B_USES | T_B_ALL | M_B_ALL) % 2 == 0
GATE_LAG, DOWN_LAG, NORM_LAG, OUT_LAG = 2, 3, 4, 5


def c_uses(first, last):
    order = []
    for j in range(CG + (OUT_LAG if last else 0)):
        if (j >= GATE_LAG or not first) and j - GATE_LAG < CG:
            order.append(("g", j - GATE_LAG))
        if j in (1, 3):
            order.append(("x", CG // 2 + j - 1))
        if j in (5, 7) and not last:
            order.append(("x", CG + j - 5))
    return {use: n for n, use in enumerate(order)}


C_USES = [c_uses(i == 0, i == C_TURNS - 1) for i in (0, 1, C_TURNS - 1)]
T_FIRST_USES, T_C_USES = len(C_USES[0]), len(C_USES[1])
assert T_FIRST_USES % 2 == T_C_USES % 2 == 0
PREVIOUS_GATE = C_USES[1]["g", CG - DOWN_LAG] - T_C_USES
assert PREVIOUS_GATE == C_USES[0]["g", CG - DOWN_LAG] - T_FIRST_USES
T_A0 = T_P_USES // 2
T_B0 = T_A0 + TURNS * T_A_USES // 2
T_X0 = T_B0 + T_B_ALL // 2
T_C0 = T_X0 + 1
M_B0 = TURNS * M_A_USES // 2
M_C0 = M_B0 + M_B_ALL // 2
S_B0 = TURNS * S_A_USES // 2
O_B0 = TURNS * O_A_USES // 2
O_C0 = O_B0 + TURNS * O_B_USES // 2
PV_C0 = S_B0 + TURNS * S_B_USES // 2
D_A_STEPS, D_B_STEPS, P_A_STEPS = 56, 40, 24


D_HEAD_STEPS, P_HEAD_STEPS = 1, 5


def gated_layers(nc, ins, out):
    ctx = ExitStack()
    with ctx:
        def sb(name, shape, dt=F32):
            return ctx.enter_context(nc.sbuf_tensor(name, shape, dt))

        def sem(name):
            return ctx.enter_context(nc.semaphore(name))

        def pair(name):
            return Pair(ctx, nc, name)

        Tb, Mb, Sb, Ob = ([ctx.enter_context(nc.psum_tensor(f"ps{n}{i}", [P, 512], F32)) for i in range(2)]
                          for n in "TMSO")
        t_full, t_free = pair("t_full"), pair("t_free")
        m_full, m_free = pair("m_full"), pair("m_free")
        s_full, s_free = pair("s_full"), pair("s_free")
        o_free = pair("o_free")
        exp_done = pair("exp_done")
        sq_done, ss_done = pair("sq_done"), pair("ss_done")
        rope_sum, rope_done = pair("rope_sum"), pair("rope_done")

        XG = nc.dram_tensor("xg_scratch", (CT * P, D), F32, kind="Internal").ap()
        YG = nc.dram_tensor("yg_scratch", (CT * P, D), F32, kind="Internal").ap()

        XALL = sb("XALL", [P, NT, D])
        XN1ALL = sb("XN1ALL", [P, NT, D])
        XNT1ALL = sb("XNT1ALL", [P, NT * P])
        S1ALL = sb("S1ALL", [P, NT, D])
        LG = sb("LG", [P, NT, E])
        ident = sb("ident", [P, P])
        identb = sb("identb", [P, P], BF16)
        mask0 = {0: sb("maskl0", [P, 512], BF16), 1: sb("maskc0", [P, 512], BF16)}
        mask1 = {0: sb("maskl1", [P, 512], BF16), 1: sb("maskc1", [P, 512], BF16)}
        shift = sb("shift", [P, P])
        carry = sb("carry", [P, P])
        trib = sb("trib", [P, P], BF16)
        onesb = sb("onesb", [P, P], BF16)
        powm = sb("powm", [P, 16])
        zeros = sb("zeros", [P, 512])
        SE = sb("SE", [P, 2, 512])
        PR = sb("PR", [P, 2, 512])
        PT = sb("PT", [P, 2, 512])
        MX = sb("MX", [P, 2, 4])
        RC = sb("RC", [P, 2, 4])
        ST = sb("ST", [P, GT, 2, 6])
        MV = sb("MV", [P, GT, 2])
        RS = sb("RS", [P, GT])
        WQT = sb("WQT", [P, P])
        WKT = sb("WKT", [P, P])
        headm = sb("headm", [P, E])
        WVT = sb("WVT", [P, P])
        WOT = sb("WOT", [P, P])
        RWT = sb("RWT", [P, E])
        borow = sb("borow", [P, D])
        rbrow = sb("rbrow", [P, E])
        GB = sb("GB", [P, E, D])
        BB = sb("BB", [P, E, D])

        ARENA = 33900
        arena = sb("arena", [P, ARENA])
        at = [0]

        def carve(*shape):
            n = 1
            for s in shape:
                n *= s
            v = arena[:, at[0]:at[0] + n]
            at[0] += n
            assert at[0] <= ARENA, at[0]
            if len(shape) == 1:
                return v
            names = "abcd"[:len(shape)]
            return v.rearrange(f"p ({' '.join(names)}) -> p {' '.join(names)}",
                               **{c: s for c, s in zip(names[1:], shape[1:])})

        S0 = carve(GT, D)
        XC = carve(GT, D)
        XNT = carve(TOK)
        XN1T = carve(TOK)
        HT = carve(2, SEQ)
        VA = carve(GT, 8, DH + 1)
        QT = carve(2, 4, TOK)
        KT = carve(4, TOK)
        SQ = carve(2, 512)
        R1 = carve(4, 512)
        R2 = carve(2, 512)
        SS = carve(4, 8)
        RN = carve(4, 8)
        OS = carve(GT, 512)
        OT = carve(GT, 512)
        HN = carve(GT, D)
        HNT = carve(TOK)
        GG = carve(2, SEQ)
        HG = carve(3, 512)
        EG = carve(GT, D)
        EA = carve(SEQ)
        AA = carve(SEQ)
        UU = carve(SEQ)
        SC = carve(SEQ)
        TC = carve(SEQ)
        CS = carve(SEQ)
        WABC = carve(3, NS)
        WD = carve(D)
        WYP = carve(2, D)
        ybrow = carve(2, D)
        bab = carve(4)
        WQKV = carve(LAYERS, 3, INNER)
        WO = carve(LAYERS, 4, D)
        W1 = carve(LAYERS, 2 * HID)
        W2 = carve(LAYERS, 3, D)
        lgc = carve(LAYERS, 2)
        b1c = carve(LAYERS, 2, 3)
        b2row = carve(LAYERS, D)
        ROPE = carve(2, 2, 2, DH)
        QKS = carve(LAYERS, 2, DH)
        RT = carve(LAYERS * 2, 2, 2, DH)
        WRAW = carve(5, P)
        at[0] = 0
        W13 = carve(E, 2 * FE)
        W2T = carve(E, 2 * D)
        after_weights = at[0]
        WST = carve(2, 3, 2 * D)
        XQ = carve(TOK)
        QT1 = carve(E, TOK)
        KT1 = carve(TOK)
        VA1 = carve(GT, E, DK1 + 1)
        XS = carve(TOK)
        CTX = carve(GT, D)
        CTXT = carve(2, SEQ)
        MAXV = carve(NT, 8)
        ONEH = carve(2, NT, E)
        MIDX = carve(NT, 8)
        MIF = carve(2, NT)
        GW = carve(2, NT)
        CNT = carve(2, NT, E)
        CUM = carve(2, E, NT)
        IOT = carve(E, NT)
        IOTS = carve(E, NT)
        IOTJ = carve(CT, E)
        KEEP = carve(E, NT)
        NTI = carve(4, E)
        PF = carve(2, NT)
        ENDS = carve(CT, E)
        IOTI, IOTI2, IOTI3 = (carve(n).bitcast(I32) for n in (E * NT, E * NT, CT * E))
        EF = carve(CT)
        MB = carve(128)
        POSU = sb("POSU", [P, 2, NT], U32)
        EID = sb("EID", [P, CT], I32)
        WGT = sb("WGT", [P, 2, NT])
        ONEH_B = MB.bitcast(BF16)
        at[0] = after_weights
        XGS = carve(2, CG // 2, D)
        XGT = carve(CG * P)
        HS = carve(2, FE)
        GS = carve(2, FE)
        GTT = carve(2, FE)
        YN = carve(2, D)
        YO = carve(4, D)
        YAB = carve(NT, 2, D)
        G2 = carve(GT, D)
        G3 = carve(GT, D)
        OUTB = carve(OUT_TILES, D)

        ld_x, ld_first, ld_a, ld_l1, ld_raw = (sem(f"ld_{n}") for n in ("x", "first", "a", "l1", "raw"))
        ld_w = pair("ld_w")
        zeroed, scattered = sem("zeroed"), sem("scattered")
        gathered = [sem(f"gathered{t}") for t in range(NT)]
        ld_g, st_y, st_out = [sem("ld_g0"), sem("ld_g1")], pair("st_y"), pair("st_out")
        pool_consts, dve_consts, tables = sem("pool_consts"), sem("dve_consts"), sem("tables")
        a_over, b_over = sem("a_over"), sem("b_over")
        dve_settled, pool_settled, sp_settled = sem("dve_settled"), sem("pool_settled"), sem("sp_settled")
        dstep, pstep = sem("dstep"), sem("pstep")
        stats_done, rstd_done = sem("stats_done"), sem("rstd_done")
        xn_ready, ea_done, cs_done = sem("xn_ready"), sem("ea_done"), sem("cs_done")
        ffn_added, gate_done = sem("ffn_added"), sem("gate_done")
        xn1_ready, xn1_kept, gelu_done = sem("xn1_ready"), sem("xn1_kept"), sem("gelu_done")
        onehot, gap_done, gap_exp = sem("onehot"), sem("gap_done"), sem("gap_exp")
        pos_done, xs_ready, xq_ready = sem("pos_done"), sem("xs_ready"), sem("xq_ready")
        c_silu, c_yo, c_stats, c_rstd = pair("c_silu"), pair("c_yo"), pair("c_stats"), pair("c_rstd")
        pv_done, iota_raw, iotas = pair("pv_done"), sem("iota_raw"), sem("iotas")
        moe_in, silu_done, out_ready = sem("moe_in"), sem("silu_done"), sem("out_ready")
        q_masked = [sem("q_masked0"), sem("q_masked1")]

        def masked(turn, n):
            return turn * E + (n + 1)

        ENGINES = 4

        XG3 = XG.rearrange("(j p) d -> j p d", p=P)
        YG3 = YG.rearrange("(j p) d -> j p d", p=P)

        def stage(lanes, dv, q, k, v, o, masks):
            units = []
            for b in range(2):
                for lane in range(lanes):
                    units.append((b, 0, lane, range(4)))
                for lane in range(lanes):
                    for h in range(2):
                        units.append((b, 1, lane, range(2 * h, 2 * h + 2)))
            return dict(lanes=lanes, dv=dv, q=q, k=k, v=v, o=o, masks=masks, units=units)

        ATT0 = stage(2, DH, lambda lane, s: QT[:, lane, s, :], lambda s: KT[:, s, :], VA, OS, (mask0[0], mask1[0]))
        ATT1 = stage(4, DK1, lambda lane, s: QT1[:, 4 * s + lane, :], lambda s: KT1, VA1, CTX, (mask0[1], mask1[1]))

        def unit_of(b, k):
            return UNITS * b + k

        def loop_b(engine, run):
            run(B_FIRST, 0, T_B0, M_B0)
            with engine.Fori(1, TURNS - 1) as it:
                run(B_MID, it, T_B0 - T_B_USES // 2 + it * (T_B_USES // 2), M_B0 - M_B_USES // 2 + it * (M_B_USES // 2))
            run(B_LAST, TURNS - 1, T_B0 + (TURNS - 2) * (T_B_USES // 2), M_B0 + (TURNS - 2) * (M_B_USES // 2))

        def lane_heads(n):
            return 4 * (n % 4) + n // 4

        def loop_c(engine, run):
            run(0, C_USES[0], T_C0, True, False)
            with engine.Fori(1, C_TURNS - 1) as i:
                run(i, C_USES[1], T_C0 + T_FIRST_USES // 2 - T_C_USES // 2 + i * (T_C_USES // 2), False, False)
            i = C_TURNS - 1
            run(i, C_USES[2], T_C0 + T_FIRST_USES // 2 + (i - 1) * (T_C_USES // 2), False, True)

        def tiles_of(lag, first, last):
            return [(j, j - lag) for j in range(CG + (OUT_LAG if last else 0))
                    if (j >= lag or not first) and j - lag < CG]

        def loop_a(engine, run, after_head):
            run(HEAD, 0, 0)
            after_head()
            with engine.Fori(0, TURNS - 1) as it:
                run(BODY, it, it + 1)
            run(TAIL, TURNS - 1, None)

        def o_use(g, u):
            b, qt, lane, slots = g["units"][u]
            return (2 * b + qt) * g["lanes"] + lane

        small_loads = []
        first_loads = []
        for i, w in enumerate(("Wa", "Wb", "Wc")):
            small_loads.append((WABC[:, i, :], ins[f"L0_attn_{w}"]))
        for i, w in enumerate(("ba", "bb", "bc")):
            for b in range(2):
                small_loads.append((bab[NS * b:NS * b + NS, i:i + 1], ins[f"L0_attn_{w}"].unsqueeze(1)))
        small_loads.append((WD, ins["L0_attn_Wd"]))
        for b in range(2):
            small_loads.append((WYP[NS * b:NS * b + NS, b, :], ins["L0_attn_Wy"]))
        small_loads.append((ybrow[:, 0, :], ins["L0_attn_by"].partition_broadcast(P)))
        small_loads.append((ybrow[:, 1, :], ins["L0_attn_bd"].partition_broadcast(P)))
        for k in range(2):
            for x in range(2):
                first_loads.append((ROPE[:, k, x], ins["rope"][k, x].rearrange("(t p) d -> p t d", p=P)))
        for l in range(LAYERS):
            (small_loads if l else first_loads).append((WQKV[:, l].rearrange("p s n -> p (s n)"),
                                                        ins["L0_ffn_wqkv"][l]))
            first_loads.append((QKS[:, l, 0, :], ins["L0_ffn_q_scale"][l].partition_broadcast(P)))
            first_loads.append((QKS[:, l, 1, :], ins["L0_ffn_k_scale"][l].partition_broadcast(P)))
            small_loads.append((WO[:, l], ins["L0_ffn_wo"][l].rearrange("(c p) n -> p c n", p=P)))
            small_loads.append((W1[:, l, :], ins["L0_ffn_w1"][l]))
            small_loads.append((W2[:, l, 0:2, :], ins["L0_ffn_w2"][l][0:256].rearrange("(c p) n -> p c n", p=P)))
            small_loads.append((W2[0:85, l, 2, :], ins["L0_ffn_w2"][l][256:HID]))
            small_loads.append((lgc[:, l, 0:1], ins["L0_ffn_ln_g"][l].unsqueeze(1)))
            small_loads.append((lgc[:, l, 1:2], ins["L0_ffn_ln_b"][l].unsqueeze(1)))
            for h in range(2):
                for c, (f, m) in enumerate(HC):
                    small_loads.append((b1c[0:m, l, h, c:c + 1],
                                        ins["L0_ffn_b1"][l][h * HID + f:h * HID + f + m].unsqueeze(1)))
            small_loads.append((b2row[:, l, :], ins["L0_ffn_b2"][l].partition_broadcast(P)))
        LOADED_A, LOADED_FIRST = 16 * len(small_loads), 16 * len(first_loads)
        POOL_CONSTS = 13 + 6 + 4 + 3

        block = ctx.enter_context(nc.Block())

        @block.sync
        def _(sp):
            st_y.begin(sp, 16)
            sp.dma_start(XALL[:], ins["L0_attn_x"].rearrange("b (t p) d -> p (b t) d", p=P)).then_inc(ld_x, 16)
            for dst, src in first_loads:
                sp.dma_start(dst, src).then_inc(ld_first, 16)
            for i, w in enumerate(("Wq", "Wk", "Wv", "Wo")):
                sp.dma_start(WRAW[:, i, :], ins[f"L1_attn_{w}"]).then_inc(ld_raw, 16)
            sp.dma_start(WRAW[0:E, 4, :], ins["L1_ffn_router_w"]).then_inc(ld_raw, 16)
            sp.wait_ge(dve_consts, 1)
            for dst, src in small_loads:
                sp.dma_start(dst, src).then_inc(ld_a, 16)
            sp.dma_start(borow[:], ins["L1_attn_bo"].partition_broadcast(P)).then_inc(ld_l1, 16)
            sp.dma_start(rbrow[:], ins["L1_ffn_router_b"].partition_broadcast(P)).then_inc(ld_l1, 16)
            sp.dma_start(GB[:].rearrange("p e d -> p (e d)"),
                         ins["L1_ffn_ln_g"].rearrange("e d -> (e d)").partition_broadcast(P)).then_inc(ld_l1, 16)
            sp.dma_start(BB[:].rearrange("p e d -> p (e d)"),
                         ins["L1_ffn_ln_b"].rearrange("e d -> (e d)").partition_broadcast(P)).then_inc(ld_l1, 16)
            sp.wait_ge(pool_consts, POOL_CONSTS)
            for j in range(0, CT, 4):
                sp.dma_start(XG3[j:j + 4].rearrange("j p d -> p j d"),
                             zeros[:].rearrange("p (j d) -> p j d", j=4)).then_inc(zeroed, 16)
            sp.wait_ge(a_over, ENGINES)
            def turn(sec, it, ht, hm):
                for j in range(4):
                    p = j % 2
                    if j >= 2 or not sec.first:
                        n = sec.T["w2", j - 2] if j >= 2 else \
                            B_MID.T["w2", j + 2] - B_MID.before["T"] - T_B_USES + sec.before["T"]
                        sp.wait_ge(t_full.sem(n), t_full.did(ht, n))
                        sp.sem_inc(sp_settled, 1)
                    for m, w in enumerate(("w1", "w3")):
                        sp.dma_start(WST[:, p, m, :].rearrange("p (k d) -> p k d", k=2),
                                     ins[f"L1_ffn_{w}"][it * 4 + j].rearrange("(k p) d -> p k d", p=P))\
                            .then_inc(ld_w.sem(p), 16)
                    sp.dma_start(WST[:, p, 2, :], ins["L1_ffn_w2"][it * 4 + j]).then_inc(ld_w.sem(p), 16)

            loop_b(sp, turn)
            sp.wait_ge(scattered, 16 * 2 * NT)
            sp.wait_ge(b_over, ENGINES)
            def load_tiles(half, j0):
                sp.dma_start(XGS[:, half], XG3[j0].rearrange("j p d -> p j d")).then_inc(ld_g[half], 16)

            for half in range(2):
                load_tiles(half, slice(half * CG // 2, (half + 1) * CG // 2))

            def turn(i, uses, ht, first, last):
                def store_two(tile):
                    for j in (tile, tile + 1):
                        sp.wait_ge(c_yo.sem(j), c_yo.did(i * (CG // 2), j))
                        sp.sem_inc(sp_settled, 1)
                    p = tile // 2
                    sp.dma_start(YG3[bass.ds(i * CG + tile, 2)].rearrange("j p d -> p j d"),
                                 YO[:, tile % 4:tile % 4 + 2, :]).then_inc(st_y.sem(p), 16)

                for half in range(2):
                    if not last:
                        for n in ((uses["x", 4], uses["x", 6]) if half else (-2, -1) if first else (-4, -1)):
                            sp.wait_ge(t_full.sem(n), t_full.did(ht, n))
                            sp.sem_inc(sp_settled, 1)
                        load_tiles(half, bass.ds(i * CG + (CG + half * CG // 2), CG // 2))
                    for tile in (-2, 0) if half else (-6, -4):
                        if tile >= 0 or not first:
                            store_two(tile)
                if last:
                    for tile in (2, 4, 6):
                        store_two(tile)

            loop_c(sp, turn)
            for n in range(NT // 2):
                sp.wait_ge(out_ready, 2 * n + 2)
                sp.dma_start(out.rearrange("b (t p) d -> p (b t) d", p=P)[:, 2 * n:2 * n + 2, :],
                             OUTB[:, (2 * n) % OUT_TILES:(2 * n) % OUT_TILES + 2, :]).then_inc(st_out.sem(n), 16)
            for p in range(2):
                sp.wait_ge(st_out.sem(p), 16 * NT // 4)

        @block.tensor
        def _(pe):
            def mm(o, lhsT, rhs, start=True, stop=True):
                return nc.tensor.matmul(o, lhsT, rhs, start=start, stop=stop)

            for events in (t_full, m_full, s_full, pv_done):
                events.begin(pe)

            def t_open(ht, n):
                pe.wait_ge(t_free.sem(n), t_free.reuse(ht, n))
                return Tb[n % 2]

            def m_open(hm, n, *read):
                for e in latest(n - 2, *read):
                    pe.wait_ge(m_free.sem(e), m_free.did(hm, e))
                return Mb[n % 2]

            def scores(g, u, hs, n):
                b, qt, lane, slots = g["units"][u]
                pe.wait_ge(s_free.sem(n), s_free.reuse(hs, n))
                bank, keys = Sb[n % 2], P * (qt + 1)
                mm(bank[:], identb[:], g["masks"][qt][:], True, False)
                for i, s in enumerate(slots):
                    last = mm(bank[:, i * keys:(i + 1) * keys],
                              g["q"](lane, s)[:, (2 * b + qt) * P:(2 * b + qt + 1) * P],
                              g["k"](s)[:, 2 * b * P:2 * b * P + keys], False, i == len(slots) - 1)
                last.then_inc(s_full.sem(n), 1)

            def turn_probs(ht, n, hs, m):
                pe.wait_ge(exp_done.sem(m), exp_done.did(hs, m))
                bank = t_open(ht, n)
                for c in range(4):
                    last = nc.tensor.transpose(bank[:, c * P:(c + 1) * P], PR[:, m % 2, c * P:(c + 1) * P], ident[:])
                last.then_inc(t_full.sem(n), 1)

            def values(g, u, ht, n, hs, m, ho, o):
                b, qt, lane, slots = g["units"][u]
                if slots[0] == 0:
                    pe.wait_ge(o_free.sem(o), o_free.reuse(ho, o))
                pe.wait_ge(t_free.sem(n), t_free.did(ht, n))
                c, w = 0, g["dv"] + 1
                for s in slots:
                    head = g["lanes"] * s + lane
                    for kt in range(qt + 1):
                        last = mm(Ob[o % 2][:, s * w:(s + 1) * w], PT[:, m % 2, c * P:(c + 1) * P],
                                  g["v"][:, 2 * b + kt, head, :], kt == 0, kt == qt)
                        c += 1
                last.then_inc(pv_done.sem(m), 1)

            pe.wait_ge(ld_raw, 16 * 5)
            pe.wait_ge(pool_consts, POOL_CONSTS)
            for c in range(4):
                last = nc.tensor.transpose(Tb[0][:, c * P:(c + 1) * P], WRAW[:, c, :], ident[:])
            last.then_inc(t_full.sem(0), 1)
            nc.tensor.transpose(Tb[1][:, 0:E], WRAW[0:E, 4, :], ident[0:E, 0:E]).then_inc(t_full.sem(1), 1)
            pe.wait_ge(ld_first, LOADED_FIRST)
            pe.wait_ge(dve_consts, 2)

            def run(sec, it, ahead):
                ht, hm = T_A0 + it * (T_A_USES // 2), it * (M_A_USES // 2)
                hs, ho, hq = it * (S_A_USES // 2), it * (O_A_USES // 2), it * (QK_EVENTS // 2)

                def copied(*items, earlier=False):
                    for n in latest(*(sec.T[i] for i in items), *(sec.earlier("T") if earlier else [])):
                        pe.wait_ge(t_free.sem(n), t_free.did(ht, n))

                for item in sec.order["PE"]:
                    kind, *of = item
                    if kind == "x":
                        l, b = of
                        if l == 0:
                            pe.wait_ge(xn_ready, (it if b else ahead) * 2 + (b + 1))
                        else:
                            pe.wait_ge(ffn_added, it * FFN_EVENTS + (sec.FFNS["w2", 0, b] + 1))
                        bank = t_open(ht, sec.T[item])
                        for t in range(2):
                            last = nc.tensor.transpose(bank[:, t * P:(t + 1) * P], XC[:, 2 * b + t, :], ident[:])
                        last.then_inc(t_full.sem(sec.T[item]), 1)
                    if kind == "ab":
                        copied(("x", 0, 1), earlier=True)
                        bank = m_open(hm, sec.M[item])
                        for i in range(2):
                            for b in range(2):
                                last = mm(bank[NS * b:NS * b + NS, i * SEQ:(i + 1) * SEQ], WABC[:, i, :],
                                          XNT[:, b * SEQ:(b + 1) * SEQ])
                        last.then_inc(m_full.sem(sec.M[item]), 1)
                    if kind == "c":
                        bank = m_open(hm, sec.M[item])
                        for b in range(2):
                            last = mm(bank[NS * b:NS * b + NS, 0:SEQ], WABC[:, 2, :], XNT[:, b * SEQ:(b + 1) * SEQ])
                        last.then_inc(m_full.sem(sec.M[item]), 1)
                    if kind == "y":
                        pe.wait_ge(cs_done, it + 1)
                        bank = m_open(hm, sec.M[item])
                        for t in range(GT):
                            mm(bank[:, t * P:(t + 1) * P], CS[0:2 * NS, (t % 2) * P:(t % 2 + 1) * P],
                               WYP[0:2 * NS, t // 2, :], True, False)
                            last = mm(bank[:, t * P:(t + 1) * P], XNT[:, t * P:(t + 1) * P], WD, False, True)
                        last.then_inc(m_full.sem(sec.M[item]), 1)
                    if kind in ("qk", "v"):
                        l, n = of
                        t, i = (n // 2, n % 2) if kind == "qk" else (n, 2)
                        if kind == "qk" and n % 4 == 0:
                            copied(("x", l, t // 2))
                        mm(m_open(hm, sec.M[item])[:], HT[:, t // 2, (t % 2) * P:(t % 2 + 1) * P], WQKV[:, l, i, :])\
                            .then_inc(m_full.sem(sec.M[item]), 1)
                    if kind == "qkT":
                        l, n = of
                        m, u = sec.QK["qk", l, n], sec.T[item]
                        pe.wait_ge(rope_done.sem(m), rope_done.did(hq, m))
                        bank = t_open(ht, u)
                        for c in range(4):
                            last = nc.tensor.transpose(bank[:, c * P:(c + 1) * P], R1[:, m % 4, c * P:(c + 1) * P],
                                                       ident[:])
                        last.then_inc(t_full.sem(u), 1)
                    if kind == "S":
                        l, b, k = of
                        if k == 0:
                            if (l, b) == (0, 0):
                                copied(earlier=True)
                            else:
                                copied(("qkT", l, 4 * b + 2), ("qkT", l, 4 * b + 3))
                        scores(ATT0, unit_of(b, k), hs, sec.S[item])
                    if kind == "T":
                        turn_probs(ht, sec.T[item], hs, sec.S["S", *of])
                    if kind == "V":
                        l, b, k = of
                        values(ATT0, unit_of(b, k), ht, sec.T["T", l, b, k], hs, sec.S["S", l, b, k], ho,
                               sec.o_of(l, b, k))
                    if kind == "oT":
                        l, t = of
                        for o in latest(*(sec.o_of(l, t // 2, k) for k in ((0, 1), (2, 4))[t % 2])):
                            pe.wait_ge(o_free.sem(o), o_free.did(ho, o))
                        bank = t_open(ht, sec.T[item])
                        for c in range(4):
                            last = nc.tensor.transpose(bank[:, c * P:(c + 1) * P], OS[:, t, c * P:(c + 1) * P],
                                                       ident[:])
                        last.then_inc(t_full.sem(sec.T[item]), 1)
                    if kind == "wo":
                        l, b = of
                        copied(("oT", l, 2 * b), ("oT", l, 2 * b + 1))
                        bank = m_open(hm, sec.M[item])
                        for t in range(2):
                            for c in range(4):
                                last = mm(bank[:, t * P:(t + 1) * P], OT[:, 2 * b + t, c * P:(c + 1) * P], WO[:, l, c, :],
                                          c == 0, c == 3)
                        last.then_inc(m_full.sem(sec.M[item]), 1)
                    if kind == "sh":
                        l, b = of
                        bank = m_open(hm, sec.M[item], sec.M["wo", l, b])
                        mm(bank[:, 0:64], shift[:], XC[:, 2 * b, 64:D])
                        mm(bank[:, 64:128], shift[:], XC[:, 2 * b + 1, 64:D], True, False)
                        mm(bank[:, 64:128], carry[:], XC[:, 2 * b, 64:D], False, True).then_inc(m_full.sem(sec.M[item]), 1)
                    if kind == "hT":
                        l, b = of
                        n = sec.M["sh", l, b]
                        pe.wait_ge(m_free.sem(n), m_free.did(hm, n))
                        bank = t_open(ht, sec.T[item])
                        for t in range(2):
                            last = nc.tensor.transpose(bank[:, t * P:(t + 1) * P], HN[:, 2 * b + t, :], ident[:])
                        last.then_inc(t_full.sem(sec.T[item]), 1)
                    if kind == "w1":
                        l, b, c = of
                        f, m = HC[c]
                        if c == 0:
                            copied(("hT", l, b))
                        bank = m_open(hm, sec.M[item])
                        for h in (1, 0):
                            last = mm(bank[0:m, (1 - h) * SEQ:(2 - h) * SEQ], W1[:, l, h * HID + f:h * HID + f + m],
                                      HNT[:, b * SEQ:(b + 1) * SEQ])
                        last.then_inc(m_full.sem(sec.M[item]), 1)
                    if kind == "w2":
                        l, b = of
                        bank = m_open(hm, sec.M[item], sec.M["w1", l, b, 2])
                        for t in range(2):
                            for c, (f, m) in enumerate(HC):
                                last = mm(bank[:, t * P:(t + 1) * P], HG[0:m, c, (2 * b + t) * P:(2 * b + t + 1) * P],
                                          W2[0:m, l, c, :], c == 0, c == 2)
                        last.then_inc(m_full.sem(sec.M[item]), 1)
                    if kind == "x1T":
                        b, = of
                        pe.wait_ge(xn1_ready, it * 2 + (b + 1))
                        bank = t_open(ht, sec.T[item])
                        for t in range(2):
                            last = nc.tensor.transpose(bank[:, t * P:(t + 1) * P], HN[:, 2 * b + t, :], ident[:])
                        last.then_inc(t_full.sem(sec.T[item]), 1)
                    if kind == "router":
                        copied(("x1T", 0), ("x1T", 1))
                        bank = m_open(hm, sec.M[item])
                        for t in range(GT):
                            last = mm(bank[:, t * E:(t + 1) * E], XN1T[:, t * P:(t + 1) * P], RWT[:])
                        last.then_inc(m_full.sem(sec.M[item]), 1)

            loop_a(pe, run, lambda: pe.wait_ge(ld_a, LOADED_A))
            pe.drain().then_inc(a_over, 1)
            pe.wait_ge(a_over, ENGINES)

            def turn(sec, it, ht, hm):
                hs, ho = S_B0 + it * (S_B_USES // 2), O_B0 + it * (O_B_USES // 2)

                def read(*ns):
                    for n in latest(*ns):
                        pe.wait_ge(m_free.sem(n), m_free.did(hm, n))

                for k in sec.steps:
                    u = sec.unit(k, 0)
                    if u is not None:
                        b = u // 12
                        if u == 0:
                            read(*sec.earlier("M"))
                        if u == 12:
                            read(sec.M["qk", 1], sec.M["v", 1])
                        if u % 12 < 4:
                            pe.wait_ge(q_masked[b], masked(it, 4 * (u % 12) + 4))
                        scores(ATT1, u, hs, u)
                    u = sec.unit(k, TURN_LAG)
                    if u is not None:
                        turn_probs(ht, sec.T["T", u], hs, u)
                    u = sec.unit(k, VALUE_LAG)
                    if u is not None:
                        n = sec.T["T", u] if ("T", u) in sec.T else sec.before["T"] - LAST_TURNED
                        values(ATT1, u % B_UNITS, ht, n, hs, u, ho, o_use(ATT1, u % B_UNITS) - (O_B_USES if u < 0 else 0))
                    for kind, b in b_extras(k, sec.first, sec.last):
                        if kind == "prep":
                            prepare(sec, it, b, hm)
                        if kind == "weights":
                            p = b % 2
                            pe.wait_ge(ld_w.sem(p), it * 96 + (b // 2 + 1) * 48)
                            n = sec.T["w13", b]
                            bank = t_open(ht, n)
                            for c in range(4):
                                last = nc.tensor.transpose(bank[:, c * P:(c + 1) * P],
                                                           WST[:, p, c // 2, (c % 2) * P:(c % 2 + 1) * P], ident[:])
                            last.then_inc(t_full.sem(n), 1)
                            n = sec.T["w2", b]
                            bank = t_open(ht, n)
                            for c in range(2):
                                last = nc.tensor.transpose(bank[:, c * P:(c + 1) * P],
                                                           WST[:, p, 2, c * P:(c + 1) * P], ident[:])
                            last.then_inc(t_full.sem(n), 1)
                        if kind == "rank":
                            pe.wait_ge(onehot, 1)
                            for part, w in (("ranks", trib), ("counts", onesb)):
                                n = sec.M[part, 0]
                                mm(m_open(hm, n)[:, 0:NT * E], w[:], ONEH_B).then_inc(m_full.sem(n), 1)
                        if kind == "ctx":
                            n = sec.T["ctx", b]
                            for o in (8 * b + 6, 8 * b + 7):
                                pe.wait_ge(o_free.sem(o), o_free.did(ho, o))
                            bank = t_open(ht, n)
                            for t in range(2):
                                last = nc.tensor.transpose(bank[:, t * P:(t + 1) * P], CTX[:, 2 * (b % 2) + t, :],
                                                           ident[:])
                            last.then_inc(t_full.sem(n), 1)
                        if kind == "out":
                            n = sec.T["ctx", b]
                            pe.wait_ge(t_free.sem(n), t_free.did(ht, n))
                            n = sec.M["out", b]
                            bank = m_open(hm, n)
                            for t in range(2):
                                last = mm(bank[:, t * P:(t + 1) * P], CTXT[:, b % 2, t * P:(t + 1) * P], WOT[:])
                            last.then_inc(m_full.sem(n), 1)

            def prepare(sec, it, b, hm):
                turn, b2 = (it + 1, 0) if b == 2 else (it, b)
                uses = (sec.M["qk", b], sec.M["v", b]) if sec else (0, 1)
                bank = m_open(hm, uses[0])
                for i, w in enumerate((WQT, WKT)):
                    last = mm(bank[:, i * SEQ:(i + 1) * SEQ], w[:], XNT1ALL[:, bass.ds(turn * TOK + b2 * SEQ, SEQ)])
                last.then_inc(m_full.sem(uses[0]), 1)
                pe.wait_ge(xs_ready, turn * 2 + (b2 + 1))
                bank = m_open(hm, uses[1])
                for t in range(2):
                    last = mm(bank[:, t * P:(t + 1) * P], XS[:, (2 * b2 + t) * P:(2 * b2 + t + 1) * P], WVT[:])
                last.then_inc(m_full.sem(uses[1]), 1)

            prepare(None, 0, 0, M_B0)
            loop_b(pe, turn)
            pe.drain().then_inc(b_over, 1)
            pe.wait_ge(b_over, ENGINES)

            def turn_tiles(half, t, n, ht):
                bank = t_open(ht, n)
                for j in range(2):
                    last = nc.tensor.transpose(bank[:, j * P:(j + 1) * P], XGS[:, half, t + j, :], ident[:])
                last.then_inc(t_full.sem(n), 1)

            pe.wait_ge(ld_g[0], 16)
            turn_tiles(0, 0, 0, T_X0)
            turn_tiles(0, 2, 1, T_X0)

            def turn(i, uses, ht, first, last):
                hm, ho = M_C0 + i * (CG // 2), O_C0 + i * (CG // 2)
                gates, downs = (dict(tiles_of(lag, first, last)) for lag in (GATE_LAG, DOWN_LAG))

                experts = {}

                def expert_ahead(tile):
                    if tile not in experts and tile < CG and (tile >= 0 or not first):
                        experts[tile] = pe.value_load(EID[0:1, bass.ds(i * CG + tile, 1)], min_val=0, max_val=E - 1)

                expert_ahead(0)
                expert_ahead(-DOWN_LAG)
                for j in range(CG + (OUT_LAG if last else 0)):
                    if j in gates:
                        tile = gates[j]
                        n = uses["g", tile]
                        pe.wait_ge(m_free.sem(tile), m_free.did(hm, tile))
                        bank = t_open(ht, n)
                        for c in range(2):
                            last_t = nc.tensor.transpose(bank[:, c * P:(c + 1) * P],
                                                         GS[:, tile % 2, c * P:(c + 1) * P], ident[:])
                        last_t.then_inc(t_full.sem(n), 1)
                    if j < CG:
                        if j % 2 == 0:
                            n = uses["x", j] if j >= 4 else ((-2, -1) if first else (-4, -1))[j // 2]
                            pe.wait_ge(t_free.sem(n), t_free.did(ht, n))
                        mm(m_open(hm, j)[:], XGT[:, j * P:(j + 1) * P], W13[:, experts[j], :])\
                            .then_inc(m_full.sem(j), 1)
                        expert_ahead(j + 1)
                        expert_ahead(j + 1 - DOWN_LAG)
                    if j in (1, 3):
                        if j == 1:
                            pe.wait_ge(ld_g[1], i * 16 + 16)
                        turn_tiles(1, j - 1, uses["x", j + 3], ht)
                    if j in (5, 7) and not last:
                        if j == 5:
                            pe.wait_ge(ld_g[0], i * 16 + 32)
                        turn_tiles(0, j - 5, uses["x", j + 3], ht)
                    if j in downs:
                        tile = downs[j]
                        n = uses["g", tile] if ("g", tile) in uses else PREVIOUS_GATE
                        pe.wait_ge(t_free.sem(n), t_free.did(ht, n))
                        pe.wait_ge(o_free.sem(tile), o_free.reuse(ho, tile))
                        for c in range(2):
                            last_t = mm(Ob[tile % 2][:, 0:D], GTT[:, tile % 2, c * P:(c + 1) * P],
                                        W2T[:, experts[tile], c * D:(c + 1) * D], c == 0, c == 1)
                        last_t.then_inc(pv_done.sem(tile), 1)

            loop_c(pe, turn)

        @block.scalar
        def _(act):
            def act_fn(o, i, f, **kw):
                return nc.scalar.activation(o, i, f, **kw)

            for events in (t_free, exp_done, sq_done, c_silu):
                events.begin(act)

            def exponentials(hs, n):
                act.wait_ge(s_free.sem(n), s_free.did(hs, n))
                act_fn(PR[:, n % 2, :], SE[:, n % 2, :], ACT.Exp).then_inc(exp_done.sem(n), 1)

            def keep_probs(ht, n, hs, m):
                act.wait_ge(t_full.sem(n), t_full.did(ht, n))
                act.wait_ge(pv_done.sem(m), pv_done.reuse(hs, m))
                act_fn(PT[:, m % 2, :], Tb[n % 2][:], ACT.Copy).then_inc(t_free.sem(n), 1)

            act.wait_ge(t_full.sem(0), t_full.did(0, 0))
            for i, w in enumerate((WQT, WKT)):
                act_fn(w[:], Tb[0][:, i * P:(i + 1) * P], ACT.Copy)
            act_fn(WVT[:], Tb[0][:, 2 * P:3 * P], ACT.Copy)
            act_fn(WOT[:], Tb[0][:, 3 * P:4 * P], ACT.Copy).then_inc(t_free.sem(0), 1)
            act.wait_ge(t_full.sem(1), t_full.did(0, 1))
            act_fn(RWT[:], Tb[1][:, 0:E], ACT.Copy).then_inc(t_free.sem(1), 1)
            act.wait_ge(dve_consts, 2)

            def run(sec, it, ahead):
                ht, hm = T_A0 + it * (T_A_USES // 2), it * (M_A_USES // 2)
                hs, hq = it * (S_A_USES // 2), it * (QK_EVENTS // 2)

                def from_t(item):
                    n = sec.T[item]
                    act.wait_ge(t_full.sem(n), t_full.did(ht, n))
                    return Tb[n % 2], t_free.sem(n)

                def from_m(item):
                    n = sec.M[item]
                    act.wait_ge(m_full.sem(n), m_full.did(hm, n))
                    return Mb[n % 2], m_free.sem(n)

                for item in sec.order["ACT"]:
                    kind, *of = item
                    if kind == "x":
                        l, b = of
                        bank, free = from_t(item)
                        if l == 0:
                            if sec is BODY and b == 0:
                                n = sec.M["y",]
                                act.wait_ge(m_full.sem(n), m_full.did(hm, n))
                            act_fn(XNT[:, b * SEQ:(b + 1) * SEQ], bank[:, 0:SEQ], ACT.Copy)
                        act_fn(HT[0:64, b], bank[0:64, 0:SEQ], ACT.Copy)
                        act_fn(HT[64:P, b, 1:SEQ], bank[64:P, 0:SEQ - 1], ACT.Copy).then_inc(free, 1)
                    if kind == "ab":
                        bank, free = from_m(item)
                        act_fn(EA[0:2 * NS], bank[0:2 * NS, 0:SEQ], ACT.Exp, scale=-1.0,
                               bias=bab[0:2 * NS, 3:4]).then_inc(ea_done, 1)
                    if kind == "c":
                        bank, free = from_m(item)
                        act_fn(TC[0:2 * NS], bank[0:2 * NS, 0:SEQ], ACT.Tanh, bias=bab[0:2 * NS, 2:3])\
                            .then_inc(free, 1)
                    if kind == "qk":
                        m = sec.QK[item]
                        bank, free = from_m(item)
                        act.wait_ge(ss_done.sem(m), ss_done.reuse(hq, m))
                        act_fn(SQ[:, m % 2, :], bank[:], ACT.Square).then_inc(sq_done.sem(m), 1)
                    if kind == "v":
                        l, t = of
                        bank, free = from_m(item)
                        act_fn(VA[:, t, :, 0:DH], bank[:].rearrange("p (h d) -> p h d", h=8), ACT.Copy)\
                            .then_inc(free, 1)
                    if kind == "qkT":
                        l, n = of
                        bank, free = from_t(item)
                        ts = slice(n // 2 * P, (n // 2 + 1) * P)
                        if n % 2 == 0:
                            for lane in range(2):
                                r = slice(DH * lane, DH * lane + DH)
                                last = act_fn(QT[r, lane, :, ts], bank[r, :].rearrange("p (c t) -> p c t", c=4),
                                              ACT.Copy)
                        else:
                            last = act_fn(KT[:, :, ts], bank[:].rearrange("p (c t) -> p c t", c=4), ACT.Copy)
                        last.then_inc(free, 1)
                    if kind == "T":
                        keep_probs(ht, sec.T[item], hs, sec.S["S", *of])
                    if kind == "S":
                        exponentials(hs, sec.S[item])
                    if kind == "oT":
                        l, t = of
                        bank, free = from_t(item)
                        act_fn(OT[:, t, :], bank[:], ACT.Copy).then_inc(free, 1)
                    if kind == "hT":
                        l, b = of
                        bank, free = from_t(item)
                        act_fn(HNT[:, b * SEQ:(b + 1) * SEQ], bank[:, 0:SEQ], ACT.Identity,
                               scale=lgc[:, l, 0:1], bias=lgc[:, l, 1:2]).then_inc(free, 1)
                    if kind == "w1":
                        l, b, c = of
                        g, m = sec.GELUS[item], HC[c][1]
                        bank, free = from_m(item)
                        if g >= 2:
                            n = next(sec.M[i] for i in sec.GELUS if sec.GELUS[i] == g - 2)
                            act.wait_ge(m_free.sem(n), m_free.did(hm, n))
                        act_fn(GG[0:m, g % 2, :], bank[0:m, 0:SEQ], ACT.Gelu, bias=b1c[0:m, l, 1, c:c + 1])\
                            .then_inc(gelu_done, 1)
                    if kind == "gate":
                        b, = of
                        act.wait_ge(ffn_added, it * FFN_EVENTS + (sec.FFNS["w2", 1, b] + 1))
                        act_fn(EG[:, 2 * b:2 * b + 2, :].rearrange("p t d -> p (t d)"),
                               XC[:, 2 * b:2 * b + 2, :].rearrange("p t d -> p (t d)"), ACT.Silu)\
                            .then_inc(gate_done, 1)
                    if kind == "x1T":
                        b, = of
                        bank, free = from_t(item)
                        act.wait_ge(xn1_kept, it * 2 + (b + 1))
                        act_fn(XN1T[:, b * SEQ:(b + 1) * SEQ], bank[:, 0:SEQ], ACT.Copy).then_inc(free, 1)

            def after_head():
                act.wait_ge(tables, 2)
                act.wait_ge(ld_a, LOADED_A)

            loop_a(act, run, after_head)
            act.drain().then_inc(a_over, 1)
            act.wait_ge(a_over, ENGINES)

            act.sem_inc(q_masked[0], 1)

            def copy_tokens(turn, b):
                act_fn(XS[:, b * SEQ:(b + 1) * SEQ], XNT1ALL[:, bass.ds(turn * TOK + b * SEQ, SEQ)], ACT.Copy)\
                    .then_inc(xs_ready, 1)

            def keep_qk(turn, b, hm, n):
                act.wait_ge(m_full.sem(n), m_full.did(hm, n))
                act.wait_ge(q_masked[b], masked(turn, 0))
                bank, ts = Mb[n % 2], slice(b * SEQ, (b + 1) * SEQ)
                act_fn(XQ[:, ts], bank[:, 0:SEQ], ACT.Copy, scale=DK1 ** -0.5).then_inc(xq_ready, 1)
                act_fn(KT1[:, ts], bank[:, SEQ:2 * SEQ], ACT.Copy).then_inc(m_free.sem(n), 1)

            def mask_head(turn, n):
                h = lane_heads(n)
                if n == 0:
                    act.wait_ge(xq_ready, turn * 2 + 1)
                act_fn(QT1[:, h, 0:SEQ], XQ[:, 0:SEQ], ACT.Identity, scale=headm[:, h:h + 1]).then_inc(q_masked[0], 1)

            def turn(sec, it, ht, hm):
                hs = S_B0 + it * (S_B_USES // 2)
                n_masked = 0
                for k in sec.steps:
                    u = sec.unit(k, TURN_LAG)
                    if u is not None:
                        keep_probs(ht, sec.T["T", u], hs, u)
                    u = sec.unit(k, 0)
                    if u is not None:
                        exponentials(hs, u)
                    if k == 1:
                        copy_tokens(it, 1)
                    if k == 15 and not sec.last:
                        copy_tokens(it + 1, 0)
                    for kind, b in b_extras(k, sec.first, sec.last):
                        if kind == "prep":
                            keep_qk(*((it + 1, 0) if b == 2 else (it, b)), hm, sec.M["qk", b])
                        if kind == "weights":
                            for part, dst, width in (("w13", W13, 2 * FE), ("w2", W2T, 2 * D)):
                                n = sec.T[part, b]
                                act.wait_ge(t_full.sem(n), t_full.did(ht, n))
                                act_fn(dst[:, it * 4 + b, :], Tb[n % 2][:, 0:width], ACT.Copy)\
                                    .then_inc(t_free.sem(n), 1)
                        if kind == "rank":
                            act.wait_ge(gap_done, 1)
                            act_fn(GW[:, 0, :], GW[:, 1, :], ACT.Exp).then_inc(gap_exp, 1)
                        if kind == "ctx":
                            n = sec.T["ctx", b]
                            act.wait_ge(t_full.sem(n), t_full.did(ht, n))
                            act_fn(CTXT[:, b % 2, :], Tb[n % 2][:, 0:SEQ], ACT.Copy).then_inc(t_free.sem(n), 1)
                    if k >= 17 and not sec.last:
                        for _ in range(2 if k < 22 else 3):
                            mask_head(it + 1, n_masked)
                            n_masked += 1
                assert n_masked == (0 if sec.last else E)

            copy_tokens(0, 0)
            keep_qk(0, 0, M_B0, 0)
            for n in range(E):
                mask_head(0, n)
            loop_b(act, turn)
            act.drain().then_inc(b_over, 1)
            act.wait_ge(b_over, ENGINES)

            def keep_tiles(t, n, ht):
                act.wait_ge(t_full.sem(n), t_full.did(ht, n))
                act_fn(XGT[:, t * P:(t + 2) * P], Tb[n % 2][:, 0:2 * P], ACT.Copy).then_inc(t_free.sem(n), 1)

            keep_tiles(0, 0, T_X0)
            keep_tiles(2, 1, T_X0)

            def turn(i, uses, ht, first, last):
                hm = M_C0 + i * (CG // 2)
                gates = dict(tiles_of(GATE_LAG, first, last))
                for j in range(CG + (OUT_LAG if last else 0)):
                    if j in gates:
                        tile = gates[j]
                        n = uses["g", tile]
                        act.wait_ge(t_full.sem(n), t_full.did(ht, n))
                        act.wait_ge(pv_done.sem(tile), pv_done.reuse(PV_C0 + i * (CG // 2), tile))
                        act_fn(GTT[:, tile % 2, :], Tb[n % 2][:, 0:FE], ACT.Copy).then_inc(t_free.sem(n), 1)
                    if j < CG:
                        act.wait_ge(m_full.sem(j), m_full.did(hm, j))
                        act.wait_ge(m_free.sem(j), m_free.reuse(hm, j))
                        act_fn(HS[:, j % 2, :], Mb[j % 2][:, 0:FE], ACT.Silu).then_inc(c_silu.sem(j), 1)
                    if j in (1, 3):
                        keep_tiles(j + 3, uses["x", j + 3], ht)
                    if j in (5, 7) and not last:
                        keep_tiles(j - 5, uses["x", j + 3], ht)

            loop_c(act, turn)
            for t in range(NT):
                act.wait_ge(moe_in, t + 1)
                act_fn(G3[:, t % GT, :], G2[:, t % GT, :], ACT.Silu).then_inc(silu_done, 1)

        @block.vector
        def _(dve):
            V = nc.vector
            for events in (m_free, s_free, o_free, ss_done, rope_done, c_stats, c_yo):
                events.begin(dve)
            steps = [0, 0]

            def settled():
                dve.sem_inc(dve_settled, 1)

            def step(instr, carry_wait=True):
                steps[1] += 1
                instr.then_inc(dstep, 1)
                dve.wait_ge(dstep, steps[0] + steps[1])
                if not carry_wait:
                    settled()

            def less_maximum(g, u, hs, n):
                b, qt, lane, slots = g["units"][u]
                dve.wait_ge(s_full.sem(n), s_full.did(hs, n))
                keys, ns = P * (qt + 1), len(slots)
                sc = Sb[n % 2][:].rearrange("p (s k) -> p s k", s=ns)
                mx = MX[:, n % 2, 0:ns]
                step(V.tensor_reduce(mx, sc, AX, ALU.max))
                dve.wait_ge(exp_done.sem(n), exp_done.reuse(hs, n))
                V.tensor_tensor(SE[:, n % 2, :].rearrange("p (s k) -> p s k", s=ns), sc,
                                mx.unsqueeze(2).broadcast_to([P, ns, keys]), ALU.subtract)\
                    .then_inc(s_free.sem(n), 1)

            def normalise(g, u, hs, m, o):
                b, qt, lane, slots = g["units"][u]
                dv, w = g["dv"], g["dv"] + 1
                dve.wait_ge(pv_done.sem(m), pv_done.did(hs, m))
                ob = Ob[o % 2][:, 0:4 * w].rearrange("p (s w) -> p s w", w=w)
                rc = RC[:, o % 2, :].unsqueeze(2)
                step(V.reciprocal(rc, ob[:, :, dv:w]))
                dst = g["o"][:, 2 * b + qt, :].rearrange("p (s j d) -> p s j d", s=4, d=dv)[:, :, lane, :]
                V.tensor_tensor(dst, ob[:, :, 0:dv], rc.broadcast_to([P, 4, dv]), ALU.mult).then_inc(o_free.sem(o), 1)

            def norm(dst, src, t):
                return V.tensor_scalar(dst, src, MV[:, t, 0:1], RS[:, t:t + 1], ALU.subtract, ALU.mult)

            V.memset(WYP[:], 0.0).then_inc(dve_consts, 1)
            V.memset(QT[DH:P, 0], 0.0)
            V.memset(QT[0:DH, 1], 0.0)
            V.memset(VA[:, :, :, DH:DH + 1], 1.0)
            V.memset(HT[64:P, :, 0:1], 0.0).then_inc(dve_consts, 1)
            dve.wait_ge(ld_first, LOADED_FIRST)
            for l in range(LAYERS):
                for k in range(2):
                    last = V.tensor_tensor(RT[:, 2 * l + k].rearrange("p x t d -> p (x t) d"),
                                    ROPE[:, k].rearrange("p x t d -> p (x t) d"),
                                    QKS[:, l, k, :].unsqueeze(1).broadcast_to([P, 4, DH]), ALU.mult)
            last.then_inc(tables, 1)
            dve.wait_ge(tables, 1)
            dve.wait_ge(ld_x, 16)
            dve.wait_ge(pool_consts, POOL_CONSTS)

            def after_head():
                dve.wait_ge(ld_a, LOADED_A)
                V.tensor_scalar(bab[0:2 * NS, 3:4], bab[0:2 * NS, 0:1], -1.0, None, ALU.mult)
                V.tensor_tensor(ybrow[:, 0, :], ybrow[:, 0, :], ybrow[:, 1, :], ALU.add).then_inc(tables, 1)
                dve.wait_ge(tables, 2)
                dve.wait_ge(ld_l1, 16 * 4)

            def run(sec, it, ahead):
                hm = it * (M_A_USES // 2)
                ht = T_A0 + it * (T_A_USES // 2)
                hs, ho = it * (S_A_USES // 2), it * (O_A_USES // 2)
                steps[:] = [0 if sec is HEAD else it * D_A_STEPS + D_HEAD_STEPS, 0]
                hq = it * (QK_EVENTS // 2)

                def m_bank(item):
                    n = sec.M[item]
                    dve.wait_ge(m_full.sem(n), m_full.did(hm, n))
                    return Mb[n % 2], m_free.sem(n)

                def scale_ready(item):
                    dve.wait_ge(rstd_done, it * STATS_EVENTS + (sec.STATS[item] + 1))

                def whole_stats(turn, b):
                    for t in (2 * b, 2 * b + 1):
                        last = V.bn_stats(ST[:, t, 0, :], XALL[:, turn * GT + t, :])
                    step(last, False)
                    for t in (2 * b, 2 * b + 1):
                        last = V.bn_aggr(MV[:, t, :], ST[:, t, 0, :])
                    last.then_inc(stats_done, 1)

                for item in sec.order["DVE"]:
                    kind, *of = item
                    if kind == "st0":
                        b, = of
                        whole_stats(it if b else ahead, b)
                    if kind == "nm0":
                        b, = of
                        scale_ready(("st0", b))
                        for t in (2 * b, 2 * b + 1):
                            last = norm(XC[:, t, :], XALL[:, (it if b else ahead) * GT + t, :], t)
                        last.then_inc(xn_ready, 1)
                    if kind == "ab":
                        dve.wait_ge(ea_done, it + 1)
                        r, n = slice(0, 2 * NS), sec.M[item]
                        step(V.tensor_scalar(AA[r], EA[r], 1.0, None, ALU.add))
                        step(V.reciprocal(AA[r], AA[r]))
                        step(V.tensor_scalar(UU[r], AA[r], -1.0, 1.0, ALU.mult, ALU.add))
                        V.scalar_tensor_tensor(UU[r], Mb[n % 2][r, SEQ:2 * SEQ], bab[r, 1:2], UU[r], ALU.add, ALU.mult)\
                            .then_inc(m_free.sem(n), 1)
                    if kind == "scan":
                        r = slice(0, 2 * NS)
                        for n in latest(sec.M["ab",], sec.M["c",]):
                            dve.wait_ge(m_free.sem(n), m_free.did(hm, n))
                        step(V.tensor_tensor_scan(SC[r], AA[r], UU[r], 0.0, ALU.mult, ALU.add))
                        V.tensor_tensor(CS[r], TC[r], SC[r], ALU.mult).then_inc(cs_done, 1)
                    if kind == "y":
                        bank, free = m_bank(item)
                        V.tensor_tensor(S0, bank[:].rearrange("p (t d) -> p t d", t=GT),
                                        ybrow[:, 0, :].unsqueeze(1).broadcast_to([P, GT, D]), ALU.add).then_inc(free, 1)
                    if kind == "qk":
                        l, n = of
                        t, i, m, u = n // 2, n % 2, sec.QK[item], sec.M[item]
                        dve.wait_ge(sq_done.sem(m), sq_done.did(hq, m))
                        V.tensor_reduce(SS[:, m % 4, :], SQ[:, m % 2, :].rearrange("p (h d) -> p h d", h=8),
                                        AX, ALU.add).then_inc(ss_done.sem(m), 1)
                        src = Mb[u % 2][:].rearrange("p (h d) -> p h d", h=8)
                        dve.wait_ge(rope_sum.sem(m), rope_sum.reuse(hq, m))
                        if sec is not HEAD:
                            four = [sec.T["qkT", *i[1:]] for i in sec.QK if sec.QK[i] == m - 4]
                            for w in four or sec.earlier("T"):
                                dve.wait_ge(t_full.sem(w), t_full.did(ht, w))
                        for x, dst in enumerate((R1[:, m % 4, :], R2[:, m % 2, :])):
                            last = V.tensor_tensor(dst.rearrange("p (h d) -> p h d", h=8), src,
                                                   RT[:, 2 * l + n % 2, x, t % 2, :].unsqueeze(1)
                                                   .broadcast_to([P, 8, DH]), ALU.mult)
                        last.then_inc(m_free.sem(u), 1)
                    if kind == "scale":
                        m = sec.QK["qk", *of]
                        dve.wait_ge(rope_sum.sem(m), rope_sum.did(hq, m))
                        r1 = R1[:, m % 4, :].rearrange("p (h d) -> p h d", h=8)
                        V.tensor_tensor(r1, r1, RN[:, m % 4, :].unsqueeze(2).broadcast_to([P, 8, DH]), ALU.mult)\
                            .then_inc(rope_done.sem(m), 1)
                    if kind == "S":
                        l, b, k = of
                        less_maximum(ATT0, unit_of(b, k), hs, sec.S[item])
                    if kind == "O":
                        l, b, k = of
                        normalise(ATT0, unit_of(b, k), hs, sec.S["S", l, b, k], sec.o_of(l, b, k))
                    if kind == "wo":
                        l, b = of
                        bank, free = m_bank(item)
                        V.tensor_tensor(XC[:, 2 * b:2 * b + 2, :], XC[:, 2 * b:2 * b + 2, :],
                                        bank[:, 0:SEQ].rearrange("p (t d) -> p t d", t=2), ALU.add).then_inc(free, 1)
                    if kind == "sh":
                        l, b = of
                        n = sec.M["wo", l, b]
                        dve.wait_ge(m_free.sem(n), m_free.did(hm, n))
                        bank, free = m_bank(item)
                        settled()
                        for t in range(2):
                            V.bn_stats(ST[:, 2 * b + t, 0, :], XC[:, 2 * b + t, 0:64])
                            last = V.bn_stats(ST[:, 2 * b + t, 1, :], bank[:, t * 64:(t + 1) * 64])
                        step(last, False)
                        for t in range(2):
                            last = V.bn_aggr(MV[:, 2 * b + t, :], ST[:, 2 * b + t].rearrange("p s c -> p (s c)"))
                        last.then_inc(stats_done, 1)
                    if kind == "nh":
                        l, b = of
                        n = sec.M["sh", l, b]
                        scale_ready(("sh", l, b))
                        for t in range(2):
                            norm(HN[:, 2 * b + t, 0:64], XC[:, 2 * b + t, 0:64], 2 * b + t)
                            last = norm(HN[:, 2 * b + t, 64:D], Mb[n % 2][:, t * 64:(t + 1) * 64], 2 * b + t)
                        last.then_inc(m_free.sem(n), 1)
                    if kind == "w1":
                        l, b, c = of
                        g, n, m = sec.GELUS[item], sec.M[item], HC[c][1]
                        dve.wait_ge(gelu_done, it * GELU_EVENTS + (g + 1))
                        V.scalar_tensor_tensor(HG[0:m, c, b * SEQ:(b + 1) * SEQ], Mb[n % 2][0:m, SEQ:2 * SEQ],
                                               b1c[0:m, l, 0, c:c + 1], GG[0:m, g % 2, :], ALU.add, ALU.mult)\
                            .then_inc(m_free.sem(n), 1)
                    if kind == "w2":
                        l, b = of
                        bank, free = m_bank(item)
                        xc, n = XC[:, 2 * b:2 * b + 2, :], sec.M[item]
                        V.tensor_tensor(xc, xc, bank[:, 0:SEQ].rearrange("p (t d) -> p t d", t=2), ALU.add)\
                            .then_inc(free, 1)
                        dve.wait_ge(m_free.sem(n), m_free.did(hm, n))
                        V.tensor_tensor(xc, xc, b2row[:, l, :].unsqueeze(1).broadcast_to([P, 2, D]), ALU.add)\
                            .then_inc(ffn_added, 1)
                    if kind == "gate":
                        b, = of
                        dve.wait_ge(gate_done, it * 2 + (b + 1))
                        eg = EG[:, 2 * b:2 * b + 2, :]
                        step(V.tensor_tensor(eg, eg, S0[:, 2 * b:2 * b + 2, :], ALU.mult))
                        xt = XALL[:, bass.ds(it * GT + 2 * b, 2), :]
                        step(V.tensor_tensor(xt, xt, eg, ALU.add), False)
                        whole_stats(it, b)
                    if kind == "nm1":
                        b, = of
                        scale_ready(("gate", b))
                        for t in (2 * b, 2 * b + 1):
                            last = norm(HN[:, t, :], XALL[:, it * GT + t, :], t)
                        last.then_inc(xn1_ready, 1)
                    if kind == "router":
                        bank, free = m_bank(item)
                        V.tensor_tensor(LG[:, bass.ds(it * GT, GT), :],
                                        bank[:, 0:GT * E].rearrange("p (t e) -> p t e", t=GT),
                                        rbrow[:].unsqueeze(1).broadcast_to([P, GT, E]), ALU.add).then_inc(free, 1)
                        n = sec.M[item]
                        dve.wait_ge(m_free.sem(n), m_free.did(hm, n))
                assert sec is not BODY or steps[1] == D_A_STEPS, steps[1]
                assert sec is not HEAD or steps[1] == D_HEAD_STEPS, steps[1]

            loop_a(dve, run, after_head)
            dve.drain().then_inc(a_over, 1)
            dve.wait_ge(a_over, ENGINES)

            steps[:] = [TURNS * D_A_STEPS, 0]
            V.memset(VA1[:, :, :, DK1:DK1 + 1], 1.0)

            def routing():
                dve.wait_ge(iotas, 3)
                V.memset(KEEP, 1.0)
                for t in range(NT):
                    last = V.max(MAXV[:, t, :], LG[:, t, :])
                step(last)
                yield
                for t in range(NT):
                    last = V.max_index(MIDX[:, t, :].bitcast(U32), MAXV[:, t, :], LG[:, t, :])
                step(last)
                yield
                V.memset(KEEP[:, :, 0:1], 0.0)
                V.tensor_tensor(GW[:, 1, :], MAXV[:, :, 1], MAXV[:, :, 0], ALU.subtract).then_inc(gap_done, 1)
                step(V.tensor_copy(MIF.rearrange("p k t -> p t k"), MIDX[:, :, 0:2].bitcast(U32)))
                yield
                for k in range(2):
                    last = V.tensor_tensor(ONEH[:, k], IOT.rearrange("p e t -> p t e"),
                                           MIF[:, k, :].unsqueeze(2).broadcast_to([P, NT, E]), ALU.is_equal)
                step(last)
                V.tensor_tensor(ONEH_B.rearrange("p (t e) -> p t e", t=NT), ONEH[:, 0], ONEH[:, 1], ALU.add)\
                    .then_inc(onehot, 1)
                yield
                for _ in range(6):
                    yield
                dve.wait_ge(gap_exp, 1)
                step(V.tensor_scalar(GW[:, 1, :], GW[:, 0, :], 1.0, None, ALU.add))
                step(V.reciprocal(WGT[:, 0, :], GW[:, 1, :]))
                V.tensor_tensor(WGT[:, 1, :], WGT[:, 0, :], GW[:, 0, :], ALU.mult)
                yield
                for k, part in enumerate(("ranks", "counts")):
                    n = B_FIRST.M[part, 0]
                    dve.wait_ge(m_full.sem(n), m_full.did(M_B0, n))
                    V.tensor_copy(CNT[:, k].rearrange("p t e -> p (t e)"), Mb[n % 2][:, 0:NT * E])\
                        .then_inc(m_free.sem(n), 1)
                for part in ("ranks", "counts"):
                    n = B_FIRST.M[part, 0]
                    dve.wait_ge(m_free.sem(n), m_free.did(M_B0, n))
                step(V.tensor_copy(CUM[:, 0], CNT[:, 1].rearrange("p t e -> p e t")))
                yield
                step(V.tensor_tensor_scan(CUM[:, 1].rearrange("p e t -> p (e t)"), KEEP.rearrange("p e t -> p (e t)"),
                                          CUM[:, 0].rearrange("p e t -> p (e t)"), 0.0, ALU.mult, ALU.add))
                yield
                step(V.tensor_tensor(CNT[:, 1], CUM[:, 1, :, NT - 1].unsqueeze(2).broadcast_to([P, E, NT]),
                                     IOTS[:], ALU.is_gt))
                yield
                step(V.tensor_reduce(NTI[:, 0, :], CNT[:, 1], AX, ALU.add))
                step(V.memset(NTI[:, 3, :], 1.0))
                step(V.tensor_tensor_scan(NTI[:, 1, :], NTI[:, 3, :], NTI[:, 0, :], 0.0, ALU.mult, ALU.add))
                step(V.tensor_tensor(NTI[:, 2, :], NTI[:, 1, :], NTI[:, 0, :], ALU.subtract))
                yield
                step(V.tensor_tensor(CUM[:, 1], CUM[:, 1], CUM[:, 0], ALU.subtract))
                step(V.tensor_tensor(CNT[:, 0], CNT[:, 0], CUM[:, 1].rearrange("p e t -> p t e"), ALU.add))
                yield
                step(V.scalar_tensor_tensor(CNT[:, 0], NTI[:, 2, :].unsqueeze(1).broadcast_to([P, NT, E]), float(P),
                                            CNT[:, 0], ALU.mult, ALU.add))
                yield
                for k in range(2):
                    step(V.tensor_tensor(ONEH[:, k], ONEH[:, k], CNT[:, 0], ALU.mult))
                    step(V.tensor_reduce(PF[:, k, :], ONEH[:, k], AX, ALU.add))
                    yield
                V.tensor_copy(POSU[:], PF).then_inc(pos_done, 1)
                yield
                step(V.tensor_tensor(ENDS, NTI[:, 1, :].unsqueeze(1).broadcast_to([P, CT, E]), IOTJ, ALU.is_le))
                step(V.tensor_reduce(EF, ENDS, AX, ALU.add))
                step(V.tensor_scalar(EF, EF, float(E - 1), None, ALU.min))
                step(V.tensor_copy(EID[:], EF))

            def keep_v(b, hm, n):
                dve.wait_ge(m_full.sem(n), m_full.did(hm, n))
                V.tensor_copy(VA1[:, 2 * b:2 * b + 2, :, 0:DK1],
                              Mb[n % 2][:, 0:SEQ].rearrange("p (t h d) -> p t h d", t=2, h=E)).then_inc(m_free.sem(n), 1)

            def turn(sec, it, ht, hm):
                hs = S_B0 + it * (S_B_USES // 2)
                if not sec.first:
                    steps[:] = [first_end[0] - D_B_STEPS + it * D_B_STEPS, 0]
                route = routing() if sec.first else iter(())
                for k in sec.steps:
                    u = sec.unit(k, O_LAG)
                    if u is not None and ATT1["units"][u % B_UNITS][3][-1] == 3:
                        normalise(ATT1, u % B_UNITS, hs, u, o_use(ATT1, u % B_UNITS) - (O_B_USES if u < 0 else 0))
                    u = sec.unit(k, 0)
                    if u is not None:
                        less_maximum(ATT1, u, hs, u)
                    for kind, b in b_extras(k, sec.first, sec.last):
                        if kind == "prep":
                            keep_v(b % 2, hm, sec.M["v", b])
                        if kind == "out":
                            n = sec.M["out", b]
                            dve.wait_ge(m_full.sem(n), m_full.did(hm, n))
                            V.tensor_tensor(S1ALL[:, bass.ds(it * GT + 2 * b, 2), :],
                                            Mb[n % 2][:, 0:SEQ].rearrange("p (t d) -> p t d", t=2),
                                            borow[:].unsqueeze(1).broadcast_to([P, 2, D]), ALU.add)\
                                .then_inc(m_free.sem(n), 1)
                    next(route, None)
                if sec.first:
                    assert next(route, "done") == "done"
                    first_end[:] = [steps[0] + steps[1]]
                else:
                    assert sec.last or steps[1] == D_B_STEPS, steps[1]

            first_end = [0]
            keep_v(0, M_B0, 1)
            loop_b(dve, turn)
            c0 = steps[0] + steps[1]
            dve.drain().then_inc(b_over, 1)
            dve.wait_ge(b_over, ENGINES)

            def turn(i, uses, ht, first, last):
                hp, hi = PV_C0 + i * (CG // 2), i * (CG // 2)

                experts = {}

                def expert_ahead(tile):
                    if tile not in experts and tile < CG and (tile >= 0 or not first):
                        experts[tile] = dve.value_load(EID[0:1, bass.ds(i * CG + tile, 1)], min_val=0, max_val=E - 1)

                expert_ahead(-OUT_LAG)
                expert_ahead(-NORM_LAG)
                steps[:] = [c0 if first else c0 - NORM_LAG + i * CG, 0]
                norms, outs = (dict(tiles_of(lag, first, last)) for lag in (NORM_LAG, OUT_LAG))
                for j in range(CG + (OUT_LAG if last else 0)):
                    if j in outs:
                        tile = outs[j]
                        p = tile // 2
                        dve.wait_ge(c_rstd.sem(tile), c_rstd.did(hi, tile))
                        dve.wait_ge(o_free.sem(tile), o_free.did(O_C0 + hi, tile))
                        dve.wait_ge(st_y.sem(p), st_y.reuse(i * (CG // 4), p) * 16)
                        V.scalar_tensor_tensor(YO[:, tile % 4, :], YN[:, tile % 2, :], RS[:, tile % 4:tile % 4 + 1],
                                               BB[:, experts[tile], :], ALU.mult, ALU.add).then_inc(c_yo.sem(tile), 1)
                    if j in norms:
                        tile = norms[j]
                        dve.wait_ge(pv_done.sem(tile), pv_done.did(hp, tile))
                        settled()
                        step(V.bn_stats(ST[:, tile % 4, 0, :], Ob[tile % 2][:, 0:D]), False)
                        V.bn_aggr(MV[:, tile % 4, :], ST[:, tile % 4, 0, :]).then_inc(c_stats.sem(tile), 1)
                        dve.wait_ge(c_stats.sem(tile), c_stats.did(hi, tile))
                        dve.wait_ge(c_yo.sem(tile), c_yo.reuse(hi, tile))
                        V.scalar_tensor_tensor(YN[:, tile % 2, :], Ob[tile % 2][:, 0:D], MV[:, tile % 4, 0:1],
                                               GB[:, experts[tile], :], ALU.subtract, ALU.mult).then_inc(o_free.sem(tile), 1)
                    if j < CG:
                        dve.wait_ge(c_silu.sem(j), c_silu.did(hi, j))
                        tile = j - GATE_LAG
                        if ("g", tile) in uses:
                            n = uses["g", tile]
                            dve.wait_ge(t_full.sem(n), t_full.did(ht, n))
                        V.tensor_tensor(GS[:, j % 2, :], HS[:, j % 2, :], Mb[j % 2][:, FE:2 * FE], ALU.mult)\
                            .then_inc(m_free.sem(j), 1)
                    expert_ahead(j + 1 - NORM_LAG)

            loop_c(dve, turn)
            steps[:] = [c0 + CT, 0]

            def output(t):
                ob = OUTB[:, t % OUT_TILES, :]
                dve.wait_ge(silu_done, t + 1)
                if t >= OUT_TILES:
                    dve.wait_ge(st_out.sem(t // 2), 16 * (t // 4))
                step(V.tensor_tensor(ob, G3[:, t % GT, :], S1ALL[:, t, :], ALU.mult))
                V.tensor_tensor(ob, ob, XALL[:, t, :], ALU.add).then_inc(out_ready, 1)

            for t in range(NT):
                dve.wait_ge(gathered[t], 16 * 2)
                step(V.tensor_scalar(G2[:, t % GT, :], YAB[:, t, 0, :], WGT[:, 0, t:t + 1], None, ALU.mult))
                V.scalar_tensor_tensor(G2[:, t % GT, :], YAB[:, t, 1, :], WGT[:, 1, t:t + 1], G2[:, t % GT, :],
                                       ALU.mult, ALU.add).then_inc(moe_in, 1)
                if t:
                    output(t - 1)
            output(NT - 1)

        @block.gpsimd
        def _(pool):
            G = nc.gpsimd
            for events in (rope_sum, c_rstd):
                events.begin(pool)
            pool.sem_inc(xn1_kept, 2)
            steps = [0, 0]

            def settled():
                pool.sem_inc(pool_settled, 1)

            def step(instr):
                steps[1] += 1
                instr.then_inc(pstep, 1)
                pool.wait_ge(pstep, steps[0] + steps[1])

            for v, c in ((ident, 0.0), (identb, 0.0), (shift, 0.0), (carry, 0.0), (trib, 1.0), (onesb, 1.0),
                         (powm, -0.5), (zeros, 0.0), (headm, 1.0), (mask0[0], 0.0), (mask1[0], 0.0), (mask0[1], 0.0),
                         (mask1[1], 0.0)):
                G.memset(v[:], c).then_inc(pool_consts, 1)
            pool.wait_ge(pool_consts, 13)
            one = dict(compare_op=ALU.not_equal, fill=1.0, channel_multiplier=1)
            for v, base in ((ident, 0), (identb, 0), (shift, 1), (carry, -(P - 1))):
                G.affine_select(out=v[:], in_=v[:], base=base, pattern=[[-1, P]], **one).then_inc(pool_consts, 1)
            G.affine_select(out=trib[:], in_=trib[:], compare_op=ALU.is_gt, fill=0.0, base=0, pattern=[[1, P]],
                            channel_multiplier=-1).then_inc(pool_consts, 1)
            G.affine_select(out=headm[:], in_=headm[:], compare_op=ALU.is_ge, fill=0.0, base=0,
                            pattern=[[-DK1, E]], channel_multiplier=1).then_inc(pool_consts, 1)
            for qt in range(2):
                keys = P * (qt + 1)
                for m in ((mask0, mask1)[qt][0], (mask0, mask1)[qt][1]):
                    G.affine_select(out=m[:], in_=m[:], compare_op=ALU.is_ge, fill=MASKED, base=qt * P,
                                    pattern=[[0, 512 // keys], [-1, keys]], channel_multiplier=1)\
                        .then_inc(pool_consts, 1)
            pool.wait_ge(pool_consts, 13 + 6 + 4)
            G.affine_select(out=headm[:], in_=headm[:], compare_op=ALU.is_ge, fill=0.0, base=DK1 - 1,
                            pattern=[[DK1, E]], channel_multiplier=-1).then_inc(pool_consts, 1)
            for qt in range(2):
                keys = P * (qt + 1)
                m = (mask0, mask1)[qt][0]
                G.affine_select(out=m[:], in_=m[:], compare_op=ALU.is_ge, fill=MASKED, base=64 - qt * P,
                                pattern=[[0, 512 // keys], [1, keys]], channel_multiplier=-1)\
                    .then_inc(pool_consts, 1)
            pool.wait_ge(pool_consts, POOL_CONSTS)

            def rstd(o, var):
                n = var.shape[1]
                step(G.tensor_scalar(o, var, EPS, None, ALU.add))
                return G.tensor_tensor(o, o, powm[:, 0:n], ALU.pow)

            def run(sec, it, ahead):
                steps[:] = [0 if sec is HEAD else it * P_A_STEPS + P_HEAD_STEPS, 0]
                ht = T_A0 + it * (T_A_USES // 2)
                hm = it * (M_A_USES // 2)
                hq = it * (QK_EVENTS // 2)
                for item in sec.order["Pool"]:
                    kind, *of = item
                    if kind in ("st0", "sh", "gate"):
                        b = of[-1]
                        pool.wait_ge(stats_done, it * STATS_EVENTS + (sec.STATS[item] + 1))
                        settled()
                        rstd(RS[:, 2 * b:2 * b + 2], MV[:, 2 * b:2 * b + 2, 1]).then_inc(rstd_done, 1)
                    if kind == "qk":
                        m, u = sec.QK[item], sec.M[item]
                        pool.wait_ge(ss_done.sem(m), ss_done.did(hq, m))
                        settled()
                        step(G.tensor_scalar(RN[:, m % 4, :], SS[:, m % 4, :], 1e-24, None, ALU.max))
                        G.tensor_tensor(RN[:, m % 4, :], RN[:, m % 4, :], powm[:, 0:8], ALU.pow)
                        pool.wait_ge(m_free.sem(u), m_free.did(hm, u))
                        r1, r2 = (r.rearrange("p (h s d) -> p h s d", h=8, s=2) for r in (R1[:, m % 4, :], R2[:, m % 2, :]))
                        G.tensor_tensor(r1, r1, r2[:, :, ::-1, :], ALU.add).then_inc(rope_sum.sem(m), 1)
                    if kind == "x1T":
                        b, = of
                        pool.wait_ge(xn1_ready, it * 2 + (b + 1))
                        G.tensor_copy(XN1ALL[:, bass.ds(it * GT + 2 * b, 2), :], HN[:, 2 * b:2 * b + 2, :])
                        n = sec.T[item]
                        pool.wait_ge(t_free.sem(n), t_free.did(ht, n))
                        G.tensor_copy(XNT1ALL[:, bass.ds(it * TOK + b * SEQ, SEQ)], XN1T[:, b * SEQ:(b + 1) * SEQ])\
                            .then_inc(xn1_kept, 1)
                assert sec is not BODY or steps[1] == P_A_STEPS, steps[1]
                assert sec is not HEAD or steps[1] == P_HEAD_STEPS, steps[1]

            loop_a(pool, run, lambda: None)
            pool.drain().then_inc(a_over, 1)
            pool.wait_ge(a_over, ENGINES)
            step_c0 = TURNS * P_A_STEPS

            G.iota(IOTI.rearrange("p (e t) -> p e t", e=E), [[1, E], [0, NT]], base=0, channel_multiplier=0)\
                .then_inc(iota_raw, 1)
            G.iota(IOTI2.rearrange("p (e t) -> p e t", e=E), [[0, E], [P, NT]], base=0, channel_multiplier=0)\
                .then_inc(iota_raw, 1)
            G.iota(IOTI3.rearrange("p (j e) -> p j e", e=E), [[1, CT], [0, E]], base=0, channel_multiplier=0)\
                .then_inc(iota_raw, 1)
            pool.wait_ge(iota_raw, 3)
            G.tensor_copy(IOT.rearrange("p e t -> p (e t)"), IOTI).then_inc(iotas, 1)
            G.tensor_copy(IOTS.rearrange("p e t -> p (e t)"), IOTI2).then_inc(iotas, 1)
            G.tensor_copy(IOTJ.rearrange("p j e -> p (j e)"), IOTI3).then_inc(iotas, 1)
            pool.sem_inc(q_masked[1], 1)

            def mask_heads(it):
                hs, n = S_B0 + it * (S_B_USES // 2), B_UNITS - 1
                pool.wait_ge(xq_ready, it * 2 + 2)
                pool.wait_ge(s_full.sem(n), s_full.did(hs - S_B_USES // 2, n))
                settled()
                for n in range(E):
                    h = lane_heads(n)
                    G.tensor_scalar(QT1[:, h, SEQ:2 * SEQ], XQ[:, SEQ:2 * SEQ], headm[:, h:h + 1], None, ALU.mult)\
                        .then_inc(q_masked[1], 1)

            mask_heads(0)
            mask_heads(1)
            pool.wait_ge(zeroed, 16 * CT // 4)
            pool.wait_ge(pos_done, 1)
            for t in range(NT):
                for k in range(2):
                    G.indirect_dma_start(XG, bass.IndirectOffsetOnAxis(POSU[:, k, t:t + 1], 0), XN1ALL[:, t, :], None)\
                        .then_inc(scattered, 16)
            with pool.Fori(2, TURNS) as it:
                mask_heads(it)
            pool.drain().then_inc(b_over, 1)
            pool.wait_ge(b_over, ENGINES)

            def turn(i, uses, ht, first, last):
                hi = i * (CG // 2)
                steps[:] = [step_c0 if first else step_c0 - NORM_LAG + i * CG, 0]
                for _, tile in tiles_of(NORM_LAG, first, last):
                    pool.wait_ge(c_stats.sem(tile), c_stats.did(hi, tile))
                    settled()
                    rstd(RS[:, tile % 4:tile % 4 + 1], MV[:, tile % 4, 1:2]).then_inc(c_rstd.sem(tile), 1)

            loop_c(pool, turn)
            for p in range(2):
                pool.wait_ge(st_y.sem(p), 16 * (CT // 4 + 1))
            for t in range(NT):
                for k in range(2):
                    G.indirect_dma_start(YAB[:, t, k, :], None, YG, bass.IndirectOffsetOnAxis(POSU[:, k, t:t + 1], 0))\
                        .then_inc(gathered[t], 16)


def rope_tables():
    import numpy as np
    n, window = SEQ, 64
    half = np.arange(0, DH, 2, dtype=np.float32)
    inv = (np.float32(1.0) / np.float32(10000.0) ** (half / np.float32(DH))).astype(np.float32)
    t = np.arange(n, dtype=np.float32)
    freqs = (t[:, None] * inv[None, :]).astype(np.float32).astype(np.float64)
    base = ((half + np.float32(0.4 * DH)) / np.float32(1.4 * DH)).astype(np.float64)
    power = (t - n // 2).astype(np.float64) / float(window // 2)
    scale = base[None, :] ** power[:, None]
    cos, sin = np.cos(freqs), np.sin(freqs)
    tab = np.zeros((2, 2, n, DH), np.float64)
    for i, s in enumerate((8.0 * scale, 1.0 / scale)):
        tab[i, 0] = np.concatenate([cos * s, cos * s], -1)
        tab[i, 1] = np.concatenate([sin * s, -sin * s], -1)
    return tab.astype(np.float32)


NAMES = [f"L0_attn_{n}" for n in ("x", "Wa", "ba", "Wb", "bb", "Wc", "bc", "Wd", "bd", "Wy", "by")] + \
        [f"L0_ffn_{n}" for n in ("wqkv", "q_scale", "k_scale", "wo", "ln_g", "ln_b", "w1", "b1", "w2", "b2")] + \
        [f"L1_attn_{n}" for n in ("Wq", "Wk", "Wv", "Wo", "bo")] + \
        [f"L1_ffn_{n}" for n in ("router_w", "router_b", "w1", "w2", "w3", "ln_g", "ln_b")]


def kernel(**inputs):
    import numpy as np
    import concourse.bacc as bacc
    from concourse.bass_utils import run_bass_kernel_spmd

    nc = bacc.Bacc("TRN2", target_bir_lowering=False, num_devices=1)
    arrays = {f"in_{n}": np.ascontiguousarray(inputs[n]) for n in NAMES}
    arrays["in_rope"] = rope_tables()
    ins = {n[3:]: nc.dram_tensor(n, a.shape, mybir.dt.from_np(a.dtype), kind="ExternalInput").ap()
           for n, a in arrays.items()}
    out = nc.dram_tensor("out", (NB, SEQ, D), F32, kind="ExternalOutput").ap()
    gated_layers(nc, ins, out)
    return run_bass_kernel_spmd(nc, [arrays], core_ids=[0]).results[0]["out"]
```
